# Optimizing a Trainium2 kernel written in Bass

```python
import numpy as np
import jax
import jax.numpy as jnp

def _softmax(x, axis=-1):
    return jax.nn.softmax(x, axis=axis)

def _gelu(x):
    return jax.nn.gelu(x, approximate=True)

def _silu(x):
    return jax.nn.silu(x)

def _sigmoid(x):
    return jax.nn.sigmoid(x)

def _layernorm(x, axis=-1, eps=1e-05):
    m = jnp.mean(x, axis=axis, keepdims=True)
    v = jnp.var(x, axis=axis, keepdims=True)
    return (x - m) / jnp.sqrt(v + eps)

def _scatter_add(tgt, idx, src, axis=0):
    return tgt.at[idx].add(src)

def _segment_sum(src, seg, n):
    return jax.ops.segment_sum(src, seg, n)
kernel_name = 'mk_xattn_ffn_d1_seqx_r4_b97ab6'

def setup_inputs(seed: int=0):
    np.random.seed(seed)
    _w = jnp.asarray

    def _rec_inputs():
        import jax
        import jax.numpy as jnp
        _rk = jax.random.key(seed)
        x = -0.0002928 + 1 * jax.random.normal(jax.random.fold_in(_rk, 1), (32, 112, 256), jnp.float32)
        _lenS = 112 - jax.random.randint(jax.random.fold_in(_rk, 7), (32,), 0, max(1, 112 // 4) + 1, jnp.int32)
        _lenS2 = 375 - jax.random.randint(jax.random.fold_in(_rk, 8), (32,), 0, max(1, 375 // 4) + 1, jnp.int32)
        _ctx_1024P = jax.random.normal(jax.random.fold_in(_rk, 11), (32, 16, 256), jnp.float32)
        _ctx_1024c = jax.random.dirichlet(jax.random.fold_in(_rk, 511), 0.3 * jnp.ones((16,), jnp.float32), (32, 375))
        _ctx_1024t = jnp.einsum('bsk,bkd->bsd', _ctx_1024c, _ctx_1024P)
        _ctx_1024t = _ctx_1024t * jax.lax.rsqrt(jnp.mean(jnp.square(_ctx_1024t)) + 1e-12) * 0.953939
        ctx_1024 = -1.39393e-06 + 0.999914 * (_ctx_1024t + 0.3 * jax.random.normal(jax.random.fold_in(_rk, 611), (32, 375, 256), jnp.float32))
        _validS = jnp.arange(112)[None, :] < _lenS[:, None]
        _validS2 = jnp.arange(375)[None, :] < _lenS2[:, None]
        _causal = jnp.tril(jnp.ones((112, 112), dtype=bool))
        mask_1x1xSxS2_ik0 = jnp.where(jnp.broadcast_to(_validS2[0:1, None, None, :], (1, 1, 112, 375)), 0, 1).astype(jnp.int32)
        return (x, ctx_1024, mask_1x1xSxS2_ik0)
    x, ctx_1024, mask_1x1xSxS2_ik0 = _rec_inputs()

    def _L0_xattn_setup():
        import jax, jax.numpy as jnp
        import numpy as np
        NEG_INF = -10000000000.0
        D_MODEL = 256
        NUM_HEADS = 16
        HEAD_DIM = D_MODEL // NUM_HEADS
        B, S = (2, 512)

        def _split_heads(x):
            b, s, _ = x.shape
            return x.reshape(b, s, NUM_HEADS, HEAD_DIM).transpose(0, 2, 1, 3)
        key = jax.random.key(seed)
        ks = jax.random.split(key, 12)
        std = 1.0 / np.sqrt(D_MODEL)
        inp = {'query': jax.random.normal(ks[0], (B, S, D_MODEL), jnp.float32), 'key': jax.random.normal(ks[1], (B, S, D_MODEL), jnp.float32), 'value': jax.random.normal(ks[2], (B, S, D_MODEL), jnp.float32), 'mask': jnp.tril(jnp.ones((S, S), jnp.int32))[None, None, :, :], 'Wq': jax.random.normal(ks[3], (D_MODEL, D_MODEL), jnp.float32) * std, 'bq': jax.random.normal(ks[4], (D_MODEL,), jnp.float32) * std, 'Wk': jax.random.normal(ks[5], (D_MODEL, D_MODEL), jnp.float32) * std, 'bk': jax.random.normal(ks[6], (D_MODEL,), jnp.float32) * std, 'Wv': jax.random.normal(ks[7], (D_MODEL, D_MODEL), jnp.float32) * std, 'bv': jax.random.normal(ks[8], (D_MODEL,), jnp.float32) * std, 'Wo': jax.random.normal(ks[9], (D_MODEL, D_MODEL), jnp.float32) * std, 'bo': jax.random.normal(ks[10], (D_MODEL,), jnp.float32) * std}
        return inp
    _L0_xattn_all = _L0_xattn_setup()
    _L0_xattn_in = {k: v for k, v in _L0_xattn_all.items() if k in ('Wq', 'bq', 'Wk', 'bk', 'Wv', 'bv', 'Wo', 'bo')}
    del _L0_xattn_all

    def _L0_ffn_setup():
        import jax, jax.numpy as jnp
        import numpy as np
        B, S, H = (8, 256, 256)
        FF = 1024
        E = 8
        TOP_K = 2
        LN_EPS = 1e-12

        def _layernorm(x, w, b):
            mu = jnp.mean(x, axis=-1, keepdims=True)
            var = jnp.mean(jnp.square(x - mu), axis=-1, keepdims=True)
            return (x - mu) * jax.lax.rsqrt(var + LN_EPS) * w + b
        key = jax.random.key(seed)
        ks = jax.random.split(key, 8)
        sc_h = 1.0 / np.sqrt(H)
        sc_ff = 1.0 / np.sqrt(FF)
        return {'hidden_states': jax.random.normal(ks[0], (B, S, H), jnp.float32), 'router_w': jax.random.normal(ks[1], (E, H), jnp.float32) * sc_h, 'router_b': jnp.zeros((E,), jnp.float32), 'w1': jax.random.normal(ks[2], (E, FF, H), jnp.float32) * sc_h, 'b1': jax.random.normal(ks[3], (E, FF), jnp.float32) * 0.01, 'w2': jax.random.normal(ks[4], (E, H, FF), jnp.float32) * sc_ff, 'b2': jax.random.normal(ks[5], (E, H), jnp.float32) * 0.01, 'ln_w': jnp.ones((H,), jnp.float32), 'ln_b': jnp.zeros((H,), jnp.float32)}
    _L0_ffn_all = _L0_ffn_setup()
    _L0_ffn_in = {k: v for k, v in _L0_ffn_all.items() if k in ('router_w', 'router_b', 'w1', 'b1', 'w2', 'b2', 'ln_w', 'ln_b')}
    del _L0_ffn_all
    return {'x': x, 'ctx_1024': ctx_1024, 'mask_1x1xSxS2_ik0': mask_1x1xSxS2_ik0, 'L0_xattn_Wq': _L0_xattn_in['Wq'], 'L0_xattn_bq': _L0_xattn_in['bq'], 'L0_xattn_Wk': _L0_xattn_in['Wk'], 'L0_xattn_bk': _L0_xattn_in['bk'], 'L0_xattn_Wv': _L0_xattn_in['Wv'], 'L0_xattn_bv': _L0_xattn_in['bv'], 'L0_xattn_Wo': _L0_xattn_in['Wo'], 'L0_xattn_bo': _L0_xattn_in['bo'], 'L0_ffn_router_w': _L0_ffn_in['router_w'], 'L0_ffn_router_b': _L0_ffn_in['router_b'], 'L0_ffn_w1': _L0_ffn_in['w1'], 'L0_ffn_b1': _L0_ffn_in['b1'], 'L0_ffn_w2': _L0_ffn_in['w2'], 'L0_ffn_b2': _L0_ffn_in['b2'], 'L0_ffn_ln_w': _L0_ffn_in['ln_w'], 'L0_ffn_ln_b': _L0_ffn_in['ln_b']}

def reference(x, ctx_1024, mask_1x1xSxS2_ik0, L0_xattn_Wq, L0_xattn_bq, L0_xattn_Wk, L0_xattn_bk, L0_xattn_Wv, L0_xattn_bv, L0_xattn_Wo, L0_xattn_bo, L0_ffn_router_w, L0_ffn_router_b, L0_ffn_w1, L0_ffn_b1, L0_ffn_w2, L0_ffn_b2, L0_ffn_ln_w, L0_ffn_ln_b):
    import jax
    import jax.numpy as jnp

    def _L0_xattn_ref(query, key, value, mask, Wq, bq, Wk, bk, Wv, bv, Wo, bo):
        import jax, jax.numpy as jnp
        import numpy as np
        NEG_INF = -10000000000.0
        D_MODEL = 256
        NUM_HEADS = 16
        HEAD_DIM = D_MODEL // NUM_HEADS
        B, S = (2, 512)

        def _split_heads(x):
            b, s, _ = x.shape
            return x.reshape(b, s, NUM_HEADS, HEAD_DIM).transpose(0, 2, 1, 3)
        q = _split_heads(query @ Wq.T + bq)
        k = _split_heads(key @ Wk.T + bk)
        v = _split_heads(value @ Wv.T + bv)
        scale = 1.0 / jnp.sqrt(jnp.float32(HEAD_DIM))
        scores = jnp.einsum('bhqd,bhkd->bhqk', q, k) * scale
        scores = jnp.where(mask == 0, NEG_INF, scores)
        probs = jax.nn.softmax(scores, axis=-1)
        out = jnp.einsum('bhqk,bhkd->bhqd', probs, v)
        out = out.transpose(0, 2, 1, 3).reshape(query.shape[0], -1, D_MODEL)
        return out @ Wo.T + bo

    def _L0_ffn_ref(hidden_states, router_w, router_b, w1, b1, w2, b2, ln_w, ln_b):
        import jax, jax.numpy as jnp
        import numpy as np
        B, S, H = (8, 256, 256)
        FF = 1024
        E = 8
        TOP_K = 2
        LN_EPS = 1e-12

        def _layernorm(x, w, b):
            mu = jnp.mean(x, axis=-1, keepdims=True)
            var = jnp.mean(jnp.square(x - mu), axis=-1, keepdims=True)
            return (x - mu) * jax.lax.rsqrt(var + LN_EPS) * w + b
        b, s, h = hidden_states.shape
        flat = hidden_states.reshape(-1, h)
        logits = flat @ router_w.T + router_b
        topk_vals, topk_idx = jax.lax.top_k(logits, TOP_K)
        topk_w = jax.nn.softmax(topk_vals, axis=-1)
        out = jnp.zeros_like(flat)
        n_exp = w1.shape[0]
        for e in range(n_exp):
            cw = jnp.sum(jnp.where(topk_idx == e, topk_w, 0.0), axis=-1)
            y = jax.nn.gelu(flat @ w1[e].T + b1[e], approximate=False)
            y = y @ w2[e].T + b2[e]
            out = out + y * cw[:, None]
        out = out.reshape(b, s, h) + hidden_states
        return _layernorm(out, ln_w, ln_b)
    x = x + _L0_xattn_ref(_layernorm(x, axis=-1), ctx_1024, ctx_1024, mask_1x1xSxS2_ik0, L0_xattn_Wq, L0_xattn_bq, L0_xattn_Wk, L0_xattn_bk, L0_xattn_Wv, L0_xattn_bv, L0_xattn_Wo, L0_xattn_bo)
    x = x + _L0_ffn_ref(_layernorm(x, axis=-1), L0_ffn_router_w, L0_ffn_router_b, L0_ffn_w1, L0_ffn_b1, L0_ffn_w2, L0_ffn_b2, L0_ffn_ln_w, L0_ffn_ln_b)
    return x

_drawn_inputs = setup_inputs


def setup_inputs(seed=0):
    import zlib

    import numpy as np

    out = dict(_drawn_inputs(seed))
    spreads = {'L0_ffn_router_b': (0.0, 0.1), 'L0_ffn_ln_w': (1.0, 0.2), 'L0_ffn_ln_b': (0.0, 0.1)}
    factors = {'L0_xattn_bk': 64.0, 'L0_ffn_b1': 26.068, 'L0_ffn_b2': 8.0}
    for name, (base, spread) in spreads.items():
        noise = np.random.default_rng([zlib.crc32(name.encode()), seed]).standard_normal(out[name].shape)
        drawn = base * np.exp(spread * noise) if base else spread * noise
        out[name] = jnp.asarray(drawn.astype(out[name].dtype))
    for name, factor in factors.items():
        out[name] = (out[name] * factor).astype(out[name].dtype)
    return out
```

```python
from contextlib import ExitStack

import concourse.bass as bass
from concourse import mybir

F32 = mybir.dt.float32
F16 = mybir.dt.float16
BF16 = mybir.dt.bfloat16
I32 = mybir.dt.int32
U32 = mybir.dt.uint32
ALU = mybir.AluOpType
ACT = mybir.ActivationFunctionType
AX = mybir.AxisListType

P = 128
B, S, T, D = 32, 112, 375, 256
H, DH = 16, 16
HALVES = D // P
CH = 3
KC = T // CH
PAIRS = H // 2
GROUPS = 4
HG = H // GROUPS
DV = DH + 1
SLOTS = GROUPS * CH
WS = 16.0
SCORE_SCALE = 1.0 / (WS * WS * DH ** 0.5)
MASKED = -float(2 ** 33)
LN1_EPS = 1e-5
E, F = 8, 1024
FC = F // P


def split_steps(eng, step):
    def edge(i):
        step(i, i % 2, i + 1 < B, 0 <= i < B, 1 <= i <= B, i >= 2, i + 2 < B, i + 3 < B)
    for i in (-1, 0, 1, 2):
        edge(i)
    pairs = (B - 3 - 3) // 2
    with eng.Fori(0, pairs) as j:
        for u in range(2):
            step(j * 2 + (3 + u), 1 - u, True, True, True, True, True, True)
    for i in range(3 + 2 * pairs, B + 2):
        edge(i)


def reached(eng, sem, count):
    if not isinstance(count, int) or count > 0:
        eng.wait_ge(sem, count)


def row_stats(nc, eng, tick, stats, mean, var, tmp):
    even, odd = stats[:, :, 1:2], stats[:, :, 4:5]
    tick(nc.vector.tensor_tensor(mean, even, odd, ALU.add))
    tick(nc.vector.tensor_tensor(tmp, even, odd, ALU.subtract))
    tick(nc.vector.tensor_tensor(var, stats[:, :, 2:3], stats[:, :, 5:6], ALU.add))
    tick(nc.vector.tensor_tensor(tmp, tmp, tmp, ALU.mult))
    tick(nc.vector.tensor_scalar(mean, mean, 0.5, None, ALU.mult))
    tick(nc.vector.tensor_scalar(var, var, 1.0 / D, None, ALU.mult))
    tick(nc.vector.scalar_tensor_tensor(var, tmp, 0.25, var, ALU.mult, ALU.add))


def attention_block(nc, sems, ctx, t, out_x, x2, slots):
    sb = lambda name, shape, dt: ctx.enter_context(nc.sbuf_tensor(name, shape, dt))
    ps = lambda name, shape, dt: ctx.enter_context(nc.psum_tensor(name, shape, dt))
    sem = sems.new
    X, stats2 = out_x

    per_row = slots.shape[0] * slots.shape[1] // B // 70
    slot_shares = slots.rearrange("r n -> (r n)").rearrange("(b p n) -> b p n", b=B, n=per_row)
    zeros = sb("zeros", [70, per_row], F16)
    ident = sb("ident", [P, P], F32)
    sel = sb("sel", [KC + 1, P], BF16)
    self32 = sb("self32", [KC + 1, P], F32)
    parity = sb("parity", [P, 2], F32)
    ones = sb("ones", [S, P], F32)
    w32 = sb("w32", [P, 3, HALVES, D], F32)
    wh = sb("wh", [P, 3, HALVES, D], F16)
    wl = sb("wl", [P, 3, HALVES, D], F16)
    wo = sb("wo", [P, HALVES, D], F32)
    bqk = sb("bqk", [P, 2, HALVES], F32)
    bqk16 = sb("bqk16", [P, 2, HALVES], F32)
    bq_par = sb("bq_par", [P, HALVES, 2], F32)
    bv = sb("bv", [P, HALVES], F32)
    bo_row = sb("bo_row", [1, D], F32)
    bo_all = sb("bo_all", [S, D], F32)
    mask_q = sb("mask_q", [S, T], I32)
    mask_k = sb("mask_k", [KC, CH, S], I32)
    mask_add = sb("mask_add", [S, T], F32)
    n_masked = sb("n_masked", [S, 1], F32)
    keep_q = sb("keep_q", [S, 1], F32)
    keep_diag = sb("keep_diag", [S, S], F32)
    keep = sb("keep", [P, S], F32)
    keep4 = sb("keep4", [P, HALVES, 2, S], F32)
    mk32 = sb("mk32", [KC, CH, S], F32)
    stats1 = sb("stats1", [S, B, 6], F32)
    mean1 = sb("mean1", [S, B, 1], F32)
    rstd1 = sb("rstd1", [S, B, 1], F32)
    shift1 = sb("shift1", [S, B, 1], F32)
    tmp1 = sb("tmp1", [S, B, 1], F32)
    ct = sb("ct", [P, 2, HALVES * T], F32)
    cth = sb("cth", [P, 2, HALVES, T], F16)
    ctl = sb("ctl", [P, 2, HALVES, T], F16)
    xn = sb("xn", [S, 2, D], F32)
    xth = sb("xth", [P, HALVES, S], F16)
    xtl = sb("xtl", [P, HALVES, S], F16)
    qf = sb("qf", [P, HALVES, 2, S], F32)
    qm = sb("qm", [P, HALVES, 2, S], F32)
    qh = sb("qh", [P, 2, HALVES, 2 * S], F16)
    ql = sb("ql", [P, 2, HALVES, 2 * S], F16)
    kh = sb("kh", [P, 2, HALVES, T], F16)
    kl = sb("kl", [P, 2, HALVES, T], F16)
    ROW = T + 2 * S
    stack = sb("stack", [96, 2, PAIRS, ROW], F16)
    vt = sb("vt", [KC, 2, CH, H, DV], F32)
    top = sb("top", [S, 2, H], F32)
    neg_top = sb("neg_top", [H, S], BF16)
    mb = sb("mb", [KC + 1, 2, CH, H * S], BF16)
    pt = sb("pt", [KC, 4, HG * S], F32)
    ots = sb("ots", [P, GROUPS * S], F32)
    rsum = sb("rsum", [S, H, 1], F32)
    at = sb("at", [S, H, DH], F32)
    att = sb("att", [P, HALVES, S], F32)
    xb = sb("xb", [S, D], F32)

    sa = [ps(f"sa{k}", [P, 512], F32) for k in range(2)]
    sbk = [ps(f"sb{k}", [P, 512], F32) for k in range(3)]
    ot = ps("ot", [P, 512], F32)
    pj = [ps(f"pj{k}", [P, 512], F32) for k in range(2)]
    JOBS = ["xT", "OT", "Q", "K0", "K1", "AT", "V01", "V2", "MT", "WO"]
    bank = {job: pj[n % 2] for n, job in enumerate(JOBS)}
    JOB_AT = {"xT": 0, "OT": 1, "Q": 2, "K0": 3, "K1": 4, "AT": 5, "V01": 6, "V2": 7, "MT": 9, "WO": 10}

    loaded = {n: sem("ld_" + n) for n in ("x", "w", "small", "wo")}
    prep = sem("prep")
    root = sem("root")
    diag = sem("diag")
    ready = sem("ready")
    prep_pe = sem("prep_pe")
    prep_act = sem("prep_act")
    ct_in = [sem(f"ct_in{k}") for k in range(2)]
    ct_hi, ct_lo = sem("ct_hi"), sem("ct_lo")
    xn_made = sem("xn_made")
    done = {job: sem("pe_" + job) for job in JOBS}
    xt_hi, xt_lo = sem("xt_hi"), sem("xt_lo")
    q_biased, q_kept, q_hi, q_lo = sem("q_biased"), sem("q_kept"), sem("q_hi"), sem("q_lo")
    k_hi = [sem(f"k_hi{k}") for k in range(2)]
    k_lo = [sem(f"k_lo{k}") for k in range(2)]
    v_out = [sem("v_out01"), sem("v_out2")]
    spilled = [sem(f"spilled{u}") for u in range(2)]
    stacked = [[sem(f"stacked{k}{u}") for u in range(2)] for k in range(HALVES)]
    a_scored = [sem(f"a_scored{k}") for k in range(H)]
    a_top = [sem(f"a_top{k}") for k in range(H)]
    top_out = sem("top_out")
    top_in = sem("top_in")
    b_scored = [sem(f"b_scored{k}") for k in range(SLOTS)]
    b_exp = [sem(f"b_exp{k}") for k in range(SLOTS)]
    b_pv = [sem(f"b_pv{k}") for k in range(SLOTS)]
    ot_out = sem("ot_out")
    zeroed, x2_stored = sem("zeroed"), sem("x2_stored")
    rs_out, at_out, att_out, xb_out, x2_out, st_out = (sem(n) for n in (
        "rs_out", "at_out", "att_out", "xb_out", "x2_out", "st_out"))

    spill = nc.dram_tensor("spill", (2, 3, P, HALVES, ROW), F16, kind="Internal").ap()
    spill_read = [[[spill[u, r].rearrange("(q p) h n -> h p q n", p=32)[k] for k in range(HALVES)]
                   for r in range(3)] for u in range(2)]

    def in_stack(b, u):
        return (b - u) * 24 + 48

    def in_spill(b, u):
        return (b - u) * 48 + 96

    block = ctx.enter_context(nc.Block())

    @block.sync
    def _(sp):
        sp.dma_start(X[0:S, :, :], t["x"].rearrange("b s d -> s b d")).then_inc(loaded["x"], 16)
        sp.dma_start(w32[:], t["wqkv"]).then_inc(loaded["w"], 16)
        for dst, src in ((ident[:], t["ident"]), (self32[:], t["sel"]), (parity[:], t["parity"]),
                         (bqk[:], t["bqk"]), (bv[:], t["bv"]), (bo_row[:], t["bo"]),
                         (mask_q[:], t["mask_q"]), (mask_k[:], t["mask_k"])):
            sp.dma_start(dst, src).then_inc(loaded["small"], 16)
        sp.dma_start(wo[:], t["wo"]).then_inc(loaded["wo"], 16)
        for b in range(2):
            sp.dma_start(ct[:, b, :], t["ctxT"][b]).then_inc(ct_in[b], 16)

        def step(i, u, project, find, attend, output, split_next, load_next):
            if load_next:
                reached(sp, ct_hi, i + 2)
                reached(sp, ct_lo, i + 2)
                sp.wait_ge(loaded["x"], 16)
                sp.dma_start(ct[:, 1 - u, :], t["ctxT"][i + 3]).then_inc(ct_in[1 - u], 16)
            if project:
                w = 1 - u
                if not isinstance(i, int) or i >= 1:
                    for k in range(HALVES):
                        sp.wait_ge(stacked[k][w], in_stack(i - 1, w))
                sp.wait_ge(q_hi, i + 2)
                for r in (0, 1):
                    sp.dma_start(spill[w, r, :, :, T:ROW], qh[:, w]).then_inc(spilled[w], 16)
                sp.wait_ge(q_lo, i + 2)
                sp.dma_start(spill[w, 2, :, :, T:ROW], ql[:, w]).then_inc(spilled[w], 16)
                for k in range(HALVES):
                    sp.wait_ge(k_hi[k], i + 2)
                for r in (0, 2):
                    sp.dma_start(spill[w, r, :, :, 0:T], kh[:, w]).then_inc(spilled[w], 16)
                if attend:
                    sp.wait_ge(b_scored[SLOTS // 2 - 1], i)
                for k in range(HALVES):
                    sp.wait_ge(k_lo[k], i + 2)
                sp.dma_start(spill[w, 1, :, :, 0:T], kl[:, w]).then_inc(spilled[w], 16)
                sp.wait_ge(spilled[w], in_spill(i + 1, w))
                for k in range(HALVES):
                    if attend and k == 1:
                        sp.wait_ge(b_scored[SLOTS - 1], i)
                    for r in range(3):
                        sp.dma_start(stack[32 * r:32 * r + 32, w, PAIRS // 2 * k:PAIRS // 2 * (k + 1), :],
                                     spill_read[w][r][k]).then_inc(stacked[k][w], 16)

            if find:
                sp.dma_start(slot_shares[i], zeros[:]).then_inc(zeroed, 16)
            if output:
                sp.wait_ge(loaded["x"], 16)
                sp.wait_ge(x2_out, i - 1)
                sp.dma_start(x2[i - 2], X[0:S, i - 2, :]).then_inc(x2_stored, 16)

        sp.wait_ge(prep_act, 3)
        split_steps(sp, step)
        sp.wait_ge(zeroed, 16 * B)
        sp.wait_ge(x2_stored, 16 * B)

    @block.gpsimd
    def _(pool):
        nc.gpsimd.memset(vt[:], 1.0).then_inc(prep_act, 1)
        nc.gpsimd.memset(ones[:], 1.0).then_inc(prep_act, 1)
        nc.gpsimd.memset(zeros[:], 0.0).then_inc(prep_act, 1)
        pool.wait_ge(ready, 1)

        def split_context(b, u):
            pool.wait_ge(ct_hi, b + 1)
            if not isinstance(b, int) or b >= 2:
                pool.wait_ge(done["V2"], b - 1)
            nc.gpsimd.tensor_tensor(ctl[:, u, :, :].rearrange("p a t -> p (a t)"), ct[:, u, :],
                                    cth[:, u, :, :].rearrange("p a t -> p (a t)"), ALU.subtract).then_inc(ct_lo, 1)

        split_context(0, 0)

        def step(i, u, project, find, attend, output, split_next, load_next):
            if output:
                if not isinstance(i, int) or i >= 3:
                    pool.wait_ge(x2_out, i - 2)
                nc.gpsimd.tensor_tensor(xb[:], X[0:S, i - 2, :], bo_all[:], ALU.add).then_inc(xb_out, 1)
            if project:
                w = 1 - u
                pool.wait_ge(q_biased, i + 2)
                reached(pool, q_lo, i + 1)
                f, fn = "p a r s -> p (a r s)", "p a n -> p (a n)"
                nc.gpsimd.tensor_tensor(qm[:].rearrange(f), qf[:].rearrange(f), keep4[:].rearrange(f),
                                        ALU.mult).then_inc(q_kept, 1)
                if not isinstance(i, int) or i >= 1:
                    pool.wait_ge(spilled[w], in_spill(i - 1, w))
                nc.gpsimd.tensor_tensor(qh[:, w].rearrange(fn), qf[:].rearrange(f), keep4[:].rearrange(f),
                                        ALU.mult).then_inc(q_hi, 1)
                pool.wait_ge(q_kept, i + 2)
                pool.wait_ge(q_hi, i + 2)
                nc.gpsimd.tensor_tensor(ql[:, w].rearrange(fn), qm[:].rearrange(f), qh[:, w].rearrange(fn),
                                        ALU.subtract).then_inc(q_lo, 1)
            if isinstance(i, int) and i == -1:
                split_context(1, 1)
            if split_next:
                if not isinstance(i, int) or i >= 0:
                    split_context(i + 2, u)

        split_steps(pool, step)

    @block.scalar
    def _(act):
        act.wait_ge(root, 1)
        nc.scalar.sqrt(rstd1[:], rstd1[:]).then_inc(root, 1)
        act.wait_ge(ready, 1)

        def split_context(b, u):
            act.wait_ge(ct_in[u], (b // 2 + 1) * 16 if isinstance(b, int) else (b - u) * 8 + 16)
            if not isinstance(b, int) or b >= 2:
                act.wait_ge(done["V2"], b - 1)
            nc.scalar.copy(cth[:, u, :, :].rearrange("p a t -> p (a t)"), ct[:, u, :]).then_inc(ct_hi, 1)

        split_context(0, 0)

        def step(i, u, project, find, attend, output, split_next, load_next):
            w = 1 - u
            for n in range(SLOTS + 1):
                if attend and n < SLOTS:
                    act.wait_ge(b_scored[n], i)
                    if n >= 4:
                        act.wait_ge(b_pv[n - 4], i)
                    elif not isinstance(i, int) or i >= 2:
                        act.wait_ge(b_pv[n + SLOTS - 4], i - 1)
                    nc.scalar.activation(pt[:, n % 4, :], sbk[n % 3][0:KC, 0:HG * S], ACT.Exp,
                                         scale=SCORE_SCALE).then_inc(b_exp[n], 1)
                if n == 0 and project:
                    act.wait_ge(done["xT"], i + 2)
                    reached(act, done["Q"], i + 1)
                    nc.scalar.copy(xth[:].rearrange("p a s -> p (a s)"),
                                   bank["xT"][:, 0:HALVES * S]).then_inc(xt_hi, 1)
                if n in (3, 4) and project:
                    half = n - 3
                    act.wait_ge(done[f"K{half}"], i + 2)
                    if not isinstance(i, int) or i >= 1:
                        act.wait_ge(spilled[w], in_spill(i - 1, w))
                    nc.scalar.activation(kh[:, w, half, :], bank[f"K{half}"][:, 0:T], ACT.Identity,
                                         bias=bqk16[:, 1, half:half + 1]).then_inc(k_hi[half], 1)
                if n == 5 and output:
                    act.wait_ge(done["AT"], i - 1)
                    if not isinstance(i, int) or i >= 3:
                        act.wait_ge(done["WO"], i - 2)
                    nc.scalar.copy(att[:].rearrange("p a s -> p (a s)"),
                                   bank["AT"][:, 0:HALVES * S]).then_inc(att_out, 1)
                if n == 7 and find:
                    act.wait_ge(done["V01"], i + 1)
                    if not isinstance(i, int) or i >= 2:
                        act.wait_ge(b_pv[SLOTS - 1], i - 1)
                    nc.scalar.activation(vt[:, u, 0:2, :, 0:DH],
                                         bank["V01"][0:KC, :].rearrange("p (c h d) -> p c h d", c=2, h=H),
                                         ACT.Copy, scale=1.0 / WS).then_inc(v_out[0], 1)
                if n == 8 and find:
                    act.wait_ge(done["V2"], i + 1)
                    nc.scalar.activation(vt[:, u, 2, :, 0:DH],
                                         bank["V2"][0:KC, 0:D].rearrange("p (h d) -> p h d", h=H),
                                         ACT.Copy, scale=1.0 / WS).then_inc(v_out[1], 1)
                if n == 9 and find:
                    act.wait_ge(done["MT"], i + 1)
                    reached(act, top_in, i * 48)
                    nc.scalar.mul(neg_top[:], bank["MT"][0:H, 0:S], -1.0).then_inc(top_out, 1)
                    act.wait_ge(top_out, i + 1)
                    if not isinstance(i, int) or i >= 2:
                        act.wait_ge(b_scored[SLOTS - 1], i - 1)
                    for c in range(CH):
                        act.dma_start(mb[KC:KC + 1, u, c, :].rearrange("o (h s) -> o h s", h=H),
                                      neg_top[:]).then_inc(top_in, 16)
                if n == 10 and isinstance(i, int) and i == -1:
                    split_context(1, 1)
                if n == 10 and split_next and (not isinstance(i, int) or i >= 0):
                    split_context(i + 2, u)
                if n == SLOTS and attend:
                    act.wait_ge(b_pv[SLOTS - 1], i)
                    reached(act, done["OT"], i - 1)
                    nc.scalar.copy(ots[:], ot[:, 0:GROUPS * S]).then_inc(ot_out, 1)

        split_steps(act, step)

    @block.vector
    def _(dve):
        count = [0]

        def tick(instruction):
            count[0] += 1
            instruction.then_inc(prep, 1)
            dve.wait_ge(prep, count[0])

        V = nc.vector
        dve.wait_ge(loaded["w"], 16)
        tick(V.tensor_scalar(wh[:], w32[:], WS, None, ALU.mult))
        tick(V.scalar_tensor_tensor(wl[:].rearrange("p w a d -> p (w a d)"), w32[:].rearrange("p w a d -> p (w a d)"),
                                    WS, wh[:].rearrange("p w a d -> p (w a d)"), ALU.mult, ALU.subtract))
        dve.wait_ge(loaded["small"], 16 * 8)
        tick(V.tensor_scalar(bqk16[:], bqk[:], WS, None, ALU.mult))
        for half in range(HALVES):
            tick(V.tensor_scalar(bq_par[:, half, :], parity[:], bqk16[:, 0, half:half + 1], None, ALU.mult))
        tick(V.tensor_copy(sel[:], self32[:]))
        tick(V.tensor_scalar(mask_add[:], mask_q[:], 0.0, None, ALU.is_equal))
        tick(V.reduce_sum(n_masked[:], mask_add[:], AX.X))
        tick(V.tensor_scalar(keep_q[:], n_masked[:], float(T), None, ALU.is_lt))
        tick(V.tensor_scalar(mask_add[:], mask_add[:], keep_q[:], MASKED, ALU.mult, ALU.mult))
        V.tensor_scalar(keep_diag[:], ident[0:S, 0:S], keep_q[:], None, ALU.mult).then_inc(diag, 1)
        dve.wait_ge(prep_pe, 1)
        tick(V.tensor_copy(keep[:], pj[0][:, 0:S]))
        tick(V.tensor_copy(keep4[:].rearrange("p a r s -> p (a r) s"), keep[:].unsqueeze(1).to_broadcast([P, 4, S])))
        tick(V.tensor_scalar(mk32[:], mask_k[:], 0.0, MASKED, ALU.is_equal, ALU.mult))
        tick(V.tensor_tensor(mk32[:], mk32[:], keep[0:KC, :].unsqueeze(1).to_broadcast([KC, CH, S]), ALU.mult))
        for c in range(CH):
            tick(V.tensor_copy(mb[0:KC, 0, c, :].rearrange("p (h s) -> p h s", h=H),
                               mk32[:, c, :].unsqueeze(1).to_broadcast([KC, H, S])))
        tick(V.tensor_copy(mb[0:KC, 1, :, :], mb[0:KC, 0, :, :]))
        dve.wait_ge(prep_pe, 2)
        tick(V.tensor_copy(bo_all[:], pj[1][0:S, 0:D]))
        dve.wait_ge(loaded["x"], 16)
        for b in range(B):
            last = V.bn_stats(stats1[:, b, :], X[0:S, b, :])
        tick(last)
        row_stats(nc, dve, tick, stats1, mean1[:], rstd1[:], tmp1[:])
        tick(V.tensor_scalar(rstd1[:], rstd1[:], LN1_EPS, None, ALU.add))
        V.tensor_copy(tmp1[:], rstd1[:]).then_inc(root, 1)
        dve.wait_ge(root, 2)
        tick(V.reciprocal(rstd1[:], rstd1[:]))
        tick(V.tensor_tensor(shift1[:], rstd1[:], rstd1[:], ALU.mult))
        tick(V.tensor_tensor(shift1[:], shift1[:], tmp1[:], ALU.mult))
        tick(V.tensor_scalar(shift1[:], shift1[:], -0.5, 1.5, ALU.mult, ALU.add))
        tick(V.tensor_tensor(rstd1[:], rstd1[:], shift1[:], ALU.mult))
        tick(V.scalar_tensor_tensor(shift1[:], mean1[:], -1.0, rstd1[:], ALU.mult, ALU.mult))

        def normalise(b, u):
            if not isinstance(b, int) or b >= 2:
                dve.wait_ge(done["xT"], b - 1)
            V.tensor_scalar(xn[:, u, :], X[0:S, b, :], rstd1[:, b, :], shift1[:, b, :],
                            ALU.mult, ALU.add).then_inc(xn_made, 1)

        normalise(0, 0)
        dve.wait_ge(prep_act, 3)
        V.memset(ot[:], 0.0).then_inc(ready, 1)

        def step(i, u, project, find, attend, output, split_next, load_next):
            w = 1 - u
            if find:
                if not isinstance(i, int) or i >= 2:
                    dve.wait_ge(done["MT"], i - 1)
                dve.wait_ge(a_scored[0], i + 1)
            for n in range(SLOTS):
                if n == 0 and project:
                    dve.wait_ge(done["xT"], i + 2)
                    dve.wait_ge(xt_hi, i + 2)
                    V.tensor_tensor(xtl[:].rearrange("p a s -> p (a s)"), bank["xT"][:, 0:HALVES * S],
                                    xth[:].rearrange("p a s -> p (a s)"), ALU.subtract).then_inc(xt_lo, 1)
                if n < 8 and find:
                    for h in (2 * n, 2 * n + 1):
                        dve.wait_ge(root, 2)
                        dve.wait_ge(a_scored[h], i + 1)
                        V.tensor_tensor_reduce(sa[h % 2][0:S, 0:T], sa[h % 2][0:S, 0:T], mask_add[:], 1.0, -3.0e38,
                                               ALU.add, ALU.max, top[:, u, h:h + 1]).then_inc(a_top[h], 1)
                if n == 1 and output:
                    dve.wait_ge(done["OT"], i - 1)
                    o = bank["OT"][0:S, :].rearrange("p (h d) -> p h d", h=H)
                    V.reciprocal(rsum[:], o[:, :, DH:DV]).then_inc(rs_out, 1)
                    dve.wait_ge(rs_out, i - 1)
                    V.tensor_tensor(at[:], o[:, :, 0:DH], rsum[:].to_broadcast([S, H, DH]),
                                    ALU.mult).then_inc(at_out, 1)
                if n == 2 and project:
                    dve.wait_ge(done["Q"], i + 2)
                    reached(dve, q_hi, i + 1)
                    for half in range(HALVES):
                        for r in range(2):
                            last = V.tensor_scalar(qf[:, half, r, :], bank["Q"][:, half * S:(half + 1) * S],
                                                   parity[:, r:r + 1], bq_par[:, half, r:r + 1], ALU.mult, ALU.add)
                    last.then_inc(q_biased, 1)
                if n in (3, 4) and project:
                    half = n - 3
                    dve.wait_ge(k_hi[half], i + 2)
                    V.scalar_tensor_tensor(kl[:, w, half, :], bank[f"K{half}"][:, 0:T], bqk16[:, 1, half:half + 1],
                                           kh[:, w, half, :], ALU.add, ALU.subtract).then_inc(k_lo[half], 1)
                if n == 10 and output:
                    dve.wait_ge(done["WO"], i - 1)
                    dve.wait_ge(xb_out, i - 1)
                    V.tensor_tensor(X[0:S, i - 2, :], bank["WO"][0:S, 0:D], xb[:], ALU.add).then_inc(x2_out, 1)
                    dve.wait_ge(x2_out, i - 1)
                    V.bn_stats(stats2[:, i - 2, :], X[0:S, i - 2, :]).then_inc(st_out, 1)
                if n == 9 and isinstance(i, int) and i == -1:
                    normalise(1, 1)
                if n == 9 and split_next and (not isinstance(i, int) or i >= 0):
                    normalise(i + 2, u)

        split_steps(dve, step)
        dve.wait_ge(st_out, B)

    @block.tensor
    def _(pe):
        MM = nc.tensor.matmul
        pe.wait_ge(diag, 1)
        pe.wait_ge(prep_act, 3)
        MM(pj[0][:, 0:S], ones[:], keep_diag[:], start=True, stop=True).then_inc(prep_pe, 1)
        pe.wait_ge(loaded["wo"], 16)
        MM(pj[1][0:S, 0:D], ones[0:1, 0:S], bo_row[:], start=True, stop=False)
        for a in range(HALVES):
            last = MM(pj[1][0:S, 0:D], bv[:, a:a + 1].to_broadcast([P, S]), wo[:, a, :], start=False,
                      stop=(a == HALVES - 1))
        last.then_inc(prep_pe, 1)
        pe.wait_ge(ready, 1)

        def project3(out, lhs, rhs):
            for a in range(HALVES):
                (lh, ll), (rh, rl) = lhs(a), rhs(a)
                MM(out, lh, rh, start=(a == 0), stop=False)
                MM(out, lh, rl, start=False, stop=False)
                last = MM(out, ll, rh, start=False, stop=(a == HALVES - 1))
            return last

        def step(i, u, project, find, attend, output, split_next, load_next):
            w = 1 - u
            later = not isinstance(i, int)

            def bank_free(job):
                users = {"xT": (project, [(xt_hi, i + 2), (xt_lo, i + 2)]), "OT": (output, [(at_out, i - 1)]),
                         "Q": (project, [(q_biased, i + 2)]), "K0": (project, [(k_hi[0], i + 2), (k_lo[0], i + 2)]),
                         "K1": (project, [(k_hi[1], i + 2), (k_lo[1], i + 2)]), "AT": (output, [(att_out, i - 1)]),
                         "V01": (find, [(v_out[0], i + 1)]), "V2": (find, [(v_out[1], i + 1)]),
                         "MT": (find, [(top_out, i + 1)]), "WO": (output, [(x2_out, i - 1)])}
                n = JOBS.index(job)
                for m in range(n - 2, -1, -2):
                    runs, emptied = users[JOBS[m]]
                    if runs:
                        for s, c in emptied:
                            pe.wait_ge(s, c)
                        return
                if n % 2 == 0:
                    reached(pe, top_out, i if later else min(i, B))
                    if not later and i == 0:
                        pe.wait_ge(k_hi[1], 1)
                        pe.wait_ge(k_lo[1], 1)
                else:
                    reached(pe, x2_out, i - 2)
                    reached(pe, v_out[1], i if later else min(i, B))
                    if not later and i == 0:
                        pe.wait_ge(k_hi[0], 1)
                        pe.wait_ge(k_lo[0], 1)

            def find_max(h):
                if h % (H // 2) == 0:
                    pe.wait_ge(stacked[2 * h // H][u], in_stack(i, u))
                if h >= 2:
                    pe.wait_ge(a_top[h - 2], i + 1)
                elif later or i >= 1:
                    pe.wait_ge(a_top[h + H - 2], i)
                q = (h % 2) * S
                MM(sa[h % 2][0:S, 0:T], stack[:, u, h // 2, T + q:T + q + S], stack[:, u, h // 2, 0:T],
                   start=True, stop=True).then_inc(a_scored[h], 1)

            def attend_scores(n):
                g, c = divmod(n, CH)
                if n >= 3:
                    pe.wait_ge(b_exp[n - 3], i)
                elif later or i >= 2:
                    pe.wait_ge(b_exp[n + SLOTS - 3], i - 1)
                if n == 0:
                    pe.wait_ge(top_in, 48 * i)
                MM(sbk[n % 3][:, 0:HG * S], sel[:], mb[:, w, c, g * HG * S:(g + 1) * HG * S], start=True, stop=False)
                for q in range(2):
                    last = MM(sbk[n % 3][:, 2 * S * q:2 * S * (q + 1)], stack[:, w, 2 * g + q, KC * c:KC * c + P],
                              stack[:, w, 2 * g + q, T:ROW], start=False, stop=(q == 1))
                last.then_inc(b_scored[n], 1)

            def attend_values(n):
                g, c = divmod(n, CH)
                pe.wait_ge(b_exp[n], i)
                if n == 0:
                    pe.wait_ge(v_out[1], i)
                    reached(pe, ot_out, i - 1)
                for j in range(HG):
                    last = MM(ot[32 * j:32 * j + DV, g * S:(g + 1) * S], vt[:, w, c, HG * g + j, :],
                              pt[:, n % 4, j * S:(j + 1) * S], start=(c == 0), stop=(c == CH - 1),
                              tile_position=(0, 32 * j))
                last.then_inc(b_pv[n], 1)

            def job(name):
                out = bank[name]
                if name == "xT" and project:
                    pe.wait_ge(xn_made, i + 2)
                    bank_free(name)
                    for a in range(HALVES):
                        last = nc.tensor.transpose(out[:, a * S:(a + 1) * S], xn[:, w, a * P:(a + 1) * P],
                                                   ident[0:S, 0:S])
                elif name == "OT" and output:
                    pe.wait_ge(ot_out, i - 1)
                    bank_free(name)
                    for g in range(GROUPS):
                        last = nc.tensor.transpose(out[0:S, g * P:(g + 1) * P], ots[:, g * S:(g + 1) * S], ident[:])
                elif name == "Q" and project:
                    pe.wait_ge(xt_lo, i + 2)
                    bank_free(name)
                    for m in range(HALVES):
                        last = project3(out[:, m * S:(m + 1) * S],
                                        lambda a: (wh[:, 0, a, m * P:(m + 1) * P], wl[:, 0, a, m * P:(m + 1) * P]),
                                        lambda a: (xth[:, a, :], xtl[:, a, :]))
                elif name in ("K0", "K1") and project:
                    m = int(name[1])
                    if m == 0:
                        pe.wait_ge(ct_lo, i + 2)
                    bank_free(name)
                    last = project3(out[:, 0:T],
                                    lambda a: (wh[:, 1, a, m * P:(m + 1) * P], wl[:, 1, a, m * P:(m + 1) * P]),
                                    lambda a: (cth[:, w, a, :], ctl[:, w, a, :]))
                elif name == "AT" and output:
                    pe.wait_ge(at_out, i - 1)
                    bank_free(name)
                    flat = at[:].rearrange("p h d -> p (h d)")
                    for a in range(HALVES):
                        last = nc.tensor.transpose(out[:, a * S:(a + 1) * S], flat[:, a * P:(a + 1) * P],
                                                   ident[0:S, 0:S])
                elif name in ("V01", "V2") and find:
                    bank_free(name)
                    for c in ((0, 1) if name == "V01" else (2,)):
                        last = project3(out[0:KC, (c % 2) * D:(c % 2 + 1) * D],
                                        lambda a: (cth[:, u, a, c * KC:(c + 1) * KC], ctl[:, u, a, c * KC:(c + 1) * KC]),
                                        lambda a: (wh[:, 2, a, :], wl[:, 2, a, :]))
                elif name == "MT" and find:
                    pe.wait_ge(a_top[H - 1], i + 1)
                    bank_free(name)
                    last = nc.tensor.transpose(out[0:H, 0:S], top[:, u, :], ident[0:S, 0:S])
                elif name == "WO" and output:
                    pe.wait_ge(att_out, i - 1)
                    bank_free(name)
                    for a in range(HALVES):
                        last = MM(out[0:S, 0:D], att[:, a, :], wo[:, a, :], start=(a == 0), stop=(a == HALVES - 1))
                else:
                    return
                last.then_inc(done[name], 1)

            for n in range(SLOTS + 2):
                if attend and n < SLOTS:
                    attend_scores(n)
                if find and n < 8:
                    find_max(2 * n)
                if attend and n >= 2:
                    attend_values(n - 2)
                if find and n < 8:
                    find_max(2 * n + 1)
                for name in JOBS:
                    if JOB_AT[name] == n:
                        job(name)

        split_steps(pe, step)


TS = 256
NT = (2 * B * S + E * (TS - 1)) // TS
WE = 256.0
LN2_EPS = 1e-5
LN3_EPS = 1e-12
UNROLL = 4


def inverse_root(nc, dve, tick, var, eps, root, old, tmp):
    V = nc.vector
    tick(V.tensor_scalar(var, var, eps, None, ALU.add))
    V.tensor_copy(old, var).then_inc(root, 1)
    dve.wait_ge(root, 2)
    tick(V.reciprocal(var, var))
    tick(V.tensor_tensor(tmp, var, var, ALU.mult))
    tick(V.tensor_tensor(tmp, tmp, old, ALU.mult))
    tick(V.tensor_scalar(tmp, tmp, -0.5, 1.5, ALU.mult, ALU.add))
    tick(V.tensor_tensor(var, var, tmp, ALU.mult))


def route_block(nc, sems, ctx, t, X, stats2, keep, rows):
    sb = lambda name, shape, dt: ctx.enter_context(nc.sbuf_tensor(name, shape, dt))
    ps = lambda name, shape, dt: ctx.enter_context(nc.psum_tensor(name, shape, dt))
    sem = sems.new
    w1h, w1l, w2h, w2l = keep["w"]
    rstd, shift, cw, slot, tile_expert = (keep[k] for k in ("rstd", "shift", "cw", "slot", "tile_expert"))

    xhl = sb("xhl", [S, B, 2 * D], F16)
    xn2 = sb("xn2", [S, 2, D], F32)
    xt2 = sb("xt2", [P, 2, HALVES, S], F32)
    ident = sb("ident2", [P, P], F32)
    rw = sb("rw", [P, HALVES, E], F32)
    rb = sb("rb", [S, E], F32)
    before32 = sb("before32", [S, S], F32)
    before = sb("before", [S, S], BF16)
    all_ones = sb("all_ones", [S, S], BF16)
    falling = sb("falling", [S, E], F32)
    tile_start = sb("tile_start", [1, NT, E], F32)
    mean = sb("mean2", [S, B, 1], F32)
    var_old = sb("var_old", [S, B, 1], F32)
    tmp = sb("tmp2", [S, B, 1], F32)
    L = sb("logits", [S, B, E], F32)
    pick = [sb(f"pick{k}", [S, B, E], F32) for k in range(2)]
    key = sb("key", [S, B, E], F32)
    m = [sb(f"m{k}", [S, B, 1], F32) for k in range(2)]
    first = sb("first", [S, B, 1], F32)
    both = sb("both", [S, B, E], BF16)
    count = [sb(f"count{k}", [S, B, E], F32) for k in range(2)]
    size = [sb(f"size{k}", [S, E], F32) for k in range(3)]
    whole = sb("whole", [S, E], I32)
    whole2 = sb("whole2", [S, E], I32)
    slot_f = first
    past = tile_start
    past_n = sb("past_n", [1, NT, 1], F32)
    stage1 = w2l[:].rearrange("p e f d -> p (e f d)").bitcast(F32).rearrange("p (k n) -> p k n", k=4)
    stage2 = X[:].rearrange("p b d -> p (b d)").rearrange("p (k n) -> p k n", k=4)

    tp = [ps(f"tp{k}", [P, 512], F32) for k in range(2)]
    lg = [ps(f"lg{k}", [P, 512], F32) for k in range(2)]
    rank, total = ps("rank", [P, 512], F32), ps("total", [P, 512], F32)

    loaded = sem("r_loaded")
    ones_set = sem("ones_set")
    steps = sem("r_steps")
    root = sem("r_root")
    normed, hi, lo, turned, copied, scored, logged = (sem("r_" + n) for n in (
        "normed", "hi", "lo", "turned", "copied", "scored", "logged"))
    w1_in = [sem(f"w1_in{u}") for u in range(2)]
    w2_in = [sem(f"w2_in{u}") for u in range(2)]
    w1_hi, w1_lo, w2_hi, w2_lo = (sem(n) for n in ("w1_hi", "w1_lo", "w2_hi", "w2_lo"))
    gap, expd, picked, ranked, slotted, scattered = (sem("r_" + n) for n in (
        "gap", "expd", "picked", "ranked", "slotted", "scattered"))

    block = ctx.enter_context(nc.Block())
    FIXED = 16 * 6

    def tiles(eng, per_expert, per_tile):
        def pair(e0):
            for u in range(2):
                per_expert(e0 + u, u)
                for k in range(UNROLL):
                    per_tile(e0 * UNROLL + (UNROLL * u + k), k % 2)
        pair(0)
        with eng.Fori(0, E // 2 - 1) as j:
            pair(j * 2 + 2)

    @block.sync
    def _(sp):
        for dst, src in ((ident[:], t["ident"]), (rw[:], t["router_w"]), (rb[:], t["router_b"].to_broadcast([S, E])),
                         (before32[:], t["before"]), (falling[:], t["falling"]),
                         (tile_start[:], t["tile_start"])):
            sp.dma_start(dst, src).then_inc(loaded, 16)
        for e in range(2):
            sp.dma_start(stage1[:, e, :], t["w1"][e]).then_inc(w1_in[e], 16)
        with sp.Fori(0, E // 2 - 1) as j:
            for u in range(2):
                sp.wait_ge(loaded, FIXED)
                sp.wait_ge(w1_hi, j * 2 + (1 + u))
                sp.wait_ge(w1_lo, j * 2 + (1 + u))
                sp.dma_start(stage1[:, u, :], t["w1"][j * 2 + (2 + u)]).then_inc(w1_in[u], 16)
        sp.wait_ge(normed, B)
        for e in range(2):
            sp.dma_start(stage2[:, e, :], t["w2"][e]).then_inc(w2_in[e], 16)
        with sp.Fori(0, E // 2 - 1) as j:
            for u in range(2):
                sp.wait_ge(loaded, FIXED)
                sp.wait_ge(w2_hi, j * 2 + (1 + u))
                sp.wait_ge(w2_lo, j * 2 + (1 + u))
                sp.dma_start(stage2[:, u, :], t["w2"][j * 2 + (2 + u)]).then_inc(w2_in[u], 16)

    @block.gpsimd
    def _(pool):
        nc.gpsimd.memset(all_ones[:], 1.0).then_inc(ones_set, 1)

        def per_tile(n, k):
            pool.wait_ge(hi, n + 1)
            nc.gpsimd.tensor_tensor(xhl[:, n, D:2 * D], xn2[:, k, :], xhl[:, n, 0:D], ALU.subtract).then_inc(lo, 1)

        tiles(pool, lambda e, u: None, per_tile)
        pool.wait_ge(lo, B)
        pool.wait_ge(slotted, 2)
        for n in range(B):
            for k in range(2):
                nc.gpsimd.indirect_dma_start(rows, bass.IndirectOffsetOnAxis(ap=slot[:, k, n:n + 1], axis=0),
                                             xhl[:, n, :], None).then_inc(scattered, 16)
        pool.wait_ge(scattered, 16 * 2 * B)

    @block.scalar
    def _(act):
        act.wait_ge(root, 1)
        nc.scalar.sqrt(rstd[:], rstd[:]).then_inc(root, 1)

        def per_expert(e, u):
            act.wait_ge(w1_in[u], (e - u) * 8 + 16)
            nc.scalar.mul(w1h[:, e].rearrange("p a f -> p (a f)"), stage1[:, u, :], WE).then_inc(w1_hi, 1)

        def per_tile(n, k):
            act.wait_ge(normed, n + 1)
            nc.scalar.copy(xhl[:, n, 0:D], xn2[:, k, :]).then_inc(hi, 1)
            act.wait_ge(turned, n + 1)
            reached(act, scored, n - 1)
            nc.scalar.copy(xt2[:, k].rearrange("p a s -> p (a s)"), tp[k][:, 0:HALVES * S]).then_inc(copied, 1)

        tiles(act, per_expert, per_tile)
        act.wait_ge(gap, 1)
        nc.scalar.activation(m[1][:], m[1][:], ACT.Exp).then_inc(expd, 1)
        with act.Fori(0, E // 2) as j:
            for u in range(2):
                act.wait_ge(w2_in[u], j * 16 + 16)
                nc.scalar.mul(w2h[:, j * 2 + u].rearrange("p f d -> p (f d)"), stage2[:, u, :], WE).then_inc(w2_hi, 1)

    @block.tensor
    def _(pe):
        MM = nc.tensor.matmul
        pe.wait_ge(loaded, FIXED)

        def logits(n, k):
            pe.wait_ge(copied, n + 1)
            reached(pe, logged, n - 1)
            for a in range(HALVES):
                last = MM(lg[k][0:S, 0:E], xt2[:, k, a, :], rw[:, a, :], start=(a == 0), stop=(a == HALVES - 1))
            last.then_inc(scored, 1)

        def per_tile(n, k):
            pe.wait_ge(normed, n + 1)
            reached(pe, copied, n - 1)
            for a in range(HALVES):
                last = nc.tensor.transpose(tp[k][:, a * S:(a + 1) * S], xn2[:, k, a * P:(a + 1) * P], ident[0:S, 0:S])
            last.then_inc(turned, 1)
            if not isinstance(n, int) or n >= 1:
                logits(n - 1, 1 - k)

        tiles(pe, lambda e, u: None, per_tile)
        logits(B - 1, 1)
        pe.wait_ge(ones_set, 1)
        pe.wait_ge(picked, 1)
        MM(rank[0:S, 0:B * E], before[:], both[:].rearrange("p b e -> p (b e)"), start=True, stop=True)
        MM(total[0:S, 0:B * E], all_ones[:], both[:].rearrange("p b e -> p (b e)"), start=True,
           stop=True).then_inc(ranked, 1)

    @block.vector
    def _(dve):
        V = nc.vector
        done = [0]

        def tick(instruction):
            done[0] += 1
            instruction.then_inc(steps, 1)
            dve.wait_ge(steps, done[0])

        row_stats(nc, dve, tick, stats2, mean[:], rstd[:], tmp[:])
        inverse_root(nc, dve, tick, rstd[:], LN2_EPS, root, var_old[:], tmp[:])
        tick(V.scalar_tensor_tensor(shift[:], mean[:], -1.0, rstd[:], ALU.mult, ALU.mult))
        dve.wait_ge(loaded, FIXED)
        tick(V.tensor_copy(before[:], before32[:]))

        def split(stage, high, low, counted):
            V.scalar_tensor_tensor(low, stage, WE, high, ALU.mult, ALU.subtract).then_inc(counted, 1)

        def per_expert(e, u):
            dve.wait_ge(w1_hi, e + 1)
            split(stage1[:, u, :], w1h[:, e].rearrange("p a f -> p (a f)"),
                  w1l[:, e].rearrange("p a f -> p (a f)"), w1_lo)

        def log(n, k):
            dve.wait_ge(scored, n + 1)
            V.tensor_tensor(L[:, n, :], lg[k][0:S, 0:E], rb[:], ALU.add).then_inc(logged, 1)

        def per_tile(n, k):
            reached(dve, turned, n - 1)
            reached(dve, hi, n - 1)
            reached(dve, lo, n - 1)
            V.tensor_scalar(xn2[:, k, :], X[0:S, n, :], rstd[:, n, :], shift[:, n, :], ALU.mult, ALU.add).then_inc(normed, 1)
            if not isinstance(n, int) or n >= 1:
                log(n - 1, 1 - k)

        tiles(dve, per_expert, per_tile)
        log(B - 1, 1)
        dve.wait_ge(logged, B)
        dve.wait_ge(w1_lo, E)
        wide = lambda a: a.to_broadcast([S, B, E])
        for k in range(2):
            tick(V.tensor_reduce(m[k][:], L[:], AX.X, ALU.max))
            tick(V.tensor_tensor(key[:], L[:], wide(m[k][:]), ALU.is_equal))
            tick(V.tensor_tensor(key[:], key[:], falling[:].unsqueeze(1).to_broadcast([S, B, E]), ALU.mult))
            tick(V.tensor_reduce(first[:], key[:], AX.X, ALU.max))
            tick(V.tensor_tensor(pick[k][:], key[:], wide(first[:]), ALU.is_equal))
            if k == 0:
                tick(V.scalar_tensor_tensor(L[:], pick[0][:], -3.0e38, L[:], ALU.mult, ALU.add))
        V.tensor_tensor(both[:], pick[0][:], pick[1][:], ALU.add).then_inc(picked, 1)
        V.tensor_tensor(m[1][:], m[1][:], m[0][:], ALU.subtract).then_inc(gap, 1)
        dve.wait_ge(ranked, 1)
        tick(V.tensor_copy(count[0][:].rearrange("p b e -> p (b e)"), total[0:S, 0:B * E]))
        at, s = 0, 1
        while s < B:
            V.tensor_copy(count[1 - at][:, 0:s, :], count[at][:, 0:s, :])
            tick(V.tensor_tensor(count[1 - at][:, s:B, :], count[at][:, s:B, :], count[at][:, 0:B - s, :], ALU.add))
            at, s = 1 - at, 2 * s
        tick(V.tensor_scalar(size[0][:], count[at][:, B - 1, :], float(TS - 1), None, ALU.add))
        shift_bits = TS.bit_length() - 1
        tick(V.tensor_copy(whole[:], size[0][:]))
        tick(V.tensor_single_scalar(whole2[:], whole[:], shift_bits, ALU.arith_shift_right))
        tick(V.tensor_copy(size[0][:], whole2[:]))
        tick(V.tensor_scalar(size[0][:], size[0][:], float(TS), None, ALU.mult))
        tick(V.tensor_copy(size[1][:], size[0][:]))
        e_at, s = 1, 1
        while s < E:
            V.tensor_copy(size[3 - e_at][:, 0:s], size[e_at][:, 0:s])
            tick(V.tensor_tensor(size[3 - e_at][:, s:E], size[e_at][:, s:E], size[e_at][:, 0:E - s], ALU.add))
            e_at, s = 3 - e_at, 2 * s
        ends, start = size[e_at], size[0]
        tick(V.tensor_tensor(start[:], ends[:], start[:], ALU.subtract))
        pos = count[at]
        flat = lambda a: a[:].rearrange("p b e -> p (b e)")
        tick(V.tensor_tensor(flat(pos), flat(pos), total[0:S, 0:B * E], ALU.subtract))
        tick(V.tensor_tensor(flat(pos), flat(pos), rank[0:S, 0:B * E], ALU.add))
        tick(V.tensor_tensor(pos[:], pos[:], start[:].unsqueeze(1).to_broadcast([S, B, E]), ALU.add))
        for k in range(2):
            tick(V.tensor_tensor(key[:], pick[k][:], pos[:], ALU.mult))
            tick(V.tensor_reduce(slot_f[:], key[:], AX.X, ALU.add))
            V.tensor_copy(slot[:, k, :], slot_f[:].rearrange("p b o -> p (b o)")).then_inc(slotted, 1)
            dve.wait_ge(slotted, k + 1)
        tick(V.tensor_tensor(past[:], tile_start[:], ends[0:1, :].unsqueeze(1).to_broadcast([1, NT, E]), ALU.is_ge))
        tick(V.tensor_reduce(past_n[:], past[:], AX.X, ALU.add))
        tick(V.tensor_scalar(past_n[:], past_n[:], float(E - 1), None, ALU.min))
        tick(V.tensor_copy(tile_expert[:], past_n[:].rearrange("p n o -> p (n o)")))
        dve.wait_ge(expd, 1)
        w = [cw[:, k, :].unsqueeze(2) for k in range(2)]
        tick(V.tensor_scalar(w[0], m[1][:], 1.0, None, ALU.add))
        tick(V.reciprocal(w[0], w[0]))
        tick(V.tensor_tensor(w[1], m[1][:], w[0], ALU.mult))
        with dve.Fori(0, E // 2) as j:
            for u in range(2):
                dve.wait_ge(w2_hi, j * 2 + (1 + u))
                split(stage2[:, u, :], w2h[:, j * 2 + u].rearrange("p f d -> p (f d)"),
                      w2l[:, j * 2 + u].rearrange("p f d -> p (f d)"), w2_lo)
        dve.wait_ge(w2_lo, E)


def expert_steps(eng, step):
    def edge(i):
        step(i, i % 2, 0 <= i < NT, 1 <= i, i + 1 < NT, i + 2 < NT)
    for i in (-1, 0, 1, 2):
        edge(i)
    pairs = (NT - 5) // 2
    with eng.Fori(0, pairs) as j:
        for u in range(2):
            step(j * 2 + (3 + u), 1 - u, True, True, True, True)
    for i in range(3 + 2 * pairs, NT + 1):
        edge(i)


def expert_block(nc, sems, ctx, t, keep, rows, y):
    sb = lambda name, shape, dt: ctx.enter_context(nc.sbuf_tensor(name, shape, dt))
    ps = lambda name, shape, dt: ctx.enter_context(nc.psum_tensor(name, shape, dt))
    sem = sems.new
    w1h, w1l, w2h, w2l = keep["w"]
    tile_expert = keep["tile_expert"]
    SUB = TS // P

    ident = sb("ident3f", [P, P], F32)
    ident16 = sb("ident16", [P, P], F16)
    b1 = sb("b1", [P, E, FC], F32)
    b2 = sb("b2", [P, E, D], F32)
    xr = sb("xr", [P, 2, SUB, 2 * D], F16)
    xt = sb("xt", [P, 2, 2 * HALVES, TS], F16)
    g = sb("g", [P, 2, 2 * TS], F32)
    hh = sb("hh", [P, 2, FC, TS], F16)
    hl = sb("hl", [P, 2, FC, TS], F16)
    ys = sb("ys", [P, 2, SUB, D], F32)

    tb = ps("tb", [P, 2 * HALVES * TS], F16)
    hb = [ps(f"hb{k}", [P, 512], F32) for k in range(3)]
    yb = [[ps(f"yb{u}{s}", [P, 512], F32) for s in range(SUB)] for u in range(2)]

    loaded, ready = sem("e_loaded"), sem("e_ready")
    rows_in = [sem(f"rows_in{u}") for u in range(2)]
    turned, moved = sem("e_turned"), sem("e_moved")
    FP = FC // 2
    h_done = [sem(f"h_done{k}") for k in range(FP)]
    h_gelu = [sem(f"h_gelu{k}") for k in range(FP)]
    h_hi = [sem(f"h_hi{k}") for k in range(FP)]
    h_lo = [sem(f"h_lo{k}") for k in range(FP)]
    y_done, y_out = sem("y_done"), sem("y_out")
    y_stored = [sem(f"y_stored{u}") for u in range(2)]

    block = ctx.enter_context(nc.Block())

    def by_parity(b, u):
        return (b - u) * 8 + 16

    @block.sync
    def _(sp):
        sp.dma_start(ident[:], t["ident"]).then_inc(loaded, 16)
        sp.dma_start(b1[:], t["b1"]).then_inc(loaded, 16)
        sp.dma_start(b2[:].rearrange("p e d -> p (e d)"), t["b2"].to_broadcast([P, E * D])).then_inc(loaded, 16)
        for b in range(1):
            sp.dma_start(xr[:, b], rows[b * TS:(b + 1) * TS, :].rearrange("(s p) n -> p s n", p=P)).then_inc(rows_in[b], 16)
        row_tiles = rows.rearrange("(i s p) n -> i p s n", p=P, s=SUB)
        y_tiles = y.rearrange("(i s p) n -> i p s n", p=P, s=SUB)

        def step(i, u, first, second, turn, load):
            if load:
                sp.wait_ge(loaded, 48)
                reached(sp, turned, i + 1)
                sp.dma_start(xr[:, u], row_tiles[i + 2]).then_inc(rows_in[u], 16)
            if second:
                sp.wait_ge(loaded, 48)
                sp.wait_ge(y_out, i)
                sp.dma_start(y_tiles[i - 1], ys[:, 1 - u]).then_inc(y_stored[1 - u], 16)

        expert_steps(sp, step)
        sp.wait_ge(y_stored[0], 16 * ((NT + 1) // 2))
        sp.wait_ge(y_stored[1], 16 * (NT // 2))

    @block.tensor
    def _(pe):
        MM = nc.tensor.matmul
        pe.wait_ge(ready, 1)
        expert = {}

        def step(i, u, first, second, turn, load):
            w = 1 - u
            if turn:
                pe.wait_ge(rows_in[w], by_parity(i + 1, w))
                reached(pe, moved, i + 1)
                for q in range(2 * HALVES):
                    for s in range(SUB):
                        last = nc.tensor.transpose(tb[:, q * TS + s * P:q * TS + (s + 1) * P],
                                                   xr[:, w, s, q * P:(q + 1) * P], ident16[:])
                last.then_inc(turned, 1)
            if first:
                e1 = pe.value_load(tile_expert[0:1, bass.ds(i, 1)], min_val=0, max_val=E - 1)
            if second:
                e2 = pe.value_load(tile_expert[0:1, bass.ds(i - 1, 1)], min_val=0, max_val=E - 1)
            if first:
                pe.wait_ge(moved, i + 1)
            for f in range(FC):
                if first:
                    n = f // 2
                    bank = hb[n % 2]
                    if f % 2 == 0:
                        if n >= 2:
                            pe.wait_ge(h_gelu[n - 2], i + 1)
                        else:
                            reached(pe, h_gelu[n + FP - 2], i)
                    out = bank[:, (f % 2) * TS:(f % 2 + 1) * TS]
                    cols = slice(f * P, (f + 1) * P)
                    for a in range(HALVES):
                        MM(out, w1h[:, e1, a, cols], xt[:, u, a, :], start=(a == 0), stop=False)
                        MM(out, w1h[:, e1, a, cols], xt[:, u, HALVES + a, :], start=False, stop=False)
                        last = MM(out, w1l[:, e1, a, cols], xt[:, u, a, :], start=False, stop=(a == HALVES - 1))
                    if f % 2 == 1:
                        last.then_inc(h_done[n], 1)
                if second:
                    if f % 2 == 0:
                        pe.wait_ge(h_lo[f // 2], i)
                    if f == 0:
                        reached(pe, y_out, i - 2)
                    for s in range(SUB):
                        out = yb[w][s][:, 0:D]
                        tok = slice(s * P, (s + 1) * P)
                        MM(out, hh[:, w, f, tok], w2h[:, e2, f, :], start=(f == 0), stop=False)
                        MM(out, hh[:, w, f, tok], w2l[:, e2, f, :], start=False, stop=False)
                        last = MM(out, hl[:, w, f, tok], w2h[:, e2, f, :], start=False, stop=(f == FC - 1))
            if second:
                last.then_inc(y_done, 1)

        expert_steps(pe, step)

    @block.scalar
    def _(act):
        act.wait_ge(ready, 1)

        def step(i, u, first, second, turn, load):
            if first:
                e1 = act.value_load(tile_expert[0:1, bass.ds(i, 1)], min_val=0, max_val=E - 1)
                for n in range(FP):
                    act.wait_ge(h_done[n], i + 1)
                    if n >= 2:
                        act.wait_ge(h_lo[n - 2], i + 1)
                    else:
                        reached(act, h_lo[n + FP - 2], i)
                    for k in range(2):
                        last = nc.scalar.activation(g[:, n % 2, k * TS:(k + 1) * TS], hb[n % 2][:, k * TS:(k + 1) * TS],
                                                    ACT.Gelu, bias=b1[:, e1, 2 * n + k:2 * n + k + 1], scale=1.0 / WE)
                    last.then_inc(h_gelu[n], 1)

        expert_steps(act, step)

    @block.vector
    def _(dve):
        V = nc.vector
        dve.wait_ge(loaded, 48)
        V.tensor_copy(ident16[:], ident[:]).then_inc(ready, 1)

        def step(i, u, first, second, turn, load):
            w = 1 - u
            if turn:
                dve.wait_ge(turned, i + 2)
                if not isinstance(i, int) or i >= 1:
                    dve.wait_ge(h_done[FP - 1], i)
                V.tensor_copy(xt[:, w].rearrange("p q n -> p (q n)"), tb[:]).then_inc(moved, 1)
            if first:
                for n in range(FP):
                    dve.wait_ge(h_gelu[n], i + 1)
                    if n == 0 and (not isinstance(i, int) or i >= 2):
                        dve.wait_ge(y_done, i - 1)
                    high = hh[:, u, 2 * n:2 * n + 2, :].rearrange("p f t -> p (f t)")
                    V.tensor_copy(high, g[:, n % 2, :]).then_inc(h_hi[n], 1)
                    dve.wait_ge(h_hi[n], i + 1)
                    V.tensor_tensor(hl[:, u, 2 * n:2 * n + 2, :].rearrange("p f t -> p (f t)"), g[:, n % 2, :],
                                    high, ALU.subtract).then_inc(h_lo[n], 1)
            if second:
                e2 = dve.value_load(tile_expert[0:1, bass.ds(i - 1, 1)], min_val=0, max_val=E - 1)
                dve.wait_ge(y_done, i)
                if not isinstance(i, int) or i >= 3:
                    dve.wait_ge(y_stored[w], by_parity(i - 3, w))
                for s in range(SUB):
                    last = V.scalar_tensor_tensor(ys[:, w, s, :], yb[w][s][:, 0:D], 1.0 / WE, b2[:, e2, :],
                                                  ALU.mult, ALU.add)
                last.then_inc(y_out, 1)

        expert_steps(dve, step)


def combine_block(nc, sems, ctx, t, keep, X, x2, y, out):
    sb = lambda name, shape, dt: ctx.enter_context(nc.sbuf_tensor(name, shape, dt))
    sem = sems.new
    rstd2, shift2, cw, slot = (keep[k] for k in ("rstd", "shift", "cw", "slot"))
    BUF = 4

    X = X[0:S]
    z = sb("z", [S, B, D], F32)
    yg = [[sb(f"yg{k}{b}", [S, D], F32) for k in range(2)] for b in range(BUF)]
    stats = sb("stats3", [S, B, 6], F32)
    mean = sb("mean3", [S, B, 1], F32)
    rstd = sb("rstd3", [S, B, 1], F32)
    old = sb("old3", [S, B, 1], F32)
    tmp = sb("tmp3", [S, B, 1], F32)
    ln_w = sb("ln_w", [S, D], F32)
    ln_b = sb("ln_b", [S, D], F32)

    x_in, loaded, steps, root = sem("c_x"), sem("c_loaded"), sem("c_steps"), sem("c_root")
    got = [sem(f"got{b}") for b in range(BUF)]
    based, half, summed, stated = sem("based"), sem("half"), sem("summed"), sem("stated")
    normed, weighted, residual, final, stored = (sem("c_" + n) for n in (
        "normed", "weighted", "residual", "final", "stored"))

    block = ctx.enter_context(nc.Block())

    @block.sync
    def _(sp):
        sp.dma_start(X[:], x2.rearrange("b s d -> s b d")).then_inc(x_in, 16)
        sp.dma_start(ln_w[:], t["ln_w"].to_broadcast([S, D])).then_inc(loaded, 16)
        sp.dma_start(ln_b[:], t["ln_b"].to_broadcast([S, D])).then_inc(loaded, 16)
        with sp.Fori(0, B // 4) as j:
            sp.wait_ge(loaded, 32)
            sp.wait_ge(final, j * 4 + 4)
            sp.dma_start(out.rearrange("(j b) s d -> j s b d", b=4)[j],
                         z[:, bass.ds(j * 4, 4), :]).then_inc(stored, 16)
        sp.wait_ge(stored, 16 * (B // 4))

    @block.gpsimd
    def _(pool):
        for n in range(B):
            b = n % BUF
            if n >= BUF:
                pool.wait_ge(summed, n - BUF + 1)
            for k in range(2):
                nc.gpsimd.indirect_dma_start(yg[b][k][:], None, y,
                                             bass.IndirectOffsetOnAxis(ap=slot[:, k, n:n + 1], axis=0)).then_inc(got[b], 16)
        pool.wait_ge(loaded, 32)
        with pool.Fori(0, B) as n:
            pool.wait_ge(normed, n + 1)
            nc.gpsimd.tensor_tensor(z[:, n, :], z[:, n, :], ln_w[:], ALU.mult).then_inc(weighted, 1)

    @block.scalar
    def _(act):
        act.wait_ge(root, 1)
        nc.scalar.sqrt(rstd[:], rstd[:]).then_inc(root, 1)

    @block.vector
    def _(dve):
        V = nc.vector
        done = [0]

        def tick(instruction):
            done[0] += 1
            instruction.then_inc(steps, 1)
            dve.wait_ge(steps, done[0])

        dve.wait_ge(x_in, 16)

        def base(n):
            V.tensor_scalar(z[:, n, :], X[:, n, :], rstd2[:, n, :], shift2[:, n, :], ALU.mult, ALU.add).then_inc(based, 1)

        for n in range(B):
            base(n)
            dve.wait_ge(based, n + 1)
            dve.wait_ge(got[n % BUF], 32 * (n // BUF + 1))
            V.scalar_tensor_tensor(z[:, n, :], yg[n % BUF][0][:], cw[:, 0, n:n + 1], z[:, n, :], ALU.mult,
                                   ALU.add).then_inc(half, 1)
            dve.wait_ge(half, n + 1)
            V.scalar_tensor_tensor(z[:, n, :], yg[n % BUF][1][:], cw[:, 1, n:n + 1], z[:, n, :], ALU.mult,
                                   ALU.add).then_inc(summed, 1)
            dve.wait_ge(summed, n + 1)
            V.bn_stats(stats[:, n, :], z[:, n, :]).then_inc(stated, 1)
        dve.wait_ge(stated, B)
        row_stats(nc, dve, tick, stats, mean[:], rstd[:], tmp[:])
        inverse_root(nc, dve, tick, rstd[:], LN3_EPS, root, old[:], tmp[:])
        dve.wait_ge(loaded, 32)
        tick(V.scalar_tensor_tensor(mean[:], mean[:], -1.0, rstd[:], ALU.mult, ALU.mult))
        with dve.Fori(0, B) as n:
            V.tensor_scalar(z[:, n, :], z[:, n, :], rstd[:, n, :], mean[:, n, :], ALU.mult, ALU.add).then_inc(normed, 1)
            V.tensor_tensor(X[:, n, :], X[:, n, :], ln_b[:], ALU.add).then_inc(residual, 1)
            dve.wait_ge(residual, n + 1)
            dve.wait_ge(weighted, n + 1)
            V.tensor_tensor(z[:, n, :], z[:, n, :], X[:, n, :], ALU.add).then_inc(final, 1)


class Semaphores:
    def __init__(self, nc):
        self.nc, self.stack, self.made = nc, ExitStack(), []

    def new(self, name):
        self.made.append(self.stack.enter_context(self.nc.semaphore(name)))
        return self.made[-1]

    def __enter__(self):
        return self

    def __exit__(self, *error):
        with self.nc.Block() as block:
            @block.gpsimd
            def _(pool):
                for s in self.made:
                    pool.sem_clear(s)
        self.stack.close()


def program(nc, t, out):
    rows = nc.dram_tensor("rows", (NT * TS, 2 * D), F16, kind="Internal").ap()
    y = nc.dram_tensor("y", (NT * TS, D), F32, kind="Internal").ap()
    x2 = nc.dram_tensor("x2", (B, S, D), F32, kind="Internal").ap()
    with ExitStack() as hold:
        sb = lambda name, shape, dt, stack=hold: stack.enter_context(nc.sbuf_tensor(name, shape, dt))
        keep = {"rstd": sb("rstd2", [S, B, 1], F32), "shift": sb("shift2", [S, B, 1], F32),
                "cw": sb("cw", [S, 2, B], F32), "slot": sb("slot", [S, 2, B], U32),
                "tile_expert": sb("tile_expert", [1, NT], I32)}
        stats2 = sb("stats2", [S, B, 6], F32)
        X = sb("X", [P, B, D], F32)
        with Semaphores(nc) as sems, ExitStack() as ctx:
            attention_block(nc, sems, ctx, t, (X, stats2), x2, rows)
        with ExitStack() as weights:
            keep["w"] = [weights.enter_context(nc.sbuf_tensor(n, s, F16)) for n, s in (
                ("w1h", [P, E, HALVES, F]), ("w1l", [P, E, HALVES, F]),
                ("w2h", [P, E, FC, D]), ("w2l", [P, E, FC, D]))]
            with Semaphores(nc) as sems, ExitStack() as ctx:
                route_block(nc, sems, ctx, t, X, stats2, keep, rows)
            with Semaphores(nc) as sems, ExitStack() as ctx:
                expert_block(nc, sems, ctx, t, keep, rows, y)
        with Semaphores(nc) as sems, ExitStack() as ctx:
            combine_block(nc, sems, ctx, t, keep, X, x2, y, out)


def kernel(**inputs):
    import numpy as np
    import concourse.bacc as bacc
    from concourse.bass_utils import run_bass_kernel_spmd

    g = {k: np.asarray(v) for k, v in inputs.items()}
    halves = lambda w: w.T.reshape(HALVES, P, -1).transpose(1, 0, 2)
    column = lambda b: b.reshape(HALVES, P).T
    mask = g["mask_1x1xSxS2_ik0"][0, 0]
    arrays = {
        "x": g["x"],
        "ctxT": g["ctx_1024"].transpose(0, 2, 1).reshape(B, HALVES, P, T).transpose(0, 2, 1, 3).reshape(B, P, HALVES * T),
        "wqkv": np.stack([halves(g["L0_xattn_W" + n]) for n in "qkv"], 1),
        "wo": halves(g["L0_xattn_Wo"]),
        "bqk": np.stack([column(g["L0_xattn_b" + n]) for n in "qk"], 1),
        "bv": column(g["L0_xattn_bv"]),
        "bo": g["L0_xattn_bo"].reshape(1, D),
        "mask_q": mask,
        "router_w": halves(g["L0_ffn_router_w"]),
        "router_b": g["L0_ffn_router_b"].reshape(1, E),
        "w1": g["L0_ffn_w1"].transpose(0, 2, 1).reshape(E, HALVES, P, F).transpose(0, 2, 1, 3).reshape(E, P, HALVES * F),
        "w2": g["L0_ffn_w2"].transpose(0, 2, 1).reshape(E, FC, P, D).transpose(0, 2, 1, 3).reshape(E, P, FC * D),
        "b1": g["L0_ffn_b1"].reshape(E, FC, P).transpose(2, 0, 1),
        "b2": g["L0_ffn_b2"].reshape(1, E * D),
        "ln_w": g["L0_ffn_ln_w"].reshape(1, D),
        "ln_b": g["L0_ffn_ln_b"].reshape(1, D),
        "mask_k": mask.T.reshape(CH, KC, S).transpose(1, 0, 2),
    }
    arrays.update(constants(np))
    arrays = {k: np.ascontiguousarray(v) for k, v in arrays.items()}
    nc = bacc.Bacc("TRN2", target_bir_lowering=False, num_devices=1)
    t = {k: nc.dram_tensor("in_" + k, a.shape, mybir.dt.from_np(a.dtype), kind="ExternalInput").ap()
         for k, a in arrays.items()}
    out = nc.dram_tensor("out_0", (B, S, D), F32, kind="ExternalOutput").ap()
    program(nc, t, out)
    r = run_bass_kernel_spmd(nc, [{"in_" + k: a for k, a in arrays.items()}], core_ids=[0])
    return r.results[0]["out_0"]


def constants(np):
    f = np.float32
    rows = np.arange(P)
    sel = np.concatenate([np.eye(KC, P), np.ones((1, P))]).astype(f)
    return {
        "ident": np.eye(P, dtype=f),
        "sel": sel,
        "before": np.triu(np.ones((S, S), f), 1),
        "falling": np.tile(np.arange(E, 0, -1, dtype=f), (S, 1)),
        "tile_start": np.tile((np.arange(NT, dtype=f) * TS)[:, None], (1, 1, E)),
        "parity": np.stack([rows // DH % 2 == 0, rows // DH % 2 == 1], 1).astype(f),
    }
```

```python
from contextlib import ExitStack

import numpy as np

import concourse.bass as bass
from concourse import mybir

F32 = mybir.dt.float32
F16 = mybir.dt.float16
BF16 = mybir.dt.bfloat16
I32 = mybir.dt.int32
U32 = mybir.dt.uint32
ALU = mybir.AluOpType
ACT = mybir.ActivationFunctionType
AX = mybir.AxisListType

P = 128
B, S, T, D = 32, 112, 375, 256
PREPARED = (0, 4, 18, 32)
H, DH = 16, 16
HALVES = D // P
CH = 3
KC = T // CH
PAIRS = H // 2
GROUPS = 4
HG = H // GROUPS
DV = DH + 1
SLOTS = GROUPS * CH
WS = 16.0
SCORE_SCALE = 1.0 / (WS * WS * DH ** 0.5)
MASKED = -float(2 ** 33)
LN1_EPS = 1e-5
E, F = 8, 1024
FC = F // P
WE = 256.0
LN2_EPS = 1e-5
PIECE = E * HALVES * F // B


def split_steps(eng, step):
    def edge(i):
        step(i, i % 2, i + 1 < B, 0 <= i < B, 1 <= i <= B, 2 <= i <= B + 1, i >= 3, i + 2 < B, i + 3 < B)
    for i in (-1, 0, 1, 2, 3):
        edge(i)
    pairs = (B - 3 - 4) // 2
    with eng.Fori(0, pairs) as j:
        for u in range(2):
            step(j * 2 + (4 + u), u, True, True, True, True, True, True, True)
    for i in range(4 + 2 * pairs, B + 3):
        edge(i)


def reached(eng, sem, count):
    if not isinstance(count, int) or count > 0:
        eng.wait_ge(sem, count)


def attention_block(nc, sems, ctx, t, keep_all, xn2_dram, rows, w2_halves):
    sb = lambda name, shape, dt: ctx.enter_context(nc.sbuf_tensor(name, shape, dt))
    ps = lambda name, shape, dt: ctx.enter_context(nc.psum_tensor(name, shape, dt))
    sem = sems.new
    w2_halves = w2_halves.rearrange("k p b n -> b p k n")
    X, L = keep_all["X"], keep_all["logits"]
    w1h, w1l = (keep_all[n][:].rearrange("p e f d -> p (e f d)").rearrange("p (b n) -> p b n", b=B)
                for n in ("w1h", "w1l"))
    row_tiles = rows[1:1 + B * S, :].rearrange("(b s) n -> b s n", b=B)

    ident = sb("ident", [P, P], F32)
    sel = sb("sel", [KC + 1, P], BF16)
    parity = sb("parity", [P, 2], F32)
    wh = sb("wh", [P, 3, HALVES, D], F16)
    wl = sb("wl", [P, 3, HALVES, D], F16)
    wo = sb("wo", [P, HALVES, D], F32)
    bqk = sb("bqk", [P, 2, HALVES], F32)
    bqk16 = sb("bqk16", [P, 2, HALVES], F32)
    bq_par = sb("bq_par", [P, HALVES, 2], F32)
    bv = sb("bv", [P, HALVES], F32)
    bo_row = sb("bo_row", [1, D], F32)
    bo_all = sb("bo_all", [S, D], F32)
    mask_add = sb("mask_add", [S, T], F32)
    n_masked = sb("n_masked", [S, 1], F32)
    keep_q = sb("keep_q", [S, 1], F32)
    keep = sb("keep", [P, S], F32)
    mv1 = sb("mv1", [S, B, 2], F32)
    ve1 = sb("ve1", [S, B, 1], F32)
    rstd1 = sb("rstd1", [S, B, 1], F32)
    shift1 = sb("shift1", [S, B, 1], F32)
    ct = sb("ct", [P, 2, HALVES * T], F32)
    cth = sb("cth", [P, 2, HALVES, T], F16)
    ctl = sb("ctl", [P, 2, HALVES, T], F16)
    xn = sb("xn", [S, D], F32)
    xth = sb("xth", [P, HALVES, S], F16)
    xtl = sb("xtl", [P, HALVES, S], F16)
    qf = sb("qf", [P, HALVES, 2, S], F32)
    qm = sb("qm", [P, HALVES, 2, S], F32)
    qh = sb("qh", [P, 2, HALVES, 2 * S], F16)
    ql = sb("ql", [P, 2, HALVES, 2 * S], F16)
    kh = sb("kh", [P, 2, HALVES, T], F16)
    kl = sb("kl", [P, 2, HALVES, T], F16)
    ROW = T + 2 * S
    stack = sb("stack", [96, 2, PAIRS, ROW], F16)
    vt = sb("vt", [KC, 2, CH, H, DV], F32)
    top = sb("top", [S, 2, H], F32)
    neg_top = sb("neg_top", [H, CH, S], BF16)
    mb = sb("mb", [KC + 1, 2, H, CH, S], BF16)
    pt = sb("pt", [P, 4, HG * S], F32)
    ots = sb("ots", [P, GROUPS * S], F32)
    rsum = sb("rsum", [S, H, 1], F32)
    at = sb("at", [S, H, DH], F32)
    att = sb("att", [P, HALVES, S], F32)
    stats2 = sb("stats2", [S, 6], F32)
    stats_now = sb("stats_now", [S, 6], F32)
    mv = sb("mv", [S, 2], F32)
    ve = sb("ve", [S, 1], F32)
    minus_half = sb("minus_half", [S, 1], F32)
    root0 = sb("root0", [S, 1], F32)
    newton = sb("newton", [S, 2], F32)
    rstd2 = sb("rstd2", [S, 1], F32)
    shift2 = sb("shift2", [S, 1], F32)
    xn2 = sb("xn2", [S, 2, D], F32)
    xhl = sb("xhl", [S, 2, 2 * D], F16)
    xt2 = sb("xt2", [P, 2 * HALVES, S], F16)
    ident16 = sb("ident16", [S, S], F16)
    rw32 = sb("rw32", [P, HALVES * E], F32)
    rw = sb("rw", [P, 2, HALVES * E], F16)
    rb = sb("rb", [S, E], F32)
    w_in = sb("w_in", [P, 2, PIECE], F32)
    w2_out = sb("w2_out", [P, 2, PIECE], F16)
    scratch = keep_all["w1l"][:].rearrange("p e f d -> p (e f d)").bitcast(F32)
    taken = [scratch.shape[1] // 2]

    def borrow(rows, *shape):
        size = int(np.prod(shape))
        taken[0] += size
        flat = scratch[0:rows, taken[0] - size:taken[0]]
        if len(shape) == 1:
            return flat
        names = "abc"[:len(shape)]
        return flat.rearrange(f"p ({' '.join(names)}) -> p {' '.join(names)}", **dict(zip(names, shape)))

    w32 = borrow(P, 3, HALVES, D)
    mask_q = borrow(S, T).bitcast(I32)
    mask_k = borrow(KC, CH, S).bitcast(I32)
    mk32 = borrow(KC, CH, S)
    sel32 = borrow(KC + 1, P)
    ones, keep_diag = borrow(S, P), borrow(S, S)
    stats1 = borrow(S, B, 6)

    sa = [ps(f"sa{k}", [P, 512], F32) for k in range(2)]
    sbk = [ps(f"sb{k}", [P, 512], F32) for k in range(3)]
    ot = ps("ot", [P, 512], F32)
    pj = [ps(f"pj{k}", [P, 512], F32) for k in range(2)]
    JOBS = ["xT", "OT", "Q", "K0", "K1", "AT", "V01", "V2", "MT", "WO"]
    bank = {job: pj[n % 2] for n, job in enumerate(JOBS)}
    turned2 = sa[0][:].bitcast(F16)[:, 0:2 * HALVES * S]
    logits_out = sa[1][0:S, 0:E]
    WO_AT, X2_AT, LG_AT = 10, 11, 12
    JOB_AT = {"xT": 0, "OT": 0, "Q": 2, "K0": 3, "K1": 4, "AT": 5, "V01": 5, "V2": 7, "MT": 9, "WO": WO_AT}

    loaded = {n: sem("ld_" + n) for n in ("x0", "x", "w", "small", "mask_k", "wo")}
    prep = sem("prep")
    varied1, rooted1 = sem("varied1"), sem("rooted1")
    mb_set, bo_set, router_set = sem("mb_set"), sem("bo_set"), sem("router_set")
    diag = sem("diag")
    ready = sem("ready")
    prep_pe = sem("prep_pe")
    prep_act = sem("prep_act")
    ct_in = [sem(f"ct_in{k}") for k in range(2)]
    ct_hi, ct_lo = sem("ct_hi"), sem("ct_lo")
    xn_made = sem("xn_made")
    done = {job: sem("pe_" + job) for job in JOBS + ["X2", "LG"]}
    xt_hi, xt_lo = sem("xt_hi"), sem("xt_lo")
    q_biased, q_kept, q_hi, q_lo = sem("q_biased"), sem("q_kept"), sem("q_hi"), sem("q_lo")
    k_hi = [sem(f"k_hi{k}") for k in range(2)]
    k_lo = [sem(f"k_lo{k}") for k in range(2)]
    v_out = [sem("v_out01"), sem("v_out2")]
    spilled = [sem(f"spilled{u}") for u in range(2)]
    stacked = [[sem(f"stacked{k}{u}") for u in range(2)] for k in range(HALVES)]
    a_scored = [sem(f"a_scored{k}") for k in range(H)]
    a_top = [sem(f"a_top{k}") for k in range(H)]
    top_out = sem("top_out")
    top_in = sem("top_in")
    b_scored = [sem(f"b_scored{k}") for k in range(SLOTS)]
    b_exp = [sem(f"b_exp{k}") for k in range(SLOTS)]
    b_pv = [sem(f"b_pv{k}") for k in range(SLOTS)]
    ot_out = sem("ot_out")
    rs_out, at_out, att_out, xb_out, x2_out, st_out = (sem(n) for n in (
        "rs_out", "at_out", "att_out", "xb_out", "x2_out", "st_out"))
    st_taken, varied, rooted, refined = sem("st_taken"), sem("varied"), sem("rooted"), sem("refined")
    n_made, n_hi, n_lo, xt2_out, lg_out = (sem(n) for n in ("n_made", "n_hi", "n_lo", "xt2_out", "lg_out"))
    n_stored = [sem(f"n_stored{u}") for u in range(2)]
    r_stored = [sem(f"r_stored{u}") for u in range(2)]
    w_loaded, w_stored = sem("w_loaded"), sem("w_stored")
    w_hi, w_lo = sem("w_hi"), sem("w_lo")

    def by_parity(b, u):
        return (b - u) * 8 + 16

    spill = nc.dram_tensor("spill", (2, 3, P, HALVES, ROW), F16, kind="Internal").ap()
    spill_read = [[[spill[u, r].rearrange("(q p) h n -> h p q n", p=32)[k] for k in range(HALVES)]
                   for r in range(3)] for u in range(2)]

    def in_stack(b, u):
        return (b - u) * 24 + 48

    def in_spill(b, u):
        return (b - u) * 48 + 96

    block = ctx.enter_context(nc.Block())

    @block.sync
    def _(sp):
        x_rows = t["x"].rearrange("b s d -> s b d")
        first = PREPARED[1]
        sp.dma_start(w32, t["wqkv"]).then_inc(loaded["w"], 16)
        for dst, src in ((mask_q, t["mask_q"]), (ident[:], t["ident"]), (parity[:], t["parity"]), (bqk[:], t["bqk"])):
            sp.dma_start(dst, src).then_inc(loaded["small"], 16)
        sp.dma_start(X[:, 0:first, :], x_rows[:, 0:first, :]).then_inc(loaded["x0"], 16)
        sp.dma_start(ct[:, 0, :], t["ctxT"][0]).then_inc(ct_in[0], 16)
        for dst, src in ((sel32, t["sel"]), (mask_k, t["mask_k"])):
            sp.dma_start(dst, src).then_inc(loaded["mask_k"], 16)
        sp.dma_start(ct[:, 1, :], t["ctxT"][1]).then_inc(ct_in[1], 16)
        sp.dma_start(X[:, first:B, :], x_rows[:, first:B, :]).then_inc(loaded["x"], 16)
        for dst, src in ((wo[:], t["wo"]), (bv[:], t["bv"]), (bo_row[:], t["bo"]), (rw32[:], t["router_w"]),
                         (rb[:], t["router_b"].to_broadcast([S, E]))):
            sp.dma_start(dst, src).then_inc(loaded["wo"], 16)

        def step(i, u, project, find, attend, output, norm, split_next, load_next):
            if load_next:
                reached(sp, ct_hi, i + 2)
                reached(sp, ct_lo, i + 2)
                sp.wait_ge(loaded["x"], 16)
                sp.dma_start(ct[:, 1 - u, :], t["ctxT"][i + 3]).then_inc(ct_in[1 - u], 16)
            if attend:
                sp.wait_ge(loaded["x"], 16)
                sp.wait_ge(w_hi, i)
                sp.wait_ge(w_lo, i)
                sp.dma_start(w2_halves[i - 1], w2_out[:]).then_inc(w_stored, 16)
            if find:
                sp.dma_start(w_in[:], t["w12"][i]).then_inc(w_loaded, 16)
            if project:
                w = 1 - u
                if not isinstance(i, int) or i >= 1:
                    for k in range(HALVES):
                        sp.wait_ge(stacked[k][w], in_stack(i - 1, w))
                sp.wait_ge(q_hi, i + 2)
                for r in (0, 1):
                    sp.dma_start(spill[w, r, :, :, T:ROW], qh[:, w]).then_inc(spilled[w], 16)
                sp.wait_ge(q_lo, i + 2)
                sp.dma_start(spill[w, 2, :, :, T:ROW], ql[:, w]).then_inc(spilled[w], 16)
                for k in range(HALVES):
                    sp.wait_ge(k_hi[k], i + 2)
                for r in (0, 2):
                    sp.dma_start(spill[w, r, :, :, 0:T], kh[:, w]).then_inc(spilled[w], 16)
                if attend:
                    sp.wait_ge(b_scored[SLOTS // 2 - 1], i)
                for k in range(HALVES):
                    sp.wait_ge(k_lo[k], i + 2)
                sp.dma_start(spill[w, 1, :, :, 0:T], kl[:, w]).then_inc(spilled[w], 16)
                sp.wait_ge(spilled[w], in_spill(i + 1, w))
                for k in range(HALVES):
                    if attend and k == 1:
                        sp.wait_ge(b_scored[SLOTS - 1], i)
                    for r in range(3):
                        sp.dma_start(stack[32 * r:32 * r + 32, w, PAIRS // 2 * k:PAIRS // 2 * (k + 1), :],
                                     spill_read[w][r][k]).then_inc(stacked[k][w], 16)

            if norm:
                w = 1 - u
                sp.wait_ge(loaded["x"], 16)
                sp.wait_ge(n_made, i - 2)
                sp.dma_start(xn2_dram[i - 3], xn2[:, w, :]).then_inc(n_stored[w], 16)
                sp.wait_ge(n_hi, i - 2)
                sp.wait_ge(n_lo, i - 2)
                sp.dma_start(row_tiles[i - 3], xhl[:, w, :]).then_inc(r_stored[w], 16)

        sp.wait_ge(prep_act, 3)
        split_steps(sp, step)
        for u in range(2):
            sp.wait_ge(n_stored[u], 8 * B)
            sp.wait_ge(r_stored[u], 8 * B)
        sp.wait_ge(w_stored, 16 * B)

    @block.gpsimd
    def _(pool):
        nc.gpsimd.memset(ones, 1.0).then_inc(prep_act, 1)
        nc.gpsimd.memset(minus_half[:], -0.5).then_inc(prep_act, 1)
        nc.gpsimd.memset(vt[:], 1.0).then_inc(prep_act, 1)

        def root1(k):
            lo, hi = PREPARED[k], PREPARED[k + 1]
            pool.wait_ge(varied1, k + 1)
            nc.gpsimd.tensor_tensor(rstd1[:, lo:hi, 0], ve1[:, lo:hi, 0], minus_half[:].to_broadcast([S, hi - lo]),
                                    ALU.pow).then_inc(rooted1, 1)

        pool.wait_ge(prep_act, 3)
        root1(0)
        pool.wait_ge(ready, 1)

        def split_context(b, u):
            pool.wait_ge(ct_hi, b + 1)
            if not isinstance(b, int) or b >= 2:
                pool.wait_ge(done["V2"], b - 1)
            nc.gpsimd.tensor_tensor(ctl[:, u, :, :].rearrange("p a t -> p (a t)"), ct[:, u, :],
                                    cth[:, u, :, :].rearrange("p a t -> p (a t)"), ALU.subtract).then_inc(ct_lo, 1)

        split_context(0, 0)

        def step(i, u, project, find, attend, output, norm, split_next, load_next):
            if project:
                w = 1 - u
                pool.wait_ge(q_biased, i + 2)
                reached(pool, q_lo, i + 1)
                f, fn, g = "p a r s -> p (a r s)", "p a n -> p (a n)", "p a r s -> p (a r) s"
                keep4 = keep[:].unsqueeze(1).to_broadcast([P, 4, S])
                nc.gpsimd.tensor_tensor(qm[:].rearrange(g), qf[:].rearrange(g), keep4,
                                        ALU.mult).then_inc(q_kept, 1)
                if not isinstance(i, int) or i >= 1:
                    pool.wait_ge(spilled[w], in_spill(i - 1, w))
                nc.gpsimd.tensor_tensor(qh[:, w].rearrange("p a (r s) -> p (a r) s", r=2), qf[:].rearrange(g), keep4,
                                        ALU.mult).then_inc(q_hi, 1)
                pool.wait_ge(q_kept, i + 2)
                pool.wait_ge(q_hi, i + 2)
                nc.gpsimd.tensor_tensor(ql[:, w].rearrange(fn), qm[:].rearrange(f), qh[:, w].rearrange(fn),
                                        ALU.subtract).then_inc(q_lo, 1)
            if norm:
                pool.wait_ge(varied, i - 2)
                nc.gpsimd.tensor_tensor(root0[:], ve[:], minus_half[:], ALU.pow).then_inc(rooted, 1)
            if output:
                if isinstance(i, int) and i == 2:
                    pool.wait_ge(bo_set, 1)
                nc.gpsimd.tensor_tensor(X[:, i - 2, :], X[:, i - 2, :], bo_all[:], ALU.add).then_inc(xb_out, 1)
            if norm:
                w = 1 - u
                pool.wait_ge(n_hi, i - 2)
                nc.gpsimd.tensor_tensor(xhl[:, w, D:2 * D], xn2[:, w, :], xhl[:, w, 0:D],
                                        ALU.subtract).then_inc(n_lo, 1)
            if isinstance(i, int) and i == -1:
                split_context(1, 1)
            if split_next:
                if not isinstance(i, int) or i >= 0:
                    split_context(i + 2, u)
            if isinstance(i, int) and i in (-1, 0):
                root1(i + 2)

        split_steps(pool, step)

    @block.scalar
    def _(act):
        act.wait_ge(ready, 1)

        def split_context(b, u):
            act.wait_ge(ct_in[u], (b // 2 + 1) * 16 if isinstance(b, int) else (b - u) * 8 + 16)
            if not isinstance(b, int) or b >= 2:
                act.wait_ge(done["V2"], b - 1)
            nc.scalar.copy(cth[:, u, :, :].rearrange("p a t -> p (a t)"), ct[:, u, :]).then_inc(ct_hi, 1)

        split_context(0, 0)

        def step(i, u, project, find, attend, output, norm, split_next, load_next):
            w = 1 - u
            for n in range(SLOTS + 1):
                if attend and n < SLOTS:
                    act.wait_ge(b_scored[n], i)
                    if n >= 4:
                        act.wait_ge(b_pv[n - 4], i)
                    elif not isinstance(i, int) or i >= 2:
                        act.wait_ge(b_pv[n + SLOTS - 4], i - 1)
                    nc.scalar.activation(pt[0:KC, n % 4, :], sbk[n % 3][0:KC, 0:HG * S], ACT.Exp,
                                         scale=SCORE_SCALE).then_inc(b_exp[n], 1)
                if n == 11 and norm:
                    act.wait_ge(done["X2"], i - 2)
                    reached(act, done["LG"], i - 3)
                    nc.scalar.copy(xt2[:].rearrange("p q s -> p (q s)"), turned2).then_inc(xt2_out, 1)
                if n == 7 and find:
                    act.wait_ge(w_loaded, 16 * i + 16)
                    nc.scalar.mul(w1h[:, i, :], w_in[:, 0, :], WE)
                    reached(act, w_stored, 16 * i)
                    nc.scalar.mul(w2_out[:, 0, :], w_in[:, 1, :], WE).then_inc(w_hi, 1)
                if n == 0 and project:
                    act.wait_ge(done["xT"], i + 2)
                    reached(act, done["Q"], i + 1)
                    nc.scalar.copy(xth[:].rearrange("p a s -> p (a s)"),
                                   bank["xT"][:, 0:HALVES * S]).then_inc(xt_hi, 1)
                if n == 2 and project:
                    act.wait_ge(done["Q"], i + 2)
                    reached(act, q_hi, i + 1)
                    for half in range(HALVES):
                        for r in range(2):
                            last = nc.scalar.activation(qf[:, half, r, :], bank["Q"][:, half * S:(half + 1) * S],
                                                        ACT.Identity, scale=parity[:, r:r + 1],
                                                        bias=bq_par[:, half, r:r + 1])
                    last.then_inc(q_biased, 1)
                if n in (3, 4) and project:
                    half = n - 3
                    act.wait_ge(done[f"K{half}"], i + 2)
                    if not isinstance(i, int) or i >= 1:
                        act.wait_ge(spilled[w], in_spill(i - 1, w))
                    nc.scalar.activation(kh[:, w, half, :], bank[f"K{half}"][:, 0:T], ACT.Identity,
                                         bias=bqk16[:, 1, half:half + 1]).then_inc(k_hi[half], 1)
                if n == 5 and output:
                    act.wait_ge(done["AT"], i - 1)
                    if not isinstance(i, int) or i >= 3:
                        act.wait_ge(done["WO"], i - 2)
                    nc.scalar.copy(att[:].rearrange("p a s -> p (a s)"),
                                   bank["AT"][:, 0:HALVES * S]).then_inc(att_out, 1)
                if n == 6 and find:
                    act.wait_ge(done["V01"], i + 1)
                    if not isinstance(i, int) or i >= 2:
                        act.wait_ge(b_pv[SLOTS - 1], i - 1)
                    nc.scalar.activation(vt[:, u, 0:2, :, 0:DH],
                                         bank["V01"][0:KC, :].rearrange("p (c h d) -> p c h d", c=2, h=H),
                                         ACT.Copy, scale=1.0 / WS).then_inc(v_out[0], 1)
                if n == 8 and find:
                    act.wait_ge(done["V2"], i + 1)
                    nc.scalar.activation(vt[:, u, 2, :, 0:DH],
                                         bank["V2"][0:KC, 0:D].rearrange("p (h d) -> p h d", h=H),
                                         ACT.Copy, scale=1.0 / WS).then_inc(v_out[1], 1)
                if n == 9 and find:
                    act.wait_ge(done["MT"], i + 1)
                    reached(act, top_in, i * 16)
                    nc.scalar.mul(neg_top[:], bank["MT"][0:H, 0:S].unsqueeze(1).to_broadcast([H, CH, S]), -1.0).then_inc(top_out, 1)
                    act.wait_ge(top_out, i + 1)
                    if not isinstance(i, int) or i >= 2:
                        act.wait_ge(b_scored[SLOTS - 1], i - 1)
                    act.dma_start(mb[KC:KC + 1, u].rearrange("o h c s -> o h (c s)"),
                                  neg_top[:].rearrange("h c s -> h (c s)")).then_inc(top_in, 16)
                if n == SLOTS and attend:
                    act.wait_ge(b_pv[SLOTS - 1], i)
                    reached(act, done["OT"], i - 1)
                    nc.scalar.copy(ots[:], ot[:, 0:GROUPS * S]).then_inc(ot_out, 1)
                if n == SLOTS and isinstance(i, int) and i == -1:
                    split_context(1, 1)
                if n == SLOTS and split_next and (not isinstance(i, int) or i >= 0):
                    split_context(i + 2, u)

        split_steps(act, step)

    @block.vector
    def _(dve):
        count = [0]

        def tick(instruction):
            count[0] += 1
            instruction.then_inc(prep, 1)
            dve.wait_ge(prep, count[0])

        V = nc.vector
        dve.wait_ge(loaded["w"], 16)
        tick(V.tensor_scalar(wh[:], w32, WS, None, ALU.mult))
        tick(V.scalar_tensor_tensor(wl[:].rearrange("p w a d -> p (w a d)"), w32.rearrange("p w a d -> p (w a d)"),
                                    WS, wh[:].rearrange("p w a d -> p (w a d)"), ALU.mult, ALU.subtract))
        dve.wait_ge(loaded["small"], 16 * 4)
        tick(V.tensor_scalar(bqk16[:], bqk[:], WS, None, ALU.mult))
        for half in range(HALVES):
            tick(V.tensor_scalar(bq_par[:, half, :], parity[:], bqk16[:, 0, half:half + 1], None, ALU.mult))
        tick(V.tensor_scalar(mask_add[:], mask_q, 0.0, None, ALU.is_equal))
        tick(V.reduce_sum(n_masked[:], mask_add[:], AX.X))
        tick(V.tensor_scalar(keep_q[:], n_masked[:], float(T), None, ALU.is_lt))
        tick(V.tensor_scalar(mask_add[:], mask_add[:], keep_q[:], MASKED, ALU.mult, ALU.mult))
        dve.wait_ge(prep_act, 3)
        V.tensor_scalar(keep_diag, ident[0:S, 0:S], keep_q[:], None, ALU.mult).then_inc(diag, 1)

        def x_stats(k):
            lo, hi = PREPARED[k], PREPARED[k + 1]
            dve.wait_ge(loaded["x0" if k == 0 else "x"], 16)
            for b in range(lo, hi):
                last = V.bn_stats(stats1[:, b, :], X[:, b, :])
            tick(last)
            for b in range(lo, hi):
                last = V.bn_aggr(mv1[:, b, :], stats1[:, b, :])
            tick(last)
            V.tensor_scalar(ve1[:, lo:hi, 0], mv1[:, lo:hi, 1], LN1_EPS, None, ALU.add).then_inc(varied1, 1)

        def x_scales(k):
            here = slice(PREPARED[k], PREPARED[k + 1])
            r, s, v = rstd1[:, here, 0], shift1[:, here, 0], ve1[:, here, 0]
            dve.wait_ge(rooted1, k + 1)
            tick(V.tensor_tensor(s, r, r, ALU.mult))
            tick(V.tensor_tensor(s, s, v, ALU.mult))
            tick(V.tensor_scalar(s, s, -0.5, 1.5, ALU.mult, ALU.add))
            tick(V.tensor_tensor(r, r, s, ALU.mult))
            tick(V.scalar_tensor_tensor(s, mv1[:, here, 0], -1.0, r, ALU.mult, ALU.mult))

        x_stats(0)
        dve.wait_ge(prep_pe, 1)
        tick(V.tensor_copy(keep[:], pj[0][:, 0:S]))
        x_scales(0)

        def normalise(b, u):
            if not isinstance(b, int) or b >= 1:
                dve.wait_ge(done["xT"], b)
            V.tensor_scalar(xn[:], X[:, b, :], rstd1[:, b, :], shift1[:, b, :],
                            ALU.mult, ALU.add).then_inc(xn_made, 1)

        normalise(0, 0)
        V.memset(ot[:], 0.0).then_inc(ready, 1)

        def step(i, u, project, find, attend, output, norm, split_next, load_next):
            w = 1 - u
            if find:
                if not isinstance(i, int) or i >= 2:
                    dve.wait_ge(done["MT"], i - 1)
                dve.wait_ge(a_scored[0], i + 1)
            if norm:
                dve.wait_ge(st_out, i - 2)
                reached(dve, n_made, i - 3)
                V.tensor_copy(stats_now[:], stats2[:]).then_inc(st_taken, 1)
            for n in range(SLOTS):
                if n < 8 and find:
                    for h in (2 * n, 2 * n + 1):
                        dve.wait_ge(loaded["w"], 16)
                        dve.wait_ge(a_scored[h], i + 1)
                        V.tensor_tensor_reduce(sa[h % 2][0:S, 0:T], sa[h % 2][0:S, 0:T], mask_add[:], 1.0, -3.0e38,
                                               ALU.add, ALU.max, top[:, u, h:h + 1]).then_inc(a_top[h], 1)
                if n == 1 and output:
                    dve.wait_ge(done["OT"], i - 1)
                    o = bank["OT"][0:S, :].rearrange("p (h d) -> p h d", h=H)
                    V.reciprocal(rsum[:], o[:, :, DH:DV]).then_inc(rs_out, 1)
                    dve.wait_ge(rs_out, i - 1)
                    V.tensor_tensor(at[:], o[:, :, 0:DH], rsum[:].to_broadcast([S, H, DH]),
                                    ALU.mult).then_inc(at_out, 1)
                if n in (3, 4) and project:
                    half = n - 3
                    dve.wait_ge(k_hi[half], i + 2)
                    V.scalar_tensor_tensor(kl[:, w, half, :], bank[f"K{half}"][:, 0:T], bqk16[:, 1, half:half + 1],
                                           kh[:, w, half, :], ALU.add, ALU.subtract).then_inc(k_lo[half], 1)
                if n == 0 and project:
                    dve.wait_ge(done["xT"], i + 2)
                    dve.wait_ge(xt_hi, i + 2)
                    V.tensor_tensor(xtl[:].rearrange("p a s -> p (a s)"), bank["xT"][:, 0:HALVES * S],
                                    xth[:].rearrange("p a s -> p (a s)"), ALU.subtract).then_inc(xt_lo, 1)
                if n == 5 and norm:
                    dve.wait_ge(loaded["w"], 16)
                    dve.wait_ge(st_taken, i - 2)
                    reached(dve, n_made, i - 3)
                    V.bn_aggr(mv[:], stats_now[:]).then_inc(refined, 1)
                    dve.wait_ge(refined, (i - 3) * 5 + 1)
                    V.tensor_scalar(ve[:], mv[:, 1:2], LN2_EPS, None, ALU.add).then_inc(varied, 1)
                if n == 8 and norm:
                    dve.wait_ge(rooted, i - 2)
                    V.tensor_scalar(newton[:, 0:1], ve[:], root0[:], None, ALU.mult).then_inc(refined, 1)
                    dve.wait_ge(refined, (i - 3) * 5 + 2)
                    V.tensor_scalar(newton[:, 1:2], newton[:, 0:1], root0[:], -0.5, ALU.mult, ALU.mult).then_inc(refined, 1)
                    dve.wait_ge(refined, (i - 3) * 5 + 3)
                    if not isinstance(i, int) or i >= 4:
                        dve.wait_ge(n_made, i - 3)
                    V.tensor_scalar(rstd2[:], newton[:, 1:2], 1.5, root0[:], ALU.add, ALU.mult).then_inc(refined, 1)
                    dve.wait_ge(refined, (i - 3) * 5 + 4)
                    V.tensor_scalar(shift2[:], mv[:, 0:1], -1.0, rstd2[:], ALU.mult, ALU.mult).then_inc(refined, 1)
                    dve.wait_ge(refined, (i - 3) * 5 + 5)
                    if not isinstance(i, int) or i >= 5:
                        dve.wait_ge(n_stored[w], by_parity(i - 5, w))
                        dve.wait_ge(r_stored[w], by_parity(i - 5, w))
                        dve.wait_ge(n_lo, i - 4)
                        dve.wait_ge(done["X2"], i - 4)
                    V.tensor_scalar(xn2[:, w, :], X[:, i - 3, :], rstd2[:], shift2[:], ALU.mult, ALU.add).then_inc(n_made, 1)
                    dve.wait_ge(n_made, i - 2)
                    V.tensor_copy(xhl[:, w, 0:D], xn2[:, w, :]).then_inc(n_hi, 1)
                if n == 9 and find:
                    dve.wait_ge(w_hi, i + 1)
                    V.scalar_tensor_tensor(w1l[:, i, :], w_in[:, 0, :], WE, w1h[:, i, :], ALU.mult, ALU.subtract)
                    V.scalar_tensor_tensor(w2_out[:, 1, :], w_in[:, 1, :], WE, w2_out[:, 0, :], ALU.mult,
                                           ALU.subtract).then_inc(w_lo, 1)
                if n == 11 and norm and (not isinstance(i, int) or i >= 4):
                    dve.wait_ge(done["LG"], i - 3)
                    V.scalar_tensor_tensor(L[:, i - 4, :], logits_out, 1.0 / WE, rb[:],
                                           ALU.mult, ALU.add).then_inc(lg_out, 1)
                if n == WO_AT and output:
                    dve.wait_ge(done["WO"], i - 1)
                    dve.wait_ge(xb_out, i - 1)
                    V.tensor_tensor(X[:, i - 2, :], bank["WO"][0:S, 0:D], X[:, i - 2, :], ALU.add).then_inc(x2_out, 1)
                    dve.wait_ge(loaded["w"], 16)
                    dve.wait_ge(x2_out, i - 1)
                    reached(dve, st_taken, i - 2)
                    V.bn_stats(stats2[:], X[:, i - 2, :]).then_inc(st_out, 1)
                if n == 9 and isinstance(i, int) and i == -1:
                    normalise(1, 1)
                    dve.wait_ge(loaded["mask_k"], 32)
                    tick(V.tensor_copy(sel[:], sel32))
                    tick(V.tensor_scalar(mk32, mask_k, 0.0, MASKED, ALU.is_equal, ALU.mult))
                    tick(V.tensor_tensor(mk32, mk32, keep[0:KC, :].unsqueeze(1).to_broadcast([KC, CH, S]), ALU.mult))
                    for k in range(2):
                        V.tensor_copy(mb[0:KC, k].rearrange("p h c s -> p h (c s)"),
                                      mk32.rearrange("p c s -> p (c s)").unsqueeze(1).to_broadcast(
                                          [KC, H, CH * S])).then_inc(mb_set, 1)
                    x_stats(1)
                if n == 11 and isinstance(i, int) and i == 0:
                    x_scales(1)
                    dve.wait_ge(prep_pe, 2)
                    V.tensor_copy(bo_all[:], sbk[2][0:S, 0:D]).then_inc(bo_set, 1)
                    tick(V.tensor_copy(ident16[:], ident[0:S, 0:S]))
                    tick(V.tensor_scalar(rw[:, 0, :], rw32[:], WE, None, ALU.mult))
                    V.scalar_tensor_tensor(rw[:, 1, :], rw32[:], WE, rw[:, 0, :], ALU.mult,
                                           ALU.subtract).then_inc(router_set, 1)
                    x_stats(2)
                if n == 11 and isinstance(i, int) and i == 1:
                    x_scales(2)
                if n == 9 and split_next and (not isinstance(i, int) or i >= 0):
                    normalise(i + 2, u)

        split_steps(dve, step)
        dve.wait_ge(done["LG"], B)
        V.scalar_tensor_tensor(L[:, B - 1, :], logits_out, 1.0 / WE, rb[:], ALU.mult, ALU.add).then_inc(lg_out, 1)
        dve.wait_ge(lg_out, B)

    @block.tensor
    def _(pe):
        MM = nc.tensor.matmul
        pe.wait_ge(diag, 1)
        pe.wait_ge(prep_act, 3)
        MM(pj[0][:, 0:S], ones, keep_diag, start=True, stop=True).then_inc(prep_pe, 1)

        def output_bias():
            pe.wait_ge(loaded["wo"], 16 * 5)
            MM(sbk[2][0:S, 0:D], ones[0:1, 0:S], bo_row[:], start=True, stop=False)
            for a in range(HALVES):
                last = MM(sbk[2][0:S, 0:D], bv[:, a:a + 1].to_broadcast([P, S]), wo[:, a, :], start=False,
                          stop=(a == HALVES - 1))
            last.then_inc(prep_pe, 1)

        pe.wait_ge(ready, 1)

        def project3(out, lhs, rhs):
            for a in range(HALVES):
                (lh, ll), (rh, rl) = lhs(a), rhs(a)
                MM(out, lh, rh, start=(a == 0), stop=False)
                MM(out, lh, rl, start=False, stop=False)
                last = MM(out, ll, rh, start=False, stop=(a == HALVES - 1))
            return last

        def step(i, u, project, find, attend, output, norm, split_next, load_next):
            w = 1 - u
            later = not isinstance(i, int)

            def bank_free(job):
                users = {"xT": (project, [(xt_hi, i + 2), (xt_lo, i + 2)]), "OT": (output, [(at_out, i - 1)]),
                         "Q": (project, [(q_biased, i + 2)]), "K0": (project, [(k_hi[0], i + 2), (k_lo[0], i + 2)]),
                         "K1": (project, [(k_hi[1], i + 2), (k_lo[1], i + 2)]), "AT": (output, [(att_out, i - 1)]),
                         "V01": (find, [(v_out[0], i + 1)]), "V2": (find, [(v_out[1], i + 1)]),
                         "MT": (find, [(top_out, i + 1)]), "WO": (output, [(x2_out, i - 1)])}
                n = JOBS.index(job)
                for m in range(n - 2, -1, -2):
                    runs, emptied = users[JOBS[m]]
                    if runs:
                        for s, c in emptied:
                            pe.wait_ge(s, c)
                        return
                if n % 2 == 0:
                    reached(pe, top_out, i if later else min(i, B))
                    if not later and i == 0:
                        pe.wait_ge(k_hi[1], 1)
                        pe.wait_ge(k_lo[1], 1)
                else:
                    reached(pe, x2_out, i - 2 if later else min(i - 2, B))
                    reached(pe, v_out[1], i if later else min(i, B))
                    if not later and i == 0:
                        pe.wait_ge(k_hi[0], 1)
                        pe.wait_ge(k_lo[0], 1)

            def find_max(h):
                if h % (H // 2) == 0:
                    pe.wait_ge(stacked[2 * h // H][u], in_stack(i, u))
                if h >= 2:
                    pe.wait_ge(a_top[h - 2], i + 1)
                elif later or i >= 1:
                    pe.wait_ge(a_top[h + H - 2], i)
                    reached(pe, xt2_out if h == 0 else lg_out, i - 3 if h == 0 else i - 4)
                q = (h % 2) * S
                MM(sa[h % 2][0:S, 0:T], stack[:, u, h // 2, T + q:T + q + S], stack[:, u, h // 2, 0:T],
                   start=True, stop=True).then_inc(a_scored[h], 1)

            def attend_scores(n):
                g, c = divmod(n, CH)
                if n >= 3:
                    pe.wait_ge(b_exp[n - 3], i)
                elif later or i >= 2:
                    pe.wait_ge(b_exp[n + SLOTS - 3], i - 1)
                if n == 0:
                    pe.wait_ge(top_in, 16 * i)
                MM(sbk[n % 3][:, 0:HG * S].rearrange("p (h s) -> p h s", h=HG), sel[:], mb[:, w, g * HG:(g + 1) * HG, c, :],
                   start=True, stop=False)
                for q in range(2):
                    last = MM(sbk[n % 3][:, 2 * S * q:2 * S * (q + 1)], stack[:, w, 2 * g + q, KC * c:KC * c + P],
                              stack[:, w, 2 * g + q, T:ROW], start=False, stop=(q == 1))
                last.then_inc(b_scored[n], 1)

            def attend_values(n):
                g, c = divmod(n, CH)
                pe.wait_ge(b_exp[n], i)
                if n == 0:
                    pe.wait_ge(v_out[1], i)
                    reached(pe, ot_out, i - 1)
                for j in range(HG):
                    last = MM(ot[32 * j:32 * j + DV, g * S:(g + 1) * S], vt[:, w, c, HG * g + j, :],
                              pt[0:KC, n % 4, j * S:(j + 1) * S], start=(c == 0), stop=(c == CH - 1),
                              tile_position=(0, 32 * j))
                last.then_inc(b_pv[n], 1)

            def job(name):
                out = bank[name]
                if name == "xT" and project:
                    pe.wait_ge(xn_made, i + 2)
                    bank_free(name)
                    for a in range(HALVES):
                        last = nc.tensor.transpose(out[:, a * S:(a + 1) * S], xn[:, a * P:(a + 1) * P],
                                                   ident[0:S, 0:S])
                elif name == "OT" and output:
                    pe.wait_ge(ot_out, i - 1)
                    bank_free(name)
                    for g in range(GROUPS):
                        last = nc.tensor.transpose(out[0:S, g * P:(g + 1) * P], ots[:, g * S:(g + 1) * S], ident[:])
                elif name == "Q" and project:
                    pe.wait_ge(xt_lo, i + 2)
                    bank_free(name)
                    for m in range(HALVES):
                        last = project3(out[:, m * S:(m + 1) * S],
                                        lambda a: (wh[:, 0, a, m * P:(m + 1) * P], wl[:, 0, a, m * P:(m + 1) * P]),
                                        lambda a: (xth[:, a, :], xtl[:, a, :]))
                elif name in ("K0", "K1") and project:
                    m = int(name[1])
                    if m == 0:
                        pe.wait_ge(ct_lo, i + 2)
                    bank_free(name)
                    last = project3(out[:, 0:T],
                                    lambda a: (wh[:, 1, a, m * P:(m + 1) * P], wl[:, 1, a, m * P:(m + 1) * P]),
                                    lambda a: (cth[:, w, a, :], ctl[:, w, a, :]))
                elif name == "AT" and output:
                    pe.wait_ge(at_out, i - 1)
                    bank_free(name)
                    flat = at[:].rearrange("p h d -> p (h d)")
                    for a in range(HALVES):
                        last = nc.tensor.transpose(out[:, a * S:(a + 1) * S], flat[:, a * P:(a + 1) * P],
                                                   ident[0:S, 0:S])
                elif name in ("V01", "V2") and find:
                    bank_free(name)
                    for c in ((0, 1) if name == "V01" else (2,)):
                        last = project3(out[0:KC, (c % 2) * D:(c % 2 + 1) * D],
                                        lambda a: (cth[:, u, a, c * KC:(c + 1) * KC], ctl[:, u, a, c * KC:(c + 1) * KC]),
                                        lambda a: (wh[:, 2, a, :], wl[:, 2, a, :]))
                elif name == "MT" and find:
                    pe.wait_ge(a_top[H - 1], i + 1)
                    bank_free(name)
                    last = nc.tensor.transpose(out[0:H, 0:S], top[:, u, :], ident[0:S, 0:S])
                elif name == "WO" and output:
                    pe.wait_ge(att_out, i - 1)
                    bank_free(name)
                    for a in range(HALVES):
                        last = MM(out[0:S, 0:D], att[:, a, :], wo[:, a, :], start=(a == 0), stop=(a == HALVES - 1))
                else:
                    return
                last.then_inc(done[name], 1)

            if not later and i == 1:
                pe.wait_ge(mb_set, 2)
                pe.wait_ge(bo_set, 1)
            if not later and i == 3:
                pe.wait_ge(router_set, 1)
            for n in range(SLOTS + 2):
                if attend and n < SLOTS:
                    attend_scores(n)
                if find and n < 8:
                    find_max(2 * n)
                if attend and n >= 2:
                    attend_values(n - 2)
                if find and n < 8:
                    find_max(2 * n + 1)
                for name in JOBS:
                    if JOB_AT[name] == n:
                        job(name)
                if n == LG_AT and norm and (later or i >= 4):
                    if find:
                        pe.wait_ge(a_top[H - 1], i + 1)
                    logits(i - 4)
                if n == X2_AT and norm:
                    pe.wait_ge(n_lo, i - 2)
                    reached(pe, xt2_out, i - 3)
                    if find:
                        pe.wait_ge(a_top[H - 2], i + 1)
                    for q in range(2 * HALVES):
                        last = nc.tensor.transpose(turned2[:, q * S:(q + 1) * S], xhl[:, w, q * P:(q + 1) * P], ident16[:])
                    last.then_inc(done["X2"], 1)
            if not later and i == 0:
                output_bias()

        def logits(b):
            pe.wait_ge(xt2_out, b + 1)
            reached(pe, lg_out, b)
            project3(logits_out, lambda a: (xt2[:, a, :], xt2[:, HALVES + a, :]),
                     lambda a: (rw[:, 0, a * E:(a + 1) * E], rw[:, 1, a * E:(a + 1) * E])).then_inc(done["LG"], 1)

        split_steps(pe, step)
        logits(B - 1)


TS = 256
NT = (2 * B * S + E * (TS - 1)) // TS
NB = NT * TS // P
LN3_EPS = 1e-12
WIDTHS = (S, E, P, B, NB, NT * E)


def route_block(nc, sems, ctx, t, keep, rows, w2_halves):
    sb = lambda name, shape, dt: ctx.enter_context(nc.sbuf_tensor(name, shape, dt))
    ps = lambda name, shape, dt: ctx.enter_context(nc.psum_tensor(name, shape, dt))
    sem = sems.new
    L, cw, tile_expert, take, put = (keep[k] for k in ("logits", "cw", "tile_expert", "take", "put"))

    fixed = sb("fixed", [P, sum(WIDTHS)], F32)
    before32, falling, counting, value, spare, tile_start = (
        fixed[:, sum(WIDTHS[:k]):sum(WIDTHS[:k + 1])] for k in range(len(WIDTHS)))
    before32, falling, counting, value = before32[0:S], falling[0:S], counting[0:S], value[0:S]
    tile_start = tile_start[0:1].rearrange("p (n e) -> p n e", e=E)
    before = sb("before", [S, S], BF16)
    all_ones = sb("all_ones", [S, S], BF16)
    pick = [sb(f"pick{k}", [S, B, E], F32) for k in range(2)]
    key = sb("key", [S, B, E], F32)
    m = [sb(f"m{k}", [S, B, 1], F32) for k in range(2)]
    first = sb("first", [S, B, 1], F32)
    both = sb("both", [S, B, E], BF16)
    count = [sb(f"count{k}", [S, B, E], F32) for k in range(2)]
    size = [sb(f"size{k}", [S, E], F32) for k in range(3)]
    whole = sb("whole", [S, E], I32)
    whole2 = sb("whole2", [S, E], I32)
    past_n = sb("past_n", [1, NT, 1], F32)
    slot = sb("slot", [S, 2, B], F32)
    slot_i = sb("slot_i", [S, 2, B], I32)
    block_i = sb("block_i", [S, 2, B], I32)
    slot_block = sb("slot_block", [S, 2, B], F32)
    slot_row = sb("slot_row", [S, 2, B], F32)
    is_row = sb("is_row", [S, 2, B, P], F16)
    in_block = sb("in_block", [S, 2, B, NB], F16)
    code = sb("code", [P, 4 * NB], F32)
    code_i = sb("code_i", [P, 4 * NB], I32)
    batch_i = sb("batch_i", [P, 4 * NB], I32)
    batch = sb("batch", [P, 4 * NB], F32)
    found = [sb(f"found{k}", [P, NB], F32) for k in range(2)]
    place = sb("place", [P, NB], F32)
    zeros = sb("zeros", [1, 2 * D], F16)

    rank, total = ps("rank", [P, 512], F32), ps("total", [P, 512], F32)
    lists = [[ps(f"lists{k}{half}", [P, 512], F32) for half in range(2)] for k in range(2)]

    loaded, w2_in, ones_set = sem("r_loaded"), sem("w2_in"), sem("ones_set")
    steps, gap, expd, picked, ranked = (sem("r_" + n) for n in ("steps", "gap", "expd", "picked", "ranked"))
    slots_made = sem("slots_made")
    block_marked, row_marked, coded = sem("block_marked"), sem("row_marked"), sem("coded")
    listed, zero_row = sem("listed"), sem("zero_row")

    block = ctx.enter_context(nc.Block())

    @block.sync
    def _(sp):
        sp.dma_start(fixed[:], t["fixed"]).then_inc(loaded, 16)
        for n, name in enumerate(("w2h", "w2l")):
            for q in range(4):
                flat = keep[name][:].rearrange("p e f d -> p (e f d)").rearrange("p (q n) -> p q n", q=4)
                sp.dma_start(flat[:, q, :], w2_halves[n].rearrange("p (q b) n -> q p (b n)", q=4)[q]).then_inc(w2_in, 16)
        sp.wait_ge(ones_set, 2)
        sp.dma_start(rows[0:1, :], zeros[:]).then_inc(zero_row, 16)
        sp.wait_ge(zero_row, 16)
        sp.wait_ge(w2_in, 16 * 8)

    @block.gpsimd
    def _(pool):
        nc.gpsimd.memset(all_ones[:], 1.0).then_inc(ones_set, 1)
        nc.gpsimd.memset(zeros[:], 0.0).then_inc(ones_set, 1)
        pool.wait_ge(loaded, 16)
        for k in range(2):
            pool.wait_ge(block_marked, k + 1)
            nc.gpsimd.tensor_tensor(in_block[:, k], in_block[:, k], value.unsqueeze(2).to_broadcast([S, B, NB]),
                                    ALU.mult).then_inc(coded, 1)

    @block.scalar
    def _(act):
        act.wait_ge(gap, 1)
        nc.scalar.activation(m[1][:], m[1][:], ACT.Exp).then_inc(expd, 1)

    @block.tensor
    def _(pe):
        MM = nc.tensor.matmul
        pe.wait_ge(ones_set, 2)
        pe.wait_ge(picked, 1)
        MM(rank[0:S, 0:B * E], before[:], both[:].rearrange("p b e -> p (b e)"), start=True, stop=True)
        MM(total[0:S, 0:B * E], all_ones[:], both[:].rearrange("p b e -> p (b e)"), start=True,
           stop=True).then_inc(ranked, 1)
        for k in range(2):
            pe.wait_ge(row_marked, k + 1)
            pe.wait_ge(coded, k + 1)
            for b in range(B):
                half, n = divmod(b, B // 2)
                last = MM(lists[k][half][:, 0:NB], is_row[:, k, b, :], in_block[:, k, b, :], start=(n == 0),
                          stop=(n == B // 2 - 1))
            last.then_inc(listed, 1)

    @block.vector
    def _(dve):
        V = nc.vector
        done = [0]

        def tick(instruction):
            done[0] += 1
            instruction.then_inc(steps, 1)
            dve.wait_ge(steps, done[0])

        dve.wait_ge(loaded, 16)
        tick(V.tensor_copy(before[:], before32))
        wide = lambda a: a.to_broadcast([S, B, E])
        for k in range(2):
            tick(V.tensor_reduce(m[k][:], L[:], AX.X, ALU.max))
            tick(V.tensor_tensor(key[:], L[:], wide(m[k][:]), ALU.is_equal))
            tick(V.tensor_tensor(key[:], key[:], falling.unsqueeze(1).to_broadcast([S, B, E]), ALU.mult))
            tick(V.tensor_reduce(first[:], key[:], AX.X, ALU.max))
            tick(V.tensor_tensor(pick[k][:], key[:], wide(first[:]), ALU.is_equal))
            if k == 0:
                tick(V.scalar_tensor_tensor(L[:], pick[0][:], -3.0e38, L[:], ALU.mult, ALU.add))
        V.tensor_tensor(both[:], pick[0][:], pick[1][:], ALU.add).then_inc(picked, 1)
        V.tensor_tensor(m[1][:], m[1][:], m[0][:], ALU.subtract).then_inc(gap, 1)
        dve.wait_ge(ranked, 1)
        tick(V.tensor_copy(count[0][:].rearrange("p b e -> p (b e)"), total[0:S, 0:B * E]))
        at, s = 0, 1
        while s < B:
            V.tensor_copy(count[1 - at][:, 0:s, :], count[at][:, 0:s, :])
            tick(V.tensor_tensor(count[1 - at][:, s:B, :], count[at][:, s:B, :], count[at][:, 0:B - s, :], ALU.add))
            at, s = 1 - at, 2 * s
        tick(V.tensor_scalar(size[0][:], count[at][:, B - 1, :], float(TS - 1), None, ALU.add))
        shift_bits = TS.bit_length() - 1
        tick(V.tensor_copy(whole[:], size[0][:]))
        tick(V.tensor_single_scalar(whole2[:], whole[:], shift_bits, ALU.arith_shift_right))
        tick(V.tensor_copy(size[0][:], whole2[:]))
        tick(V.tensor_scalar(size[0][:], size[0][:], float(TS), None, ALU.mult))
        tick(V.tensor_copy(size[1][:], size[0][:]))
        e_at, s = 1, 1
        while s < E:
            V.tensor_copy(size[3 - e_at][:, 0:s], size[e_at][:, 0:s])
            tick(V.tensor_tensor(size[3 - e_at][:, s:E], size[e_at][:, s:E], size[e_at][:, 0:E - s], ALU.add))
            e_at, s = 3 - e_at, 2 * s
        ends, start = size[e_at], size[0]
        tick(V.tensor_tensor(start[:], ends[:], start[:], ALU.subtract))
        pos = count[at]
        flat = lambda a: a[:].rearrange("p b e -> p (b e)")
        tick(V.tensor_tensor(flat(pos), flat(pos), total[0:S, 0:B * E], ALU.subtract))
        tick(V.tensor_tensor(flat(pos), flat(pos), rank[0:S, 0:B * E], ALU.add))
        tick(V.tensor_tensor(pos[:], pos[:], start[:].unsqueeze(1).to_broadcast([S, B, E]), ALU.add))
        for k in range(2):
            tick(V.tensor_tensor(key[:], pick[k][:], pos[:], ALU.mult))
            tick(V.tensor_reduce(slot[:, k, :].unsqueeze(2), key[:], AX.X, ALU.add))
        tick(V.tensor_copy(slot_i[:], slot[:]))
        tick(V.tensor_single_scalar(block_i[:], slot_i[:], P.bit_length() - 1, ALU.arith_shift_right))
        tick(V.tensor_copy(slot_block[:], block_i[:]))
        V.scalar_tensor_tensor(slot_row[:], slot_block[:], -float(P), slot[:], ALU.mult, ALU.add).then_inc(slots_made, 1)
        dve.wait_ge(slots_made, 1)
        wide_to = lambda a, n: a.unsqueeze(2).to_broadcast([S, B, n])
        for k in range(2):
            V.tensor_tensor(in_block[:, k], counting[:, 0:NB].unsqueeze(1).to_broadcast([S, B, NB]),
                            wide_to(slot_block[:, k, :], NB), ALU.is_equal).then_inc(block_marked, 1)
        for k in range(2):
            V.tensor_tensor(is_row[:, k], counting.unsqueeze(1).to_broadcast([S, B, P]),
                            wide_to(slot_row[:, k, :], P), ALU.is_equal).then_inc(row_marked, 1)
        tick(V.tensor_tensor(tile_start, tile_start, ends[0:1, :].unsqueeze(1).to_broadcast([1, NT, E]), ALU.is_ge))
        tick(V.tensor_reduce(past_n[:], tile_start, AX.X, ALU.add))
        tick(V.tensor_scalar(past_n[:], past_n[:], float(E - 1), None, ALU.min))
        tick(V.tensor_copy(tile_expert[:], past_n[:].rearrange("p n o -> p (n o)")))
        dve.wait_ge(expd, 1)
        w = [cw[:, k, :].unsqueeze(2) for k in range(2)]
        tick(V.tensor_scalar(w[0], m[1][:], 1.0, None, ALU.add))
        tick(V.reciprocal(w[0], w[0]))
        tick(V.tensor_tensor(w[1], m[1][:], w[0], ALU.mult))
        dve.wait_ge(listed, 2)
        for k in range(2):
            for half in range(2):
                q = 2 * k + half
                last = V.tensor_copy(code[:, q * NB:(q + 1) * NB], lists[k][half][:, 0:NB])
        tick(last)
        tick(V.tensor_copy(code_i[:], code[:]))
        tick(V.tensor_single_scalar(batch_i[:], code_i[:], P.bit_length() - 1, ALU.arith_shift_right))
        tick(V.tensor_copy(batch[:], batch_i[:]))
        tick(V.scalar_tensor_tensor(batch[:], batch[:], -float(P - S), code[:], ALU.mult, ALU.add))
        tick(V.tensor_scalar(code[:], code[:], 0.0, float(B // 2 * S), ALU.is_gt, ALU.mult))
        for k in range(2):
            first_half, second_half = (batch[:, (2 * k + h) * NB:(2 * k + h + 1) * NB] for h in range(2))
            tick(V.tensor_tensor(found[k][:], first_half, second_half, ALU.add))
            tick(V.tensor_tensor(found[k][:], found[k][:], code[:, (2 * k + 1) * NB:(2 * k + 2) * NB], ALU.add))
        tick(V.tensor_scalar(place[:], found[1][:], 0.0, float(B * S), ALU.is_gt, ALU.mult))
        tick(V.tensor_tensor(found[0][:], found[0][:], found[1][:], ALU.add))
        tick(V.tensor_copy(take[:], found[0][:]))
        tick(V.tensor_single_scalar(found[1][:], found[0][:], 0.0, ALU.is_equal))
        tick(V.tensor_tensor(found[1][:], found[1][:], spare, ALU.mult))
        tick(V.tensor_tensor(place[:], place[:], found[1][:], ALU.add))
        tick(V.tensor_tensor(place[:], place[:], found[0][:], ALU.add))
        tick(V.tensor_copy(put[:], place[:]))


def expert_steps(eng, step):
    def edge(i):
        step(i, i % 2, 0 <= i < NT, 1 <= i, i + 1 < NT, i + 2 < NT)
    for i in (-1, 0, 1, 2):
        edge(i)
    pairs = (NT - 5) // 2
    with eng.Fori(0, pairs) as j:
        for u in range(2):
            step(j * 2 + (3 + u), 1 - u, True, True, True, True)
    for i in range(3 + 2 * pairs, NT + 1):
        edge(i)


def expert_block(nc, sems, ctx, t, keep, rows, y):
    sb = lambda name, shape, dt: ctx.enter_context(nc.sbuf_tensor(name, shape, dt))
    ps = lambda name, shape, dt: ctx.enter_context(nc.psum_tensor(name, shape, dt))
    sem = sems.new
    w1h, w1l, w2h, w2l = (keep[n] for n in ("w1h", "w1l", "w2h", "w2l"))
    tile_expert, take, put, X = (keep[n] for n in ("tile_expert", "take", "put", "X"))
    SUB = TS // P

    ident = sb("ident3f", [P, P], F32)
    ident16 = sb("ident16e", [P, P], F16)
    b1 = sb("b1", [P, E, FC], F32)
    b2 = sb("b2", [P, E, D], F32)
    ln_b = sb("ln_b", [S, D], F32)
    xr = sb("xr", [P, 2, SUB, 2 * D], F16)
    xt = sb("xt", [P, 2, 2 * HALVES, TS], F16)
    g = sb("g", [P, 2, 2 * TS], F32)
    hh = sb("hh", [P, 2, FC, TS], F16)
    hl = sb("hl", [P, 2, FC, TS], F16)
    ys = sb("ys", [P, 2, SUB, D], F32)
    take_now = sb("take_now", [P, 2, SUB], U32)
    put_now = sb("put_now", [P, 2, SUB], U32)

    tb = ps("tb", [P, 2 * HALVES * TS], F16)
    hb = [ps(f"hb{k}", [P, 512], F32) for k in range(3)]
    yb = [[ps(f"yb{u}{s}", [P, 512], F32) for s in range(SUB)] for u in range(2)]

    ident_in, loaded, ready, biased = sem("e_ident_in"), sem("e_loaded"), sem("e_ready"), sem("e_biased")
    rows_in = [sem(f"rows_in{u}") for u in range(2)]
    turned, moved = sem("e_turned"), sem("e_moved")
    FP = FC // 2
    h_done = [sem(f"h_done{k}") for k in range(FP)]
    h_gelu = [sem(f"h_gelu{k}") for k in range(FP)]
    h_hi = [sem(f"h_hi{k}") for k in range(FP)]
    h_lo = [sem(f"h_lo{k}") for k in range(FP)]
    y_done, y_out = sem("y_done"), sem("y_out")
    y_stored = [sem(f"y_stored{u}") for u in range(2)]
    take_first, take_set, put_set = sem("take_first"), sem("take_set"), sem("put_set")

    block = ctx.enter_context(nc.Block())

    def by_parity(b, u):
        return (b - u) * 8 * SUB + 16 * SUB

    def blocks(index, i):
        return index[:, i * SUB:(i + 1) * SUB] if isinstance(i, int) else index[:, bass.ds(i * SUB, SUB)]

    @block.sync
    def _(sp):
        sp.dma_start(ident[:], t["ident"]).then_inc(ident_in, 16)
        sp.dma_start(ln_b[:], t["ln_b"].to_broadcast([S, D])).then_inc(loaded, 16)
        sp.dma_start(b1[:], t["b1"]).then_inc(loaded, 16)
        sp.dma_start(b2[:].rearrange("p e d -> p (e d)"), t["b2"].to_broadcast([P, E * D])).then_inc(loaded, 16)

    @block.gpsimd
    def _(pool):
        def gather(i, u):
            if isinstance(i, int) and i < 2:
                nc.gpsimd.tensor_copy(take_now[:, u, :], blocks(take, i)).then_inc(take_first, 1)
                pool.wait_ge(take_first, i + 1)
            else:
                pool.wait_ge(turned, i - 1)
                nc.gpsimd.tensor_copy(take_now[:, u, :], blocks(take, i)).then_inc(take_set, 1)
                pool.wait_ge(loaded, 48)
                pool.wait_ge(take_set, i - 1)
            for s in range(SUB):
                nc.gpsimd.indirect_dma_start(xr[:, u, s, :], None, rows,
                                             bass.IndirectOffsetOnAxis(ap=take_now[:, u, s:s + 1], axis=0)).then_inc(rows_in[u], 16)

        def scatter(i, u):
            if not isinstance(i, int) or i >= 2:
                pool.wait_ge(y_stored[u], by_parity(i - 2, u))
            pool.wait_ge(y_out, i + 1)
            nc.gpsimd.tensor_copy(put_now[:, u, :], blocks(put, i)).then_inc(put_set, 1)
            pool.wait_ge(loaded, 48)
            pool.wait_ge(put_set, i + 1)
            for s in range(SUB):
                nc.gpsimd.indirect_dma_start(y, bass.IndirectOffsetOnAxis(ap=put_now[:, u, s:s + 1], axis=0),
                                             ys[:, u, s, :], None).then_inc(y_stored[u], 16)

        gather(0, 0)
        gather(1, 1)
        pool.wait_ge(loaded, 48)

        def step(i, u, first, second, turn, load):
            if load and (not isinstance(i, int) or i >= 0):
                gather(i + 2, u)
            if second:
                scatter(i - 1, 1 - u)
            if not isinstance(i, int) or 3 <= i < B + 3:
                nc.gpsimd.tensor_tensor(X[:, i - 3, :], X[:, i - 3, :], ln_b[:], ALU.add).then_inc(biased, 1)

        expert_steps(pool, step)
        pool.wait_ge(biased, B)
        for u in range(2):
            pool.wait_ge(y_stored[u], 16 * SUB * ((NT + 1 - u) // 2))

    @block.tensor
    def _(pe):
        MM = nc.tensor.matmul
        pe.wait_ge(ready, 1)
        expert = {}

        def step(i, u, first, second, turn, load):
            w = 1 - u
            if turn:
                pe.wait_ge(rows_in[w], by_parity(i + 1, w))
                reached(pe, moved, i + 1)
                for q in range(2 * HALVES):
                    for s in range(SUB):
                        last = nc.tensor.transpose(tb[:, q * TS + s * P:q * TS + (s + 1) * P],
                                                   xr[:, w, s, q * P:(q + 1) * P], ident16[:])
                last.then_inc(turned, 1)
            if first:
                e1 = pe.value_load(tile_expert[0:1, bass.ds(i, 1)], min_val=0, max_val=E - 1)
            if second:
                e2 = pe.value_load(tile_expert[0:1, bass.ds(i - 1, 1)], min_val=0, max_val=E - 1)
            if first:
                pe.wait_ge(moved, i + 1)
            for f in range(FC):
                if first:
                    n = f // 2
                    bank = hb[n % 2]
                    if f % 2 == 0:
                        if n >= 2:
                            pe.wait_ge(h_gelu[n - 2], i + 1)
                        else:
                            reached(pe, h_gelu[n + FP - 2], i)
                    out = bank[:, (f % 2) * TS:(f % 2 + 1) * TS]
                    cols = slice(f * P, (f + 1) * P)
                    for a in range(HALVES):
                        MM(out, w1h[:, e1, a, cols], xt[:, u, a, :], start=(a == 0), stop=False)
                        MM(out, w1h[:, e1, a, cols], xt[:, u, HALVES + a, :], start=False, stop=False)
                        last = MM(out, w1l[:, e1, a, cols], xt[:, u, a, :], start=False, stop=(a == HALVES - 1))
                    if f % 2 == 1:
                        last.then_inc(h_done[n], 1)
                if second:
                    if f % 2 == 0:
                        pe.wait_ge(h_lo[f // 2], i)
                    if f == 0:
                        reached(pe, y_out, i - 2)
                    for s in range(SUB):
                        out = yb[w][s][:, 0:D]
                        tok = slice(s * P, (s + 1) * P)
                        MM(out, hh[:, w, f, tok], w2h[:, e2, f, :], start=(f == 0), stop=False)
                        MM(out, hh[:, w, f, tok], w2l[:, e2, f, :], start=False, stop=False)
                        last = MM(out, hl[:, w, f, tok], w2h[:, e2, f, :], start=False, stop=(f == FC - 1))
            if second:
                last.then_inc(y_done, 1)

        expert_steps(pe, step)

    @block.scalar
    def _(act):
        act.wait_ge(ready, 1)
        act.wait_ge(loaded, 48)

        def step(i, u, first, second, turn, load):
            if first:
                e1 = act.value_load(tile_expert[0:1, bass.ds(i, 1)], min_val=0, max_val=E - 1)
                for n in range(FP):
                    act.wait_ge(h_done[n], i + 1)
                    if n >= 2:
                        act.wait_ge(h_lo[n - 2], i + 1)
                    else:
                        reached(act, h_lo[n + FP - 2], i)
                    for k in range(2):
                        last = nc.scalar.activation(g[:, n % 2, k * TS:(k + 1) * TS], hb[n % 2][:, k * TS:(k + 1) * TS],
                                                    ACT.Gelu, bias=b1[:, e1, 2 * n + k:2 * n + k + 1], scale=1.0 / WE)
                    last.then_inc(h_gelu[n], 1)

        expert_steps(act, step)

    @block.vector
    def _(dve):
        V = nc.vector
        dve.wait_ge(ident_in, 16)
        V.tensor_copy(ident16[:], ident[:]).then_inc(ready, 1)

        def step(i, u, first, second, turn, load):
            w = 1 - u
            if turn:
                dve.wait_ge(turned, i + 2)
                if not isinstance(i, int) or i >= 1:
                    dve.wait_ge(h_done[FP - 1], i)
                V.tensor_copy(xt[:, w].rearrange("p q n -> p (q n)"), tb[:]).then_inc(moved, 1)
            if first:
                for n in range(FP):
                    dve.wait_ge(h_gelu[n], i + 1)
                    if n == 0 and (not isinstance(i, int) or i >= 2):
                        dve.wait_ge(y_done, i - 1)
                    high = hh[:, u, 2 * n:2 * n + 2, :].rearrange("p f t -> p (f t)")
                    V.tensor_copy(high, g[:, n % 2, :]).then_inc(h_hi[n], 1)
                    dve.wait_ge(h_hi[n], i + 1)
                    V.tensor_tensor(hl[:, u, 2 * n:2 * n + 2, :].rearrange("p f t -> p (f t)"), g[:, n % 2, :],
                                    high, ALU.subtract).then_inc(h_lo[n], 1)
            if second:
                e2 = dve.value_load(tile_expert[0:1, bass.ds(i - 1, 1)], min_val=0, max_val=E - 1)
                dve.wait_ge(y_done, i)
                if isinstance(i, int) and i == 1:
                    dve.wait_ge(loaded, 48)
                if not isinstance(i, int) or i >= 3:
                    dve.wait_ge(y_stored[w], by_parity(i - 3, w))
                for s in range(SUB):
                    last = V.scalar_tensor_tensor(ys[:, w, s, :], yb[w][s][:, 0:D], 1.0 / WE, b2[:, e2, :],
                                                  ALU.mult, ALU.add)
                last.then_inc(y_out, 1)

        expert_steps(dve, step)


def combine_block(nc, sems, ctx, t, keep, xn2_dram, y, out):
    sb = lambda name, shape, dt: ctx.enter_context(nc.sbuf_tensor(name, shape, dt))
    sem = sems.new
    X, cw = keep["X"], keep["cw"]
    LB = 4
    GB = 8
    NG = B // GB

    y0 = sb("y0", [S, B, D], F32)
    y1 = sb("y1", [S, B, D], F32)
    xn2 = sb("xn2c", [S, B, D], F32)
    stats = sb("stats3", [S, B, 6], F32)
    mv = sb("mv3", [S, B, 2], F32)
    ve = sb("ve3", [S, B], F32)
    minus_half = sb("minus_half3", [S, B], F32)
    rstd = sb("rstd3", [S, B], F32)
    tmp = sb("tmp3", [S, B], F32)
    shift = sb("shift3", [S, B], F32)
    ln_w = sb("ln_w", [S, D], F32)

    loaded, half_set, aggregated, squared, centred = (sem(n) for n in (
        "c_loaded", "half_set", "aggregated", "squared", "centred"))
    y0_in, y1_in, xn_in = ([sem(f"{n}{g}") for g in range(B // LB)] for n in ("y0_in", "y1_in", "xn_in"))
    weighted, based, summed, stated, varied, rooted, refined, normed, scaled, final, stored = (sem("c_" + n) for n in (
        "weighted", "based", "summed", "stated", "varied", "rooted", "refined", "normed", "scaled", "final", "stored"))

    block = ctx.enter_context(nc.Block())
    y_read = [y[1 + k * B * S:1 + (k + 1) * B * S, :].rearrange("(g b s) d -> g s b d", b=LB, s=S) for k in range(2)]
    loads = lambda a: a.rearrange("(g b) s d -> g s b d", b=LB)
    group = lambda g: range(g * GB, (g + 1) * GB)
    cols = lambda g: slice(g * GB, (g + 1) * GB)
    LAST = NG - 1

    @block.sync
    def _(sp):
        for g in range(B // LB):
            here = slice(g * LB, (g + 1) * LB)
            sp.dma_start(y1[:, here, :], y_read[1][g]).then_inc(y1_in[g], 16)
            sp.dma_start(xn2[:, here, :], loads(xn2_dram)[g]).then_inc(xn_in[g], 16)
            sp.dma_start(y0[:, here, :], y_read[0][g]).then_inc(y0_in[g], 16)
            if g == 0:
                sp.dma_start(ln_w[:], t["ln_w"].to_broadcast([S, D])).then_inc(loaded, 16)
        for g in range(B // LB):
            sp.wait_ge(final, (g + 1) * LB)
            sp.dma_start(loads(out)[g], y0[:, g * LB:(g + 1) * LB, :]).then_inc(stored, 16)
        sp.wait_ge(stored, 16 * (B // LB))

    @block.scalar
    def _(act):
        def weight(g):
            for n in group(g):
                if n % LB == 0:
                    act.wait_ge(y1_in[n // LB], 16)
                nc.scalar.activation(y1[:, n, :], y1[:, n, :], ACT.Copy, scale=cw[:, 1, n:n + 1]).then_inc(weighted, 1)

        def normalise(g):
            act.wait_ge(refined, 4 * (g + 1))
            for n in group(g):
                nc.scalar.activation(y0[:, n, :], y0[:, n, :], ACT.Identity, scale=rstd[:, n:n + 1],
                                     bias=shift[:, n:n + 1]).then_inc(normed, 1)

        weight(0)
        weight(1)
        for g in range(2, NG):
            weight(g)
            normalise(g - 2)
        normalise(LAST - 1)

    @block.gpsimd
    def _(pool):
        def base(g):
            for n in group(g):
                if n % LB == 0:
                    pool.wait_ge(xn_in[n // LB], 16)
                pool.wait_ge(weighted, n + 1)
                nc.gpsimd.tensor_tensor(xn2[:, n, :], xn2[:, n, :], y1[:, n, :], ALU.add).then_inc(based, 1)

        def root(g):
            pool.wait_ge(varied, g + 1)
            nc.gpsimd.tensor_tensor(rstd[:, cols(g)], ve[:, cols(g)], minus_half[:, cols(g)], ALU.pow).then_inc(rooted, 1)

        def scale(g):
            for n in group(g):
                pool.wait_ge(normed, n + 1)
                nc.gpsimd.tensor_tensor(y0[:, n, :], y0[:, n, :], ln_w[:], ALU.mult).then_inc(scaled, 1)

        nc.gpsimd.memset(minus_half[:], -0.5).then_inc(half_set, 1)
        base(0)
        base(1)
        pool.wait_ge(half_set, 1)
        root(0)
        pool.wait_ge(loaded, 16)
        for g in range(2, NG):
            base(g)
            root(g - 1)
            scale(g - 2)
        root(LAST)
        scale(LAST - 1)

    @block.vector
    def _(dve):
        V = nc.vector

        def sum_and_stats(g):
            for n in group(g):
                if n % LB == 0:
                    dve.wait_ge(y0_in[n // LB], 16)
                dve.wait_ge(based, n + 1)
                V.scalar_tensor_tensor(y0[:, n, :], y0[:, n, :], cw[:, 0, n:n + 1], xn2[:, n, :], ALU.mult,
                                       ALU.add).then_inc(summed, 1)
                if n % GB:
                    stats_of(n - 1)
            stats_of(n)
            for n in group(g):
                dve.wait_ge(stated, n + 1)
                last = V.bn_aggr(mv[:, n, :], stats[:, n, :])
            last.then_inc(aggregated, 1)
            dve.wait_ge(aggregated, g + 1)
            V.tensor_scalar(ve[:, cols(g)], mv[:, cols(g), 1], LN3_EPS, None, ALU.add).then_inc(varied, 1)

        def stats_of(n):
            dve.wait_ge(summed, n + 1)
            V.bn_stats(stats[:, n, :], y0[:, n, :]).then_inc(stated, 1)

        def refine(g):
            c = cols(g)
            dve.wait_ge(rooted, g + 1)
            V.tensor_tensor(tmp[:, c], rstd[:, c], rstd[:, c], ALU.mult).then_inc(squared, 1)
            dve.wait_ge(squared, g + 1)
            V.tensor_tensor(tmp[:, c], tmp[:, c], ve[:, c], ALU.mult).then_inc(refined, 1)
            dve.wait_ge(refined, 4 * g + 1)
            V.tensor_scalar(tmp[:, c], tmp[:, c], -0.5, 1.5, ALU.mult, ALU.add).then_inc(refined, 1)
            dve.wait_ge(refined, 4 * g + 2)
            V.tensor_tensor(rstd[:, c], rstd[:, c], tmp[:, c], ALU.mult).then_inc(refined, 1)
            dve.wait_ge(refined, 4 * g + 3)
            V.scalar_tensor_tensor(shift[:, c], mv[:, c, 0], -1.0, rstd[:, c], ALU.mult, ALU.mult).then_inc(refined, 1)

        def finish(g):
            for n in group(g):
                dve.wait_ge(scaled, n + 1)
                V.tensor_tensor(y0[:, n, :], y0[:, n, :], X[:, n, :], ALU.add).then_inc(final, 1)

        sum_and_stats(0)
        sum_and_stats(1)
        refine(0)
        for g in range(2, NG):
            sum_and_stats(g)
            refine(g - 1)
            finish(g - 2)
        refine(LAST)
        dve.wait_ge(refined, 4 * NG)
        dve.wait_ge(loaded, 16)
        for n in group(LAST):
            V.scalar_tensor_tensor(y0[:, n, :], y0[:, n, :], mv[:, n, 0:1], ln_w[:], ALU.subtract,
                                   ALU.mult).then_inc(centred, 1)
        finish(LAST - 1)
        for n in group(LAST):
            dve.wait_ge(centred, n + 1 - LAST * GB)
            V.scalar_tensor_tensor(y0[:, n, :], y0[:, n, :], rstd[:, n:n + 1], X[:, n, :], ALU.mult,
                                   ALU.add).then_inc(final, 1)


class Semaphores:
    def __init__(self, nc):
        self.nc, self.stack, self.made = nc, ExitStack(), []

    def new(self, name):
        self.made.append(self.stack.enter_context(self.nc.semaphore(name)))
        return self.made[-1]

    def __enter__(self):
        return self

    def __exit__(self, *error):
        if error[0] is not None:
            return
        with self.nc.Block() as block:
            @block.gpsimd
            def _(pool):
                numbers = sorted(s.num for s in self.made)
                starts = [n for n in numbers if n - 1 not in numbers]
                ends = [n for n in numbers if n + 1 not in numbers]
                for first, last in zip(starts, ends):
                    pool.sem_clear(range(first, last + 1))
        self.stack.close()


def program(nc, t, out):
    rows = nc.dram_tensor("rows", (1 + B * S, 2 * D), F16, kind="Internal").ap()
    y = nc.dram_tensor("y", (1 + 2 * B * S + NT * TS, D), F32, kind="Internal").ap()
    xn2 = nc.dram_tensor("xn2_dram", (B, S, D), F32, kind="Internal").ap()
    w2_halves = nc.dram_tensor("w2_halves", (2, P, B, PIECE), F16, kind="Internal").ap()
    with ExitStack() as hold:
        sb = lambda name, shape, dt, stack=hold: stack.enter_context(nc.sbuf_tensor(name, shape, dt))
        keep = {"cw": sb("cw", [S, 2, B], F32), "tile_expert": sb("tile_expert", [1, NT], I32),
                "take": sb("take", [P, NB], U32), "put": sb("put", [P, NB], U32),
                "logits": sb("logits", [S, B, E], F32), "X": sb("X", [S, B, D], F32)}
        with ExitStack() as weights:
            for name in ("w1h", "w1l"):
                keep[name] = sb(name, [P, E, HALVES, F], F16, weights)
            with Semaphores(nc) as sems, ExitStack() as ctx:
                attention_block(nc, sems, ctx, t, keep, xn2, rows, w2_halves)
            for name in ("w2h", "w2l"):
                keep[name] = sb(name, [P, E, FC, D], F16, weights)
            with Semaphores(nc) as sems, ExitStack() as ctx:
                route_block(nc, sems, ctx, t, keep, rows, w2_halves)
            with Semaphores(nc) as sems, ExitStack() as ctx:
                expert_block(nc, sems, ctx, t, keep, rows, y)
        with Semaphores(nc) as sems, ExitStack() as ctx:
            combine_block(nc, sems, ctx, t, keep, xn2, y, out)




def kernel(**inputs):
    import numpy as np
    import concourse.bacc as bacc
    from concourse.bass_utils import run_bass_kernel_spmd

    g = {k: np.asarray(v) for k, v in inputs.items()}
    halves = lambda w: w.T.reshape(HALVES, P, -1).transpose(1, 0, 2)
    column = lambda b: b.reshape(HALVES, P).T
    pieces = lambda w, blocks, n: w.transpose(0, 2, 1).reshape(E, blocks, P, n).transpose(2, 0, 1, 3).reshape(
        P, B, PIECE).transpose(1, 0, 2)
    mask = g["mask_1x1xSxS2_ik0"][0, 0]
    arrays = {
        "x": g["x"],
        "ctxT": g["ctx_1024"].transpose(0, 2, 1).reshape(B, HALVES, P, T).transpose(0, 2, 1, 3).reshape(B, P, HALVES * T),
        "wqkv": np.stack([halves(g["L0_xattn_W" + n]) for n in "qkv"], 1),
        "wo": halves(g["L0_xattn_Wo"]),
        "bqk": np.stack([column(g["L0_xattn_b" + n]) for n in "qk"], 1),
        "bv": column(g["L0_xattn_bv"]),
        "bo": g["L0_xattn_bo"].reshape(1, D),
        "mask_q": mask,
        "router_w": halves(g["L0_ffn_router_w"]).reshape(P, HALVES * E),
        "router_b": g["L0_ffn_router_b"].reshape(1, E),
        "w12": np.stack([pieces(g["L0_ffn_w1"], HALVES, F), pieces(g["L0_ffn_w2"], FC, D)], 2),
        "b1": g["L0_ffn_b1"].reshape(E, FC, P).transpose(2, 0, 1),
        "b2": g["L0_ffn_b2"].reshape(1, E * D),
        "ln_w": g["L0_ffn_ln_w"].reshape(1, D),
        "ln_b": g["L0_ffn_ln_b"].reshape(1, D),
        "mask_k": mask.T.reshape(CH, KC, S).transpose(1, 0, 2),
    }
    arrays.update(constants(np))
    arrays = {k: np.ascontiguousarray(v) for k, v in arrays.items()}
    nc = bacc.Bacc("TRN2", target_bir_lowering=False, num_devices=1)
    t = {k: nc.dram_tensor("in_" + k, a.shape, mybir.dt.from_np(a.dtype), kind="ExternalInput").ap()
         for k, a in arrays.items()}
    out = nc.dram_tensor("out_0", (B, S, D), F32, kind="ExternalOutput").ap()
    program(nc, t, out)
    r = run_bass_kernel_spmd(nc, [{"in_" + k: a for k, a in arrays.items()}], core_ids=[0])
    return r.results[0]["out_0"]


def constants(np):
    f = np.float32
    rows = np.arange(P)
    sel = np.concatenate([np.eye(KC, P), np.ones((1, P))]).astype(f)
    parts = (np.triu(np.ones((P, S)), 1), np.tile(np.arange(E, 0, -1), (P, 1)), np.tile(np.arange(P), (P, 1)),
             P * (np.arange(B) % (B // 2)) + rows[:, None] + 1,
             (1 + 2 * B * S + np.arange(NT * TS)).reshape(NB, P).T,
             np.tile(np.repeat(np.arange(NT) * TS, E), (P, 1)))
    fixed = np.concatenate(parts, 1).astype(f)
    return {
        "ident": np.eye(P, dtype=f),
        "sel": sel,
        "fixed": fixed,
        "parity": np.stack([rows // DH % 2 == 0, rows // DH % 2 == 1], 1).astype(f),
    }
```

```python
from contextlib import ExitStack

import numpy as np

import concourse.bass as bass
from concourse import mybir

F32 = mybir.dt.float32
F16 = mybir.dt.float16
BF16 = mybir.dt.bfloat16
I32 = mybir.dt.int32
U32 = mybir.dt.uint32
ALU = mybir.AluOpType
ACT = mybir.ActivationFunctionType
AX = mybir.AxisListType

P = 128
B, S, T, D = 32, 112, 375, 256
PREPARED = (0, 3, 18, 25, 32)
H, DH = 16, 16
HALVES = D // P
CH = 3
KC = T // CH
PAIRS = H // 2
GROUPS = 4
HG = H // GROUPS
DV = DH + 1
SLOTS = GROUPS * CH
NA, NS = 3, 2
WS = 16.0
SCORE_SCALE = 1.0 / (WS * WS * DH ** 0.5)
MASKED = -float(2 ** 33)
LN1_EPS = 1e-5
E, F = 8, 1024
FC = F // P
WE = 256.0
LN2_EPS = 1e-5
PIECE = E * HALVES * F // B
TS = 256
NT = (2 * B * S + E * (TS - 1)) // TS
NB = NT * TS // P
WIDTHS = (S, E, P, B, NB, NT * E)


def split_steps(eng, step):
    def edge(i):
        step(i, i % 2, i + 1 < B, 0 <= i < B, 1 <= i <= B, 2 <= i <= B + 1, i >= 3, i + 2 < B, i + 3 < B)
    for i in (-1, 0, 1, 2, 3, 4):
        edge(i)
    pairs = (B - 3 - 5) // 2
    with eng.Fori(0, pairs) as j:
        for u in range(2):
            step(j * 2 + (5 + u), 1 - u, True, True, True, True, True, True, True)
    for i in range(5 + 2 * pairs, B + 3):
        edge(i)


def reached(eng, sem, count):
    if not isinstance(count, int) or count > 0:
        eng.wait_ge(sem, count)


def attention_block(nc, sems, ctx, t, keep_all, rows, w2_halves):
    sb = lambda name, shape, dt: ctx.enter_context(nc.sbuf_tensor(name, shape, dt))
    ps = lambda name, shape, dt: ctx.enter_context(nc.psum_tensor(name, shape, dt))
    sem = sems.new
    w2_halves = w2_halves.rearrange("k p b n -> b p k n")
    X, L = keep_all["X"], keep_all["logits"]
    w1h, w1l = (keep_all[n][:].rearrange("p e f d -> p (e f d)").rearrange("p (b n) -> p b n", b=B)
                for n in ("w1h", "w1l"))
    row_tiles = rows[1:1 + B * S, :].rearrange("(b s) n -> b s n", b=B)

    ident = sb("ident", [P, P], F32)
    sel = sb("sel", [KC + 1, P], BF16)
    parity = sb("parity", [P, 2], F32)
    wh = sb("wh", [P, 3, HALVES, D], F16)
    wl = sb("wl", [P, 3, HALVES, D], F16)
    wo = sb("wo", [P, HALVES, D], F32)
    bqk = sb("bqk", [P, 2, HALVES], F32)
    bqk16 = sb("bqk16", [P, 2, HALVES], F32)
    bq_par = sb("bq_par", [P, HALVES, 2], F32)
    bv = sb("bv", [P, HALVES], F32)
    bo_row = sb("bo_row", [1, D], F32)
    bo_all = sb("bo_all", [S, D], F32)
    mask_add = sb("mask_add", [S, T], F32)
    n_masked = sb("n_masked", [S, 1], F32)
    keep_q = sb("keep_q", [S, 1], F32)
    keep = sb("keep", [P, S], F32)
    mv1 = sb("mv1", [S, B, 2], F32)
    ve1 = sb("ve1", [S, B, 1], F32)
    rstd1 = sb("rstd1", [S, B, 1], F32)
    shift1 = sb("shift1", [S, B, 1], F32)
    ct = sb("ct", [P, 2, HALVES * T], F32)
    cth = sb("cth", [P, 2, HALVES, T], F16)
    ctl = sb("ctl", [P, 2, HALVES, T], F16)
    xn = sb("xn", [S, D], F32)
    xth = sb("xth", [P, HALVES, S], F16)
    xtl = sb("xtl", [P, HALVES, S], F16)
    qf = sb("qf", [P, HALVES, 2, S], F32)
    qm = sb("qm", [P, HALVES, 2, S], F32)
    qh = sb("qh", [P, 2, HALVES, 2 * S], F16)
    ql = sb("ql", [P, 2, HALVES, 2 * S], F16)
    kh = sb("kh", [P, 2, HALVES, T], F16)
    kl = sb("kl", [P, 2, HALVES, T], F16)
    ROW = T + 2 * S
    stack = sb("stack", [96, 2, PAIRS, ROW], F16)
    vt = sb("vt", [KC, 2, CH, H, DV], F32)
    top = sb("top", [S, 2, H], F32)
    neg_top = sb("neg_top", [H, CH, S], BF16)
    mb = sb("mb", [KC + 1, 2, H, CH, S], BF16)
    pt = sb("pt", [P, 4, HG * S], F32)
    ots = sb("ots", [P, GROUPS * S], F32)
    rsum = sb("rsum", [S, H, 1], F32)
    at = sb("at", [S, H, DH], F32)
    att = sb("att", [P, HALVES, S], F32)
    stats2 = sb("stats2", [S, 6], F32)
    stats_now = sb("stats_now", [S, 6], F32)
    mv = sb("mv", [S, 2], F32)
    ve = sb("ve", [S, 1], F32)
    minus_half = sb("minus_half", [S, 1], F32)
    first_root = sb("first_root", [S, 1], F32)
    newton = sb("newton", [S, 2], F32)
    rstd2 = sb("rstd2", [S, 1], F32)
    shift2 = sb("shift2", [S, 1], F32)
    xn2 = sb("xn2", [S, 2, D], F32)
    xt2 = sb("xt2", [P, 2 * HALVES, S], F16)
    rw32 = sb("rw32", [P, HALVES * E], F32)
    rw = sb("rw", [P, 2, HALVES * E], F16)
    rb = sb("rb", [S, E], F32)
    w_in = sb("w_in", [P, 2, PIECE], F32)
    w2_out = sb("w2_out", [P, 2, PIECE], F16)
    scratch = keep_all["w1l"][:].rearrange("p e f d -> p (e f d)").bitcast(F32)
    taken = [scratch.shape[1] // 2]

    def borrow(rows, *shape):
        size = int(np.prod(shape))
        taken[0] += size
        flat = scratch[0:rows, taken[0] - size:taken[0]]
        if len(shape) == 1:
            return flat
        names = "abc"[:len(shape)]
        return flat.rearrange(f"p ({' '.join(names)}) -> p {' '.join(names)}", **dict(zip(names, shape)))

    w32 = borrow(P, 3, HALVES, D)
    mask_q = borrow(S, T).bitcast(I32)
    mask_k = borrow(KC, CH, S).bitcast(I32)
    mk32 = borrow(KC, CH, S)
    sel32 = borrow(KC + 1, P)
    ones, keep_diag = borrow(S, P), borrow(S, S)
    stats1 = borrow(S, B, 6)

    sa = [ps(f"sa{k}", [P, 512], F32) for k in range(NA)]
    sbk = [ps(f"sb{k}", [P, 512], F32) for k in range(NS)]
    ot = ps("ot", [P, 512], F32)
    pj = [ps(f"pj{k}", [P, 512], F32) for k in range(2)]
    JOBS = ["xT", "OT", "Q", "K0", "K1", "AT", "V01", "V2", "MT", "WO"]
    bank = {job: pj[n % 2] for n, job in enumerate(JOBS)}
    turned2 = sa[0][:, 0:HALVES * S]
    logits_out = sa[1][0:S, 0:E]
    WO_AT, X2_AT, LG_AT = 10, 11, 9
    JOB_AT = {"xT": 0, "OT": 0, "Q": 2, "K0": 3, "K1": 4, "AT": 5, "V01": 6, "V2": 7, "MT": 9, "WO": WO_AT}

    loaded = {n: sem("ld_" + n) for n in ("x0", "x", "w", "small", "mask_k", "wo", "fixed")}
    prep = sem("prep")
    varied1, rooted1, mask_made = sem("varied1"), sem("rooted1"), sem("mask_made")
    mb_set, bo_set, router_set = sem("mb_set"), sem("bo_set"), sem("router_set")
    diag = sem("diag")
    ready = sem("ready")
    turned_prep = sem("turned_prep")
    filled = sem("filled")
    ct_in = [sem(f"ct_in{k}") for k in range(2)]
    ct_hi, ct_lo = sem("ct_hi"), sem("ct_lo")
    xn_made = sem("xn_made")
    done = {job: sem("pe_" + job) for job in JOBS + ["X2", "LG"]}
    xt_hi, xt_lo = sem("xt_hi"), sem("xt_lo")
    q_biased, q_kept, q_hi, q_lo = sem("q_biased"), sem("q_kept"), sem("q_hi"), sem("q_lo")
    k_hi = [sem(f"k_hi{k}") for k in range(2)]
    k_lo = [sem(f"k_lo{k}") for k in range(2)]
    v_out = [sem("v_out01"), sem("v_out2")]
    spilled = [sem(f"spilled{u}") for u in range(2)]
    stacked = [[sem(f"stacked{k}{u}") for u in range(2)] for k in range(HALVES)]
    a_scored = [sem(f"a_scored{k}") for k in range(H)]
    a_top = [sem(f"a_top{k}") for k in range(H)]
    top_out = sem("top_out")
    top_in = sem("top_in")
    b_scored = [sem(f"b_scored{k}") for k in range(SLOTS)]
    b_exp = [sem(f"b_exp{k}") for k in range(SLOTS)]
    b_pv = [sem(f"b_pv{k}") for k in range(SLOTS)]
    ot_out = sem("ot_out")
    rs_out, at_out, att_out, xb_out, x2_out, st_out = (sem(n) for n in (
        "rs_out", "at_out", "att_out", "xb_out", "x2_out", "st_out"))
    st_taken, varied, rooted, refined = sem("st_taken"), sem("varied"), sem("rooted"), sem("refined")
    n_made, xt2_hi, xt2_lo, lg_out = (sem(n) for n in ("n_made", "xt2_hi", "xt2_lo", "lg_out"))
    n_stored = [sem(f"n_stored{u}") for u in range(2)]
    w_loaded, w_stored = sem("w_loaded"), sem("w_stored")
    w_hi, w_lo = sem("w_hi"), sem("w_lo")

    def by_parity(b, u):
        return (b - u) * 8 + 16

    spill = nc.dram_tensor("spill", (2, 3, P, HALVES, ROW), F16, kind="Internal").ap()
    spill_read = [[[spill[u, r].rearrange("(q p) h n -> h p q n", p=32)[k] for k in range(HALVES)]
                   for r in range(3)] for u in range(2)]

    def in_stack(b, u):
        return (b - u) * 24 + 48

    def in_spill(b, u):
        return (b - u) * 48 + 96

    block = ctx.enter_context(nc.Block())

    @block.sync
    def _(sp):
        x_rows = t["x"].rearrange("b s d -> s b d")
        first = PREPARED[1]
        sp.dma_start(w32, t["wqkv"]).then_inc(loaded["w"], 16)
        for dst, src in ((mask_q, t["mask_q"]), (ident[:], t["ident"]), (parity[:], t["parity"]), (bqk[:], t["bqk"])):
            sp.dma_start(dst, src).then_inc(loaded["small"], 16)
        sp.dma_start(X[:, 0:first, :], x_rows[:, 0:first, :]).then_inc(loaded["x0"], 16)
        sp.dma_start(ct[:, 0, :], t["ctxT"][0]).then_inc(ct_in[0], 16)
        for dst, src in ((sel32, t["sel"]), (mask_k, t["mask_k"])):
            sp.dma_start(dst, src).then_inc(loaded["mask_k"], 16)
        sp.dma_start(ct[:, 1, :], t["ctxT"][1]).then_inc(ct_in[1], 16)
        sp.dma_start(X[:, first:B, :], x_rows[:, first:B, :]).then_inc(loaded["x"], 16)
        for dst, src in ((wo[:], t["wo"]), (bv[:], t["bv"]), (bo_row[:], t["bo"]), (rw32[:], t["router_w"]),
                         (rb[:], t["router_b"].to_broadcast([S, E]))):
            sp.dma_start(dst, src).then_inc(loaded["wo"], 16)
        sp.dma_start(keep_all["fixed"][:], t["fixed"]).then_inc(loaded["fixed"], 16)

        def step(i, u, project, find, attend, output, norm, split_next, load_next):
            if load_next:
                reached(sp, ct_hi, i + 2)
                reached(sp, ct_lo, i + 2)
                sp.wait_ge(loaded["x"], 16)
                sp.dma_start(ct[:, 1 - u, :], t["ctxT"][i + 3]).then_inc(ct_in[1 - u], 16)
            if attend:
                sp.wait_ge(loaded["x"], 16)
                sp.wait_ge(w_hi, i)
                sp.wait_ge(w_lo, i)
                sp.dma_start(w2_halves[i - 1], w2_out[:]).then_inc(w_stored, 16)
            if find:
                sp.dma_start(w_in[:], t["w12"][i]).then_inc(w_loaded, 16)
            if project:
                w = 1 - u
                if not isinstance(i, int) or i >= 1:
                    for k in range(HALVES):
                        sp.wait_ge(stacked[k][w], in_stack(i - 1, w))
                sp.wait_ge(q_hi, i + 2)
                for r in (0, 1):
                    sp.dma_start(spill[w, r, :, :, T:ROW], qh[:, w]).then_inc(spilled[w], 16)
                sp.wait_ge(q_lo, i + 2)
                sp.dma_start(spill[w, 2, :, :, T:ROW], ql[:, w]).then_inc(spilled[w], 16)
                for k in range(HALVES):
                    sp.wait_ge(k_hi[k], i + 2)
                for r in (0, 2):
                    sp.dma_start(spill[w, r, :, :, 0:T], kh[:, w]).then_inc(spilled[w], 16)
                if attend:
                    sp.wait_ge(b_scored[SLOTS // 2 - 1], i)
                for k in range(HALVES):
                    sp.wait_ge(k_lo[k], i + 2)
                sp.dma_start(spill[w, 1, :, :, 0:T], kl[:, w]).then_inc(spilled[w], 16)
                sp.wait_ge(spilled[w], in_spill(i + 1, w))
                for k in range(HALVES):
                    if attend and k == 1:
                        sp.wait_ge(b_scored[SLOTS - 1], i)
                    for r in range(3):
                        sp.dma_start(stack[32 * r:32 * r + 32, w, PAIRS // 2 * k:PAIRS // 2 * (k + 1), :],
                                     spill_read[w][r][k]).then_inc(stacked[k][w], 16)

            if norm:
                w = 1 - u
                sp.wait_ge(loaded["x"], 16)
                sp.wait_ge(n_made, i - 2)
                sp.dma_start(row_tiles[i - 3], xn2[:, w, :]).then_inc(n_stored[w], 16)

        sp.wait_ge(filled, 3)
        split_steps(sp, step)
        for u in range(2):
            sp.wait_ge(n_stored[u], 8 * B)
        sp.wait_ge(w_stored, 16 * B)
        sp.wait_ge(loaded["fixed"], 16)

    @block.gpsimd
    def _(pool):
        nc.gpsimd.memset(ones, 1.0).then_inc(filled, 1)
        nc.gpsimd.memset(minus_half[:], -0.5).then_inc(filled, 1)
        nc.gpsimd.memset(vt[:], 1.0).then_inc(filled, 1)

        def root1(k):
            lo, hi = PREPARED[k], PREPARED[k + 1]
            pool.wait_ge(varied1, k + 1)
            nc.gpsimd.tensor_tensor(rstd1[:, lo:hi, 0], ve1[:, lo:hi, 0], minus_half[:].to_broadcast([S, hi - lo]),
                                    ALU.pow).then_inc(rooted1, 1)

        pool.wait_ge(filled, 3)
        root1(0)

        def split_context(b, u):
            pool.wait_ge(ct_hi, b + 1)
            if not isinstance(b, int) or b >= 2:
                pool.wait_ge(done["V2"], b - 1)
            nc.gpsimd.tensor_tensor(ctl[:, u, :, :].rearrange("p a t -> p (a t)"), ct[:, u, :],
                                    cth[:, u, :, :].rearrange("p a t -> p (a t)"), ALU.subtract).then_inc(ct_lo, 1)

        split_context(0, 0)
        pool.wait_ge(ready, 1)

        def step(i, u, project, find, attend, output, norm, split_next, load_next):
            if project:
                w = 1 - u
                pool.wait_ge(q_biased, i + 2)
                reached(pool, q_lo, i + 1)
                f, fn, g = "p a r s -> p (a r s)", "p a n -> p (a n)", "p a r s -> p (a r) s"
                keep4 = keep[:].unsqueeze(1).to_broadcast([P, 4, S])
                nc.gpsimd.tensor_tensor(qm[:].rearrange(g), qf[:].rearrange(g), keep4,
                                        ALU.mult).then_inc(q_kept, 1)
                if not isinstance(i, int) or i >= 1:
                    pool.wait_ge(spilled[w], in_spill(i - 1, w))
                nc.gpsimd.tensor_tensor(qh[:, w].rearrange("p a (r s) -> p (a r) s", r=2), qf[:].rearrange(g), keep4,
                                        ALU.mult).then_inc(q_hi, 1)
                pool.wait_ge(q_kept, i + 2)
                pool.wait_ge(q_hi, i + 2)
                nc.gpsimd.tensor_tensor(ql[:, w].rearrange(fn), qm[:].rearrange(f), qh[:, w].rearrange(fn),
                                        ALU.subtract).then_inc(q_lo, 1)
            if norm:
                pool.wait_ge(varied, i - 2)
                nc.gpsimd.tensor_tensor(first_root[:], ve[:], minus_half[:], ALU.pow).then_inc(rooted, 1)
            if output:
                if isinstance(i, int) and i == 2:
                    pool.wait_ge(bo_set, 1)
                nc.gpsimd.tensor_tensor(X[:, i - 2, :], X[:, i - 2, :], bo_all[:], ALU.add).then_inc(xb_out, 1)
            if isinstance(i, int) and i == -1:
                split_context(1, 1)
            if split_next:
                if not isinstance(i, int) or i >= 0:
                    split_context(i + 2, u)
            if isinstance(i, int) and i + 2 < len(PREPARED) - 1:
                root1(i + 2)

        split_steps(pool, step)

    @block.scalar
    def _(act):
        def split_context(b, u):
            act.wait_ge(ct_in[u], (b // 2 + 1) * 16 if isinstance(b, int) else (b - u) * 8 + 16)
            if not isinstance(b, int) or b >= 2:
                act.wait_ge(done["V2"], b - 1)
            nc.scalar.copy(cth[:, u, :, :].rearrange("p a t -> p (a t)"), ct[:, u, :]).then_inc(ct_hi, 1)

        split_context(0, 0)
        act.wait_ge(ready, 1)

        def step(i, u, project, find, attend, output, norm, split_next, load_next):
            w = 1 - u
            for n in range(SLOTS + 1):
                if attend and n < SLOTS:
                    act.wait_ge(b_scored[n], i)
                    if n >= 4:
                        act.wait_ge(b_pv[n - 4], i)
                    elif not isinstance(i, int) or i >= 2:
                        act.wait_ge(b_pv[n + SLOTS - 4], i - 1)
                    nc.scalar.activation(pt[0:KC, n % 4, :], sbk[n % NS][0:KC, 0:HG * S], ACT.Exp,
                                         scale=SCORE_SCALE).then_inc(b_exp[n], 1)
                if n == 11 and norm:
                    act.wait_ge(done["X2"], i - 2)
                    reached(act, done["LG"], i - 3)
                    nc.scalar.copy(xt2[:, 0:HALVES].rearrange("p q s -> p (q s)"), turned2).then_inc(xt2_hi, 1)
                if n == 6 and find:
                    act.wait_ge(w_loaded, 16 * i + 16)
                    nc.scalar.mul(w1h[:, i, :], w_in[:, 0, :], WE)
                    reached(act, w_stored, 16 * i)
                    nc.scalar.mul(w2_out[:, 0, :], w_in[:, 1, :], WE).then_inc(w_hi, 1)
                if n == 0 and project:
                    act.wait_ge(done["xT"], i + 2)
                    reached(act, done["Q"], i + 1)
                    nc.scalar.copy(xth[:].rearrange("p a s -> p (a s)"),
                                   bank["xT"][:, 0:HALVES * S]).then_inc(xt_hi, 1)
                if n == 2 and project:
                    act.wait_ge(done["Q"], i + 2)
                    reached(act, q_hi, i + 1)
                    for half in range(HALVES):
                        for r in range(2):
                            last = nc.scalar.activation(qf[:, half, r, :], bank["Q"][:, half * S:(half + 1) * S],
                                                        ACT.Identity, scale=parity[:, r:r + 1],
                                                        bias=bq_par[:, half, r:r + 1])
                    last.then_inc(q_biased, 1)
                if n in (3, 4) and project:
                    half = n - 3
                    act.wait_ge(done[f"K{half}"], i + 2)
                    if not isinstance(i, int) or i >= 1:
                        act.wait_ge(spilled[w], in_spill(i - 1, w))
                    nc.scalar.activation(kh[:, w, half, :], bank[f"K{half}"][:, 0:T], ACT.Identity,
                                         bias=bqk16[:, 1, half:half + 1]).then_inc(k_hi[half], 1)
                if n == 5 and output:
                    act.wait_ge(done["AT"], i - 1)
                    if not isinstance(i, int) or i >= 3:
                        act.wait_ge(done["WO"], i - 2)
                    nc.scalar.copy(att[:].rearrange("p a s -> p (a s)"),
                                   bank["AT"][:, 0:HALVES * S]).then_inc(att_out, 1)
                if n == 7 and find:
                    act.wait_ge(done["V01"], i + 1)
                    if not isinstance(i, int) or i >= 2:
                        act.wait_ge(b_pv[SLOTS - 1], i - 1)
                    nc.scalar.activation(vt[:, u, 0:2, :, 0:DH],
                                         bank["V01"][0:KC, :].rearrange("p (c h d) -> p c h d", c=2, h=H),
                                         ACT.Copy, scale=1.0 / WS).then_inc(v_out[0], 1)
                if n == 8 and find:
                    act.wait_ge(done["V2"], i + 1)
                    nc.scalar.activation(vt[:, u, 2, :, 0:DH],
                                         bank["V2"][0:KC, 0:D].rearrange("p (h d) -> p h d", h=H),
                                         ACT.Copy, scale=1.0 / WS).then_inc(v_out[1], 1)
                if n == 9 and find:
                    act.wait_ge(done["MT"], i + 1)
                    reached(act, top_in, i * 16)
                    nc.scalar.mul(neg_top[:], bank["MT"][0:H, 0:S].unsqueeze(1).to_broadcast([H, CH, S]), -1.0).then_inc(top_out, 1)
                    act.wait_ge(top_out, i + 1)
                    if not isinstance(i, int) or i >= 2:
                        act.wait_ge(b_scored[SLOTS - 1], i - 1)
                    act.dma_start(mb[KC:KC + 1, u].rearrange("o h c s -> o h (c s)"),
                                  neg_top[:].rearrange("h c s -> h (c s)")).then_inc(top_in, 16)
                if n == SLOTS and attend:
                    act.wait_ge(b_pv[SLOTS - 1], i)
                    reached(act, done["OT"], i - 1)
                    nc.scalar.copy(ots[:], ot[:, 0:GROUPS * S]).then_inc(ot_out, 1)
                if n == SLOTS and isinstance(i, int) and i == -1:
                    split_context(1, 1)
                    act.wait_ge(mask_made, 1)
                    for k in range(2):
                        nc.scalar.copy(mb[0:KC, k].rearrange("p h c s -> p h (c s)"),
                                       mk32.rearrange("p c s -> p (c s)").unsqueeze(1).to_broadcast(
                                           [KC, H, CH * S])).then_inc(mb_set, 1)
                if n == SLOTS and split_next and (not isinstance(i, int) or i >= 0):
                    split_context(i + 2, u)

        split_steps(act, step)

    @block.vector
    def _(dve):
        count = [0]

        def tick(instruction):
            count[0] += 1
            instruction.then_inc(prep, 1)
            dve.wait_ge(prep, count[0])

        V = nc.vector
        dve.wait_ge(loaded["w"], 16)
        tick(V.tensor_scalar(wh[:], w32, WS, None, ALU.mult))
        tick(V.scalar_tensor_tensor(wl[:].rearrange("p w a d -> p (w a d)"), w32.rearrange("p w a d -> p (w a d)"),
                                    WS, wh[:].rearrange("p w a d -> p (w a d)"), ALU.mult, ALU.subtract))
        dve.wait_ge(loaded["small"], 16 * 4)
        tick(V.tensor_scalar(bqk16[:], bqk[:], WS, None, ALU.mult))
        for half in range(HALVES):
            tick(V.tensor_scalar(bq_par[:, half, :], parity[:], bqk16[:, 0, half:half + 1], None, ALU.mult))
        tick(V.tensor_scalar(mask_add[:], mask_q, 0.0, None, ALU.is_equal))
        tick(V.reduce_sum(n_masked[:], mask_add[:], AX.X))
        tick(V.tensor_scalar(keep_q[:], n_masked[:], float(T), None, ALU.is_lt))
        tick(V.tensor_scalar(mask_add[:], mask_add[:], keep_q[:], MASKED, ALU.mult, ALU.mult))
        dve.wait_ge(filled, 3)
        V.tensor_scalar(keep_diag, ident[0:S, 0:S], keep_q[:], None, ALU.mult).then_inc(diag, 1)

        def x_stats(k):
            lo, hi = PREPARED[k], PREPARED[k + 1]
            dve.wait_ge(loaded["x0" if k == 0 else "x"], 16)
            for b in range(lo, hi):
                last = V.bn_stats(stats1[:, b, :], X[:, b, :])
            tick(last)
            for b in range(lo, hi):
                last = V.bn_aggr(mv1[:, b, :], stats1[:, b, :])
            tick(last)
            V.tensor_scalar(ve1[:, lo:hi, 0], mv1[:, lo:hi, 1], LN1_EPS, None, ALU.add).then_inc(varied1, 1)

        def x_scales(k):
            here = slice(PREPARED[k], PREPARED[k + 1])
            r, s, v = rstd1[:, here, 0], shift1[:, here, 0], ve1[:, here, 0]
            dve.wait_ge(rooted1, k + 1)
            tick(V.tensor_tensor(s, r, r, ALU.mult))
            tick(V.tensor_tensor(s, s, v, ALU.mult))
            tick(V.tensor_scalar(s, s, -0.5, 1.5, ALU.mult, ALU.add))
            tick(V.tensor_tensor(r, r, s, ALU.mult))
            tick(V.scalar_tensor_tensor(s, mv1[:, here, 0], -1.0, r, ALU.mult, ALU.mult))

        x_stats(0)
        dve.wait_ge(turned_prep, 1)
        tick(V.tensor_copy(keep[:], pj[0][:, 0:S]))
        x_scales(0)

        def normalise(b, u):
            if not isinstance(b, int) or b >= 1:
                dve.wait_ge(done["xT"], b)
            V.tensor_scalar(xn[:], X[:, b, :], rstd1[:, b, :], shift1[:, b, :],
                            ALU.mult, ALU.add).then_inc(xn_made, 1)

        normalise(0, 0)
        V.memset(ot[:], 0.0).then_inc(ready, 1)

        def step(i, u, project, find, attend, output, norm, split_next, load_next):
            w = 1 - u
            if find:
                if not isinstance(i, int) or i >= 2:
                    dve.wait_ge(done["MT"], i - 1)
                dve.wait_ge(a_scored[0], i + 1)
            if norm:
                dve.wait_ge(st_out, i - 2)
                reached(dve, n_made, i - 3)
                V.tensor_copy(stats_now[:], stats2[:]).then_inc(st_taken, 1)
            for n in range(SLOTS):
                if n < 8 and find:
                    for h in (2 * n, 2 * n + 1):
                        dve.wait_ge(loaded["w"], 16)
                        dve.wait_ge(a_scored[h], i + 1)
                        V.tensor_tensor_reduce(sa[h % NA][0:S, 0:T], sa[h % NA][0:S, 0:T], mask_add[:], 1.0, -3.0e38,
                                               ALU.add, ALU.max, top[:, u, h:h + 1]).then_inc(a_top[h], 1)
                if n == 1 and output:
                    dve.wait_ge(done["OT"], i - 1)
                    o = bank["OT"][0:S, :].rearrange("p (h d) -> p h d", h=H)
                    V.reciprocal(rsum[:], o[:, :, DH:DV]).then_inc(rs_out, 1)
                    dve.wait_ge(rs_out, i - 1)
                    V.tensor_tensor(at[:], o[:, :, 0:DH], rsum[:].to_broadcast([S, H, DH]),
                                    ALU.mult).then_inc(at_out, 1)
                if n in (3, 4) and project:
                    half = n - 3
                    dve.wait_ge(k_hi[half], i + 2)
                    V.scalar_tensor_tensor(kl[:, w, half, :], bank[f"K{half}"][:, 0:T], bqk16[:, 1, half:half + 1],
                                           kh[:, w, half, :], ALU.add, ALU.subtract).then_inc(k_lo[half], 1)
                if n == 0 and project:
                    dve.wait_ge(done["xT"], i + 2)
                    dve.wait_ge(xt_hi, i + 2)
                    V.tensor_tensor(xtl[:].rearrange("p a s -> p (a s)"), bank["xT"][:, 0:HALVES * S],
                                    xth[:].rearrange("p a s -> p (a s)"), ALU.subtract).then_inc(xt_lo, 1)
                if n == 5 and norm:
                    dve.wait_ge(loaded["w"], 16)
                    dve.wait_ge(st_taken, i - 2)
                    reached(dve, n_made, i - 3)
                    V.bn_aggr(mv[:], stats_now[:]).then_inc(refined, 1)
                    dve.wait_ge(refined, (i - 3) * 5 + 1)
                    V.tensor_scalar(ve[:], mv[:, 1:2], LN2_EPS, None, ALU.add).then_inc(varied, 1)
                if n == 8 and norm:
                    dve.wait_ge(rooted, i - 2)
                    V.tensor_scalar(newton[:, 0:1], ve[:], first_root[:], None, ALU.mult).then_inc(refined, 1)
                    dve.wait_ge(refined, (i - 3) * 5 + 2)
                    V.tensor_scalar(newton[:, 1:2], newton[:, 0:1], first_root[:], -0.5, ALU.mult, ALU.mult).then_inc(refined, 1)
                    dve.wait_ge(refined, (i - 3) * 5 + 3)
                    if not isinstance(i, int) or i >= 4:
                        dve.wait_ge(n_made, i - 3)
                    V.tensor_scalar(rstd2[:], newton[:, 1:2], 1.5, first_root[:], ALU.add, ALU.mult).then_inc(refined, 1)
                    dve.wait_ge(refined, (i - 3) * 5 + 4)
                    V.tensor_scalar(shift2[:], mv[:, 0:1], -1.0, rstd2[:], ALU.mult, ALU.mult).then_inc(refined, 1)
                    dve.wait_ge(refined, (i - 3) * 5 + 5)
                    if not isinstance(i, int) or i >= 5:
                        dve.wait_ge(n_stored[w], by_parity(i - 5, w))
                        dve.wait_ge(done["X2"], i - 4)
                    V.tensor_scalar(xn2[:, w, :], X[:, i - 3, :], rstd2[:], shift2[:], ALU.mult, ALU.add).then_inc(n_made, 1)
                if n == 9 and find:
                    dve.wait_ge(w_hi, i + 1)
                    V.scalar_tensor_tensor(w1l[:, i, :], w_in[:, 0, :], WE, w1h[:, i, :], ALU.mult, ALU.subtract)
                    V.scalar_tensor_tensor(w2_out[:, 1, :], w_in[:, 1, :], WE, w2_out[:, 0, :], ALU.mult,
                                           ALU.subtract).then_inc(w_lo, 1)
                if n == 10 and norm and (not isinstance(i, int) or i >= 4):
                    dve.wait_ge(done["LG"], i - 3)
                    V.scalar_tensor_tensor(L[:, i - 4, :], logits_out, 1.0 / WE, rb[:],
                                           ALU.mult, ALU.add).then_inc(lg_out, 1)
                if n == WO_AT and output:
                    dve.wait_ge(done["WO"], i - 1)
                    dve.wait_ge(xb_out, i - 1)
                    V.tensor_tensor(X[:, i - 2, :], bank["WO"][0:S, 0:D], X[:, i - 2, :], ALU.add).then_inc(x2_out, 1)
                    dve.wait_ge(loaded["w"], 16)
                    dve.wait_ge(x2_out, i - 1)
                    reached(dve, st_taken, i - 2)
                    V.bn_stats(stats2[:], X[:, i - 2, :]).then_inc(st_out, 1)
                if n == 11 and norm:
                    dve.wait_ge(xt2_hi, i - 2)
                    V.tensor_tensor(xt2[:, HALVES:].rearrange("p q s -> p (q s)"), turned2,
                                    xt2[:, 0:HALVES].rearrange("p q s -> p (q s)"), ALU.subtract).then_inc(xt2_lo, 1)
                if n == 9 and isinstance(i, int) and i == -1:
                    normalise(1, 1)
                    dve.wait_ge(loaded["mask_k"], 32)
                    tick(V.tensor_copy(sel[:], sel32))
                    tick(V.tensor_scalar(mk32, mask_k, 0.0, MASKED, ALU.is_equal, ALU.mult))
                    V.tensor_tensor(mk32, mk32, keep[0:KC, :].unsqueeze(1).to_broadcast([KC, CH, S]),
                                    ALU.mult).then_inc(mask_made, 1)
                if n == 11 and isinstance(i, int) and 0 <= i < len(PREPARED) - 2:
                    x_scales(i + 1)
                if n == 11 and isinstance(i, int) and i == 0:
                    dve.wait_ge(turned_prep, 2)
                    V.tensor_copy(bo_all[:], sbk[1][0:S, 0:D]).then_inc(bo_set, 1)
                    tick(V.tensor_scalar(rw[:, 0, :], rw32[:], WE, None, ALU.mult))
                    V.scalar_tensor_tensor(rw[:, 1, :], rw32[:], WE, rw[:, 0, :], ALU.mult,
                                           ALU.subtract).then_inc(router_set, 1)
                if n == 11 and isinstance(i, int) and i + 2 < len(PREPARED) - 1:
                    x_stats(i + 2)
                if n == 9 and split_next and (not isinstance(i, int) or i >= 0):
                    normalise(i + 2, u)

        split_steps(dve, step)
        dve.wait_ge(done["LG"], B)
        V.scalar_tensor_tensor(L[:, B - 1, :], logits_out, 1.0 / WE, rb[:], ALU.mult, ALU.add).then_inc(lg_out, 1)
        dve.wait_ge(lg_out, B)

    @block.tensor
    def _(pe):
        MM = nc.tensor.matmul
        pe.wait_ge(diag, 1)
        pe.wait_ge(filled, 3)
        MM(pj[0][:, 0:S], ones, keep_diag, start=True, stop=True).then_inc(turned_prep, 1)

        def output_bias():
            pe.wait_ge(loaded["wo"], 16 * 5)
            MM(sbk[1][0:S, 0:D], ones[0:1, 0:S], bo_row[:], start=True, stop=False)
            for a in range(HALVES):
                last = MM(sbk[1][0:S, 0:D], bv[:, a:a + 1].to_broadcast([P, S]), wo[:, a, :], start=False,
                          stop=(a == HALVES - 1))
            last.then_inc(turned_prep, 1)

        pe.wait_ge(ready, 1)

        def project3(out, lhs, rhs):
            for a in range(HALVES):
                (lh, ll), (rh, rl) = lhs(a), rhs(a)
                MM(out, lh, rh, start=(a == 0), stop=False)
                MM(out, lh, rl, start=False, stop=False)
                last = MM(out, ll, rh, start=False, stop=(a == HALVES - 1))
            return last

        def step(i, u, project, find, attend, output, norm, split_next, load_next):
            w = 1 - u
            later = not isinstance(i, int)

            def bank_free(job):
                users = {"xT": (project, [(xt_hi, i + 2), (xt_lo, i + 2)]), "OT": (output, [(at_out, i - 1)]),
                         "Q": (project, [(q_biased, i + 2)]), "K0": (project, [(k_hi[0], i + 2), (k_lo[0], i + 2)]),
                         "K1": (project, [(k_hi[1], i + 2), (k_lo[1], i + 2)]), "AT": (output, [(att_out, i - 1)]),
                         "V01": (find, [(v_out[0], i + 1)]), "V2": (find, [(v_out[1], i + 1)]),
                         "MT": (find, [(top_out, i + 1)]), "WO": (output, [(x2_out, i - 1)])}
                n = JOBS.index(job)
                for m in range(n - 2, -1, -2):
                    runs, emptied = users[JOBS[m]]
                    if runs:
                        for s, c in emptied:
                            pe.wait_ge(s, c)
                        return
                if n % 2 == 0:
                    reached(pe, top_out, i if later else min(i, B))
                    if not later and i == 0:
                        pe.wait_ge(k_hi[1], 1)
                        pe.wait_ge(k_lo[1], 1)
                else:
                    reached(pe, x2_out, i - 2 if later else min(i - 2, B))
                    reached(pe, v_out[1], i if later else min(i, B))
                    if not later and i == 0:
                        pe.wait_ge(k_hi[0], 1)
                        pe.wait_ge(k_lo[0], 1)

            def find_max(h):
                if h % (H // 2) == 0:
                    pe.wait_ge(stacked[2 * h // H][u], in_stack(i, u))
                if h >= NA:
                    pe.wait_ge(a_top[h - NA], i + 1)
                elif later or i >= 1:
                    pe.wait_ge(a_top[max(g for g in range(H) if g % NA == h)], i)
                    if h < 2:
                        reached(pe, xt2_lo if h == 0 else lg_out, i - 3 if h == 0 else i - 4)
                q = (h % 2) * S
                MM(sa[h % NA][0:S, 0:T], stack[:, u, h // 2, T + q:T + q + S], stack[:, u, h // 2, 0:T],
                   start=True, stop=True).then_inc(a_scored[h], 1)

            def attend_scores(n):
                g, c = divmod(n, CH)
                if n >= NS:
                    pe.wait_ge(b_exp[n - NS], i)
                elif later or i >= 2:
                    pe.wait_ge(b_exp[n + SLOTS - NS], i - 1)
                if n == 0:
                    pe.wait_ge(top_in, 16 * i)
                MM(sbk[n % NS][:, 0:HG * S].rearrange("p (h s) -> p h s", h=HG), sel[:], mb[:, w, g * HG:(g + 1) * HG, c, :],
                   start=True, stop=False)
                for q in range(2):
                    last = MM(sbk[n % NS][:, 2 * S * q:2 * S * (q + 1)], stack[:, w, 2 * g + q, KC * c:KC * c + P],
                              stack[:, w, 2 * g + q, T:ROW], start=False, stop=(q == 1))
                last.then_inc(b_scored[n], 1)

            def attend_values(n):
                g, c = divmod(n, CH)
                pe.wait_ge(b_exp[n], i)
                if n == 0:
                    pe.wait_ge(v_out[1], i)
                    reached(pe, ot_out, i - 1)
                for j in range(HG):
                    last = MM(ot[32 * j:32 * j + DV, g * S:(g + 1) * S], vt[:, w, c, HG * g + j, :],
                              pt[0:KC, n % 4, j * S:(j + 1) * S], start=(c == 0), stop=(c == CH - 1),
                              tile_position=(0, 32 * j))
                last.then_inc(b_pv[n], 1)

            def job(name):
                out = bank[name]
                if name == "xT" and project:
                    pe.wait_ge(xn_made, i + 2)
                    bank_free(name)
                    for a in range(HALVES):
                        last = nc.tensor.transpose(out[:, a * S:(a + 1) * S], xn[:, a * P:(a + 1) * P],
                                                   ident[0:S, 0:S])
                elif name == "OT" and output:
                    pe.wait_ge(ot_out, i - 1)
                    bank_free(name)
                    for g in range(GROUPS):
                        last = nc.tensor.transpose(out[0:S, g * P:(g + 1) * P], ots[:, g * S:(g + 1) * S], ident[:])
                elif name == "Q" and project:
                    pe.wait_ge(xt_lo, i + 2)
                    bank_free(name)
                    for m in range(HALVES):
                        last = project3(out[:, m * S:(m + 1) * S],
                                        lambda a: (wh[:, 0, a, m * P:(m + 1) * P], wl[:, 0, a, m * P:(m + 1) * P]),
                                        lambda a: (xth[:, a, :], xtl[:, a, :]))
                elif name in ("K0", "K1") and project:
                    m = int(name[1])
                    if m == 0:
                        pe.wait_ge(ct_lo, i + 2)
                    bank_free(name)
                    last = project3(out[:, 0:T],
                                    lambda a: (wh[:, 1, a, m * P:(m + 1) * P], wl[:, 1, a, m * P:(m + 1) * P]),
                                    lambda a: (cth[:, w, a, :], ctl[:, w, a, :]))
                elif name == "AT" and output:
                    pe.wait_ge(at_out, i - 1)
                    bank_free(name)
                    flat = at[:].rearrange("p h d -> p (h d)")
                    for a in range(HALVES):
                        last = nc.tensor.transpose(out[:, a * S:(a + 1) * S], flat[:, a * P:(a + 1) * P],
                                                   ident[0:S, 0:S])
                elif name in ("V01", "V2") and find:
                    bank_free(name)
                    for c in ((0, 1) if name == "V01" else (2,)):
                        last = project3(out[0:KC, (c % 2) * D:(c % 2 + 1) * D],
                                        lambda a: (cth[:, u, a, c * KC:(c + 1) * KC], ctl[:, u, a, c * KC:(c + 1) * KC]),
                                        lambda a: (wh[:, 2, a, :], wl[:, 2, a, :]))
                elif name == "MT" and find:
                    pe.wait_ge(a_top[H - 1], i + 1)
                    bank_free(name)
                    last = nc.tensor.transpose(out[0:H, 0:S], top[:, u, :], ident[0:S, 0:S])
                elif name == "WO" and output:
                    pe.wait_ge(att_out, i - 1)
                    bank_free(name)
                    for a in range(HALVES):
                        last = MM(out[0:S, 0:D], att[:, a, :], wo[:, a, :], start=(a == 0), stop=(a == HALVES - 1))
                else:
                    return
                last.then_inc(done[name], 1)

            if not later and i == 1:
                pe.wait_ge(mb_set, 2)
                pe.wait_ge(bo_set, 1)
            if not later and i == 3:
                pe.wait_ge(router_set, 1)
            for n in range(SLOTS + 2):
                if attend and n < SLOTS:
                    attend_scores(n)
                if find and n < 8:
                    find_max(2 * n)
                if attend and n >= 2:
                    attend_values(n - 2)
                if find and n < 8:
                    find_max(2 * n + 1)
                for name in JOBS:
                    if JOB_AT[name] == n:
                        job(name)
                if n == LG_AT and norm and (later or i >= 4):
                    if find:
                        pe.wait_ge(a_top[H - 3], i + 1)
                    logits(i - 4)
                if n == X2_AT and norm:
                    pe.wait_ge(n_made, i - 2)
                    reached(pe, xt2_lo, i - 3)
                    if find:
                        pe.wait_ge(a_top[H - 1], i + 1)
                    for a in range(HALVES):
                        last = nc.tensor.transpose(turned2[:, a * S:(a + 1) * S], xn2[:, w, a * P:(a + 1) * P],
                                                   ident[0:S, 0:S])
                    last.then_inc(done["X2"], 1)
            if not later and i == 0:
                output_bias()

        def logits(b):
            pe.wait_ge(xt2_hi, b + 1)
            pe.wait_ge(xt2_lo, b + 1)
            reached(pe, lg_out, b)
            project3(logits_out, lambda a: (xt2[:, a, :], xt2[:, HALVES + a, :]),
                     lambda a: (rw[:, 0, a * E:(a + 1) * E], rw[:, 1, a * E:(a + 1) * E])).then_inc(done["LG"], 1)

        split_steps(pe, step)
        logits(B - 1)


LN3_EPS = 1e-12


def route_block(nc, sems, ctx, t, keep, rows, w2_halves):
    sb = lambda name, shape, dt: ctx.enter_context(nc.sbuf_tensor(name, shape, dt))
    ps = lambda name, shape, dt: ctx.enter_context(nc.psum_tensor(name, shape, dt))
    sem = sems.new
    L, cw, tile_expert, take, put = (keep[k] for k in ("logits", "cw", "tile_expert", "take", "put"))

    fixed = keep["fixed"]
    before32, falling, counting, value, spare, tile_start = (
        fixed[:, sum(WIDTHS[:k]):sum(WIDTHS[:k + 1])] for k in range(len(WIDTHS)))
    before32, falling, counting, value = before32[0:S], falling[0:S], counting[0:S], value[0:S]
    tile_start = tile_start[0:1].rearrange("p (n e) -> p n e", e=E)
    before = sb("before", [S, S], BF16)
    all_ones = sb("all_ones", [S, S], BF16)
    pick = [sb(f"pick{k}", [S, B, E], F32) for k in range(2)]
    key = sb("key", [S, B, E], F32)
    m = [sb(f"m{k}", [S, B, 1], F32) for k in range(2)]
    first = sb("first", [S, B, 1], F32)
    both = sb("both", [S, B, E], BF16)
    count = [sb(f"count{k}", [S, B, E], F32) for k in range(2)]
    size = [sb(f"size{k}", [S, E], F32) for k in range(3)]
    whole = sb("whole", [S, E], I32)
    whole2 = sb("whole2", [S, E], I32)
    past_n = sb("past_n", [1, NT, 1], F32)
    slot = sb("slot", [S, 2, B], F32)
    slot_i = sb("slot_i", [S, 2, B], I32)
    block_i = sb("block_i", [S, 2, B], I32)
    slot_block = sb("slot_block", [S, 2, B], F32)
    slot_row = sb("slot_row", [S, 2, B], F32)
    is_row = sb("is_row", [S, 2, B, P], F16)
    in_block = sb("in_block", [S, 2, B, NB], F16)
    code = sb("code", [P, 4 * NB], F32)
    code_i = sb("code_i", [P, 4 * NB], I32)
    batch_i = sb("batch_i", [P, 4 * NB], I32)
    batch = sb("batch", [P, 4 * NB], F32)
    found = [sb(f"found{k}", [P, NB], F32) for k in range(2)]
    place = sb("place", [P, NB], F32)
    zeros = sb("zeros", [1, D], F32)

    rank, total = ps("rank", [P, 512], F32), ps("total", [P, 512], F32)
    lists = [[ps(f"lists{k}{half}", [P, 512], F32) for half in range(2)] for k in range(2)]

    w2_in, ones_set = sem("w2_in"), sem("ones_set")
    steps, gap, expd, picked, ranked = (sem("r_" + n) for n in ("steps", "gap", "expd", "picked", "ranked"))
    slots_made = sem("slots_made")
    block_marked, row_marked, coded = sem("block_marked"), sem("row_marked"), sem("coded")
    listed, zero_row = sem("listed"), sem("zero_row")

    block = ctx.enter_context(nc.Block())

    @block.sync
    def _(sp):
        for n, name in enumerate(("w2h", "w2l")):
            for q in range(4):
                flat = keep[name][:].rearrange("p e f d -> p (e f d)").rearrange("p (q n) -> p q n", q=4)
                sp.dma_start(flat[:, q, :], w2_halves[n].rearrange("p (q b) n -> q p (b n)", q=4)[q]).then_inc(w2_in, 16)
        sp.wait_ge(ones_set, 2)
        sp.dma_start(rows[0:1, :], zeros[:]).then_inc(zero_row, 16)
        sp.wait_ge(zero_row, 16)
        sp.wait_ge(w2_in, 16 * 8)

    @block.gpsimd
    def _(pool):
        nc.gpsimd.memset(all_ones[:], 1.0).then_inc(ones_set, 1)
        nc.gpsimd.memset(zeros[:], 0.0).then_inc(ones_set, 1)
        for k in range(2):
            pool.wait_ge(block_marked, k + 1)
            nc.gpsimd.tensor_tensor(in_block[:, k], in_block[:, k], value.unsqueeze(2).to_broadcast([S, B, NB]),
                                    ALU.mult).then_inc(coded, 1)

    @block.scalar
    def _(act):
        act.wait_ge(gap, 1)
        nc.scalar.activation(m[1][:], m[1][:], ACT.Exp).then_inc(expd, 1)

    @block.tensor
    def _(pe):
        MM = nc.tensor.matmul
        pe.wait_ge(ones_set, 2)
        pe.wait_ge(picked, 1)
        MM(rank[0:S, 0:B * E], before[:], both[:].rearrange("p b e -> p (b e)"), start=True, stop=True)
        MM(total[0:S, 0:B * E], all_ones[:], both[:].rearrange("p b e -> p (b e)"), start=True,
           stop=True).then_inc(ranked, 1)
        for k in range(2):
            pe.wait_ge(row_marked, k + 1)
            pe.wait_ge(coded, k + 1)
            for b in range(B):
                half, n = divmod(b, B // 2)
                last = MM(lists[k][half][:, 0:NB], is_row[:, k, b, :], in_block[:, k, b, :], start=(n == 0),
                          stop=(n == B // 2 - 1))
            last.then_inc(listed, 1)

    @block.vector
    def _(dve):
        V = nc.vector
        done = [0]

        def tick(instruction):
            done[0] += 1
            instruction.then_inc(steps, 1)
            dve.wait_ge(steps, done[0])

        tick(V.tensor_copy(before[:], before32))
        wide = lambda a: a.to_broadcast([S, B, E])
        for k in range(2):
            tick(V.tensor_reduce(m[k][:], L[:], AX.X, ALU.max))
            tick(V.tensor_tensor(key[:], L[:], wide(m[k][:]), ALU.is_equal))
            tick(V.tensor_tensor(key[:], key[:], falling.unsqueeze(1).to_broadcast([S, B, E]), ALU.mult))
            tick(V.tensor_reduce(first[:], key[:], AX.X, ALU.max))
            tick(V.tensor_tensor(pick[k][:], key[:], wide(first[:]), ALU.is_equal))
            if k == 0:
                tick(V.scalar_tensor_tensor(L[:], pick[0][:], -3.0e38, L[:], ALU.mult, ALU.add))
        V.tensor_tensor(both[:], pick[0][:], pick[1][:], ALU.add).then_inc(picked, 1)
        V.tensor_tensor(m[1][:], m[1][:], m[0][:], ALU.subtract).then_inc(gap, 1)
        dve.wait_ge(ranked, 1)
        tick(V.tensor_copy(count[0][:].rearrange("p b e -> p (b e)"), total[0:S, 0:B * E]))
        at, s = 0, 1
        while s < B:
            V.tensor_copy(count[1 - at][:, 0:s, :], count[at][:, 0:s, :])
            tick(V.tensor_tensor(count[1 - at][:, s:B, :], count[at][:, s:B, :], count[at][:, 0:B - s, :], ALU.add))
            at, s = 1 - at, 2 * s
        tick(V.tensor_scalar(size[0][:], count[at][:, B - 1, :], float(TS - 1), None, ALU.add))
        shift_bits = TS.bit_length() - 1
        tick(V.tensor_copy(whole[:], size[0][:]))
        tick(V.tensor_single_scalar(whole2[:], whole[:], shift_bits, ALU.arith_shift_right))
        tick(V.tensor_copy(size[0][:], whole2[:]))
        tick(V.tensor_scalar(size[0][:], size[0][:], float(TS), None, ALU.mult))
        tick(V.tensor_copy(size[1][:], size[0][:]))
        e_at, s = 1, 1
        while s < E:
            V.tensor_copy(size[3 - e_at][:, 0:s], size[e_at][:, 0:s])
            tick(V.tensor_tensor(size[3 - e_at][:, s:E], size[e_at][:, s:E], size[e_at][:, 0:E - s], ALU.add))
            e_at, s = 3 - e_at, 2 * s
        ends, start = size[e_at], size[0]
        tick(V.tensor_tensor(start[:], ends[:], start[:], ALU.subtract))
        pos = count[at]
        flat = lambda a: a[:].rearrange("p b e -> p (b e)")
        tick(V.tensor_tensor(flat(pos), flat(pos), total[0:S, 0:B * E], ALU.subtract))
        tick(V.tensor_tensor(flat(pos), flat(pos), rank[0:S, 0:B * E], ALU.add))
        tick(V.tensor_tensor(pos[:], pos[:], start[:].unsqueeze(1).to_broadcast([S, B, E]), ALU.add))
        for k in range(2):
            tick(V.tensor_tensor(key[:], pick[k][:], pos[:], ALU.mult))
            tick(V.tensor_reduce(slot[:, k, :].unsqueeze(2), key[:], AX.X, ALU.add))
        tick(V.tensor_copy(slot_i[:], slot[:]))
        tick(V.tensor_single_scalar(block_i[:], slot_i[:], P.bit_length() - 1, ALU.arith_shift_right))
        tick(V.tensor_copy(slot_block[:], block_i[:]))
        V.scalar_tensor_tensor(slot_row[:], slot_block[:], -float(P), slot[:], ALU.mult, ALU.add).then_inc(slots_made, 1)
        dve.wait_ge(slots_made, 1)
        wide_to = lambda a, n: a.unsqueeze(2).to_broadcast([S, B, n])
        for k in range(2):
            V.tensor_tensor(in_block[:, k], counting[:, 0:NB].unsqueeze(1).to_broadcast([S, B, NB]),
                            wide_to(slot_block[:, k, :], NB), ALU.is_equal).then_inc(block_marked, 1)
        for k in range(2):
            V.tensor_tensor(is_row[:, k], counting.unsqueeze(1).to_broadcast([S, B, P]),
                            wide_to(slot_row[:, k, :], P), ALU.is_equal).then_inc(row_marked, 1)
        tick(V.tensor_tensor(tile_start, tile_start, ends[0:1, :].unsqueeze(1).to_broadcast([1, NT, E]), ALU.is_ge))
        tick(V.tensor_reduce(past_n[:], tile_start, AX.X, ALU.add))
        tick(V.tensor_scalar(past_n[:], past_n[:], float(E - 1), None, ALU.min))
        tick(V.tensor_copy(tile_expert[:], past_n[:].rearrange("p n o -> p (n o)")))
        dve.wait_ge(expd, 1)
        w = [cw[:, k, :].unsqueeze(2) for k in range(2)]
        tick(V.tensor_scalar(w[0], m[1][:], 1.0, None, ALU.add))
        tick(V.reciprocal(w[0], w[0]))
        tick(V.tensor_tensor(w[1], m[1][:], w[0], ALU.mult))
        dve.wait_ge(listed, 2)
        for k in range(2):
            for half in range(2):
                q = 2 * k + half
                last = V.tensor_copy(code[:, q * NB:(q + 1) * NB], lists[k][half][:, 0:NB])
        tick(last)
        tick(V.tensor_copy(code_i[:], code[:]))
        tick(V.tensor_single_scalar(batch_i[:], code_i[:], P.bit_length() - 1, ALU.arith_shift_right))
        tick(V.tensor_copy(batch[:], batch_i[:]))
        tick(V.scalar_tensor_tensor(batch[:], batch[:], -float(P - S), code[:], ALU.mult, ALU.add))
        tick(V.tensor_scalar(code[:], code[:], 0.0, float(B // 2 * S), ALU.is_gt, ALU.mult))
        for k in range(2):
            first_half, second_half = (batch[:, (2 * k + h) * NB:(2 * k + h + 1) * NB] for h in range(2))
            tick(V.tensor_tensor(found[k][:], first_half, second_half, ALU.add))
            tick(V.tensor_tensor(found[k][:], found[k][:], code[:, (2 * k + 1) * NB:(2 * k + 2) * NB], ALU.add))
        tick(V.tensor_scalar(place[:], found[1][:], 0.0, float(B * S), ALU.is_gt, ALU.mult))
        tick(V.tensor_tensor(found[0][:], found[0][:], found[1][:], ALU.add))
        tick(V.tensor_copy(take[:], found[0][:]))
        tick(V.tensor_single_scalar(found[1][:], found[0][:], 0.0, ALU.is_equal))
        tick(V.tensor_tensor(found[1][:], found[1][:], spare, ALU.mult))
        tick(V.tensor_tensor(place[:], place[:], found[1][:], ALU.add))
        tick(V.tensor_tensor(place[:], place[:], found[0][:], ALU.add))
        tick(V.tensor_copy(put[:], place[:]))


def expert_steps(eng, step):
    def edge(i):
        step(i, i % 2, 0 <= i < NT, 1 <= i, i + 1 < NT, i + 2 < NT)
    for i in (-1, 0, 1, 2):
        edge(i)
    pairs = (NT - 5) // 2
    with eng.Fori(0, pairs) as j:
        for u in range(2):
            step(j * 2 + (3 + u), 1 - u, True, True, True, True)
    for i in range(3 + 2 * pairs, NT + 1):
        edge(i)


def expert_block(nc, sems, ctx, t, keep, rows, y):
    sb = lambda name, shape, dt: ctx.enter_context(nc.sbuf_tensor(name, shape, dt))
    ps = lambda name, shape, dt: ctx.enter_context(nc.psum_tensor(name, shape, dt))
    sem = sems.new
    w1h, w1l, w2h, w2l = (keep[n] for n in ("w1h", "w1l", "w2h", "w2l"))
    tile_expert, take, put, X = (keep[n] for n in ("tile_expert", "take", "put", "X"))
    SUB = TS // P

    ident = sb("ident3f", [P, P], F32)
    b1 = sb("b1", [P, E, FC], F32)
    b2 = sb("b2", [P, E, D], F32)
    ln_b = sb("ln_b", [S, D], F32)
    xr = sb("xr", [P, 2, SUB, D], F32)
    xt = sb("xt", [P, 2, 2 * HALVES, TS], F16)
    g = sb("g", [P, 2, 2 * TS], F32)
    warm = sb("warm", [P, 1], F32)
    hh = sb("hh", [P, 2, FC, TS], F16)
    hl = sb("hl", [P, 2, FC, TS], F16)
    ys = sb("ys", [P, 2, SUB, D], F32)
    take_now = sb("take_now", [P, 2, SUB], U32)
    put_now = sb("put_now", [P, 2, SUB], U32)

    tb = ps("tb", [P, HALVES * TS], F32)
    hb = [ps(f"hb{k}", [P, 512], F32) for k in range(2)]
    yb = [[ps(f"yb{u}{s}", [P, 512], F32) for s in range(SUB)] for u in range(2)]

    ident_in, loaded, biased = sem("e_ident_in"), sem("e_loaded"), sem("e_biased")
    rows_in = [sem(f"rows_in{u}") for u in range(2)]
    turned, x_hi, x_lo = sem("e_turned"), sem("x_hi"), sem("x_lo")
    FP = FC // 2
    h_done = [sem(f"h_done{k}") for k in range(FP)]
    h_gelu = [sem(f"h_gelu{k}") for k in range(FP)]
    h_hi = [sem(f"h_hi{k}") for k in range(FP)]
    h_lo = [sem(f"h_lo{k}") for k in range(FP)]
    y_done, y_out = sem("y_done"), sem("y_out")
    y_stored = [sem(f"y_stored{u}") for u in range(2)]
    take_first, take_set, put_set = sem("take_first"), sem("take_set"), sem("put_set")

    block = ctx.enter_context(nc.Block())

    def by_parity(b, u):
        return (b - u) * 8 * SUB + 16 * SUB

    def blocks(index, i):
        return index[:, i * SUB:(i + 1) * SUB] if isinstance(i, int) else index[:, bass.ds(i * SUB, SUB)]

    @block.sync
    def _(sp):
        sp.dma_start(ident[:], t["ident"]).then_inc(ident_in, 16)
        sp.dma_start(ln_b[:], t["ln_b"].to_broadcast([S, D])).then_inc(loaded, 16)
        sp.dma_start(b1[:], t["b1"]).then_inc(loaded, 16)
        sp.dma_start(b2[:].rearrange("p e d -> p (e d)"), t["b2"].to_broadcast([P, E * D])).then_inc(loaded, 16)

    @block.gpsimd
    def _(pool):
        def gather(i, u):
            if isinstance(i, int) and i < 2:
                nc.gpsimd.tensor_copy(take_now[:, u, :], blocks(take, i)).then_inc(take_first, 1)
                pool.wait_ge(take_first, i + 1)
            else:
                pool.wait_ge(turned, i - 1)
                nc.gpsimd.tensor_copy(take_now[:, u, :], blocks(take, i)).then_inc(take_set, 1)
                pool.wait_ge(loaded, 48)
                pool.wait_ge(take_set, i - 1)
            for s in range(SUB):
                nc.gpsimd.indirect_dma_start(xr[:, u, s, :], None, rows,
                                             bass.IndirectOffsetOnAxis(ap=take_now[:, u, s:s + 1], axis=0)).then_inc(rows_in[u], 16)

        def scatter(i, u):
            if not isinstance(i, int) or i >= 2:
                pool.wait_ge(y_stored[u], by_parity(i - 2, u))
            pool.wait_ge(y_out, i + 1)
            nc.gpsimd.tensor_copy(put_now[:, u, :], blocks(put, i)).then_inc(put_set, 1)
            pool.wait_ge(loaded, 48)
            pool.wait_ge(put_set, i + 1)
            for s in range(SUB):
                nc.gpsimd.indirect_dma_start(y, bass.IndirectOffsetOnAxis(ap=put_now[:, u, s:s + 1], axis=0),
                                             ys[:, u, s, :], None).then_inc(y_stored[u], 16)

        gather(0, 0)
        gather(1, 1)
        pool.wait_ge(loaded, 48)

        def step(i, u, first, second, turn, load):
            if load and (not isinstance(i, int) or i >= 0):
                gather(i + 2, u)
            if second:
                scatter(i - 1, 1 - u)
            if not isinstance(i, int) or 3 <= i < B + 3:
                nc.gpsimd.tensor_tensor(X[:, i - 3, :], X[:, i - 3, :], ln_b[:], ALU.add).then_inc(biased, 1)

        expert_steps(pool, step)
        pool.wait_ge(biased, B)
        for u in range(2):
            pool.wait_ge(y_stored[u], 16 * SUB * ((NT + 1 - u) // 2))

    @block.tensor
    def _(pe):
        MM = nc.tensor.matmul
        pe.wait_ge(ident_in, 16)

        def transpose(i, w):
            pe.wait_ge(rows_in[w], by_parity(i + 1, w))
            reached(pe, x_lo, i + 1)
            for a in range(HALVES):
                for s in range(SUB):
                    last = nc.tensor.transpose(tb[:, a * TS + s * P:a * TS + (s + 1) * P],
                                               xr[:, w, s, a * P:(a + 1) * P], ident[:])
            last.then_inc(turned, 1)

        def step(i, u, first, second, turn, load):
            w = 1 - u
            if first:
                e1 = pe.value_load(tile_expert[0:1, bass.ds(i, 1)], min_val=0, max_val=E - 1)
            if second:
                e2 = pe.value_load(tile_expert[0:1, bass.ds(i - 1, 1)], min_val=0, max_val=E - 1)
            at_once = not isinstance(i, int) or i != 0
            if turn and at_once:
                transpose(i, w)
            if first:
                pe.wait_ge(x_hi, i + 1)
                pe.wait_ge(x_lo, i + 1)
            for f in range(FC):
                if f == 2 and turn and first and not at_once:
                    transpose(i, w)
                if first:
                    n = f // 2
                    bank = hb[n % 2]
                    if f % 2 == 0:
                        if n >= 2:
                            pe.wait_ge(h_gelu[n - 2], i + 1)
                        else:
                            reached(pe, h_gelu[n + FP - 2], i)
                    out = bank[:, (f % 2) * TS:(f % 2 + 1) * TS]
                    cols = slice(f * P, (f + 1) * P)
                    for a in range(HALVES):
                        MM(out, w1h[:, e1, a, cols], xt[:, u, a, :], start=(a == 0), stop=False)
                        MM(out, w1h[:, e1, a, cols], xt[:, u, HALVES + a, :], start=False, stop=False)
                        last = MM(out, w1l[:, e1, a, cols], xt[:, u, a, :], start=False, stop=(a == HALVES - 1))
                    if f % 2 == 1:
                        last.then_inc(h_done[n], 1)
                if second:
                    if f % 2 == 0:
                        pe.wait_ge(h_lo[f // 2], i)
                    if f == 0:
                        reached(pe, y_out, i - 2)
                    for s in range(SUB):
                        out = yb[w][s][:, 0:D]
                        tok = slice(s * P, (s + 1) * P)
                        MM(out, hh[:, w, f, tok], w2h[:, e2, f, :], start=(f == 0), stop=False)
                        MM(out, hh[:, w, f, tok], w2l[:, e2, f, :], start=False, stop=False)
                        last = MM(out, hl[:, w, f, tok], w2h[:, e2, f, :], start=False, stop=(f == FC - 1))
            if second:
                last.then_inc(y_done, 1)

        expert_steps(pe, step)

    @block.scalar
    def _(act):
        act.wait_ge(loaded, 48)
        nc.scalar.activation(warm[:], b1[:, 0, 0:1], ACT.Gelu)

        def step(i, u, first, second, turn, load):
            if first:
                e1 = act.value_load(tile_expert[0:1, bass.ds(i, 1)], min_val=0, max_val=E - 1)
                for n in range(FP):
                    act.wait_ge(h_done[n], i + 1)
                    if n >= 2:
                        act.wait_ge(h_lo[n - 2], i + 1)
                    else:
                        reached(act, h_lo[n + FP - 2], i)
                    for k in range(2):
                        last = nc.scalar.activation(g[:, n % 2, k * TS:(k + 1) * TS], hb[n % 2][:, k * TS:(k + 1) * TS],
                                                    ACT.Gelu, bias=b1[:, e1, 2 * n + k:2 * n + k + 1], scale=1.0 / WE)
                    last.then_inc(h_gelu[n], 1)

        expert_steps(act, step)

    @block.vector
    def _(dve):
        V = nc.vector
        def step(i, u, first, second, turn, load):
            w = 1 - u
            if turn:
                dve.wait_ge(turned, i + 2)
                if not isinstance(i, int) or i >= 1:
                    dve.wait_ge(h_done[FP - 1], i)
                high, low = (xt[:, w, k * HALVES:(k + 1) * HALVES].rearrange("p q n -> p (q n)") for k in range(2))
                V.tensor_copy(high, tb[:]).then_inc(x_hi, 1)
                dve.wait_ge(x_hi, i + 2)
                V.tensor_tensor(low, tb[:], high, ALU.subtract).then_inc(x_lo, 1)
            if first:
                for n in range(FP):
                    dve.wait_ge(h_gelu[n], i + 1)
                    if n == 0 and (not isinstance(i, int) or i >= 2):
                        dve.wait_ge(y_done, i - 1)
                    high = hh[:, u, 2 * n:2 * n + 2, :].rearrange("p f t -> p (f t)")
                    V.tensor_copy(high, g[:, n % 2, :]).then_inc(h_hi[n], 1)
                    dve.wait_ge(h_hi[n], i + 1)
                    V.tensor_tensor(hl[:, u, 2 * n:2 * n + 2, :].rearrange("p f t -> p (f t)"), g[:, n % 2, :],
                                    high, ALU.subtract).then_inc(h_lo[n], 1)
            if second:
                e2 = dve.value_load(tile_expert[0:1, bass.ds(i - 1, 1)], min_val=0, max_val=E - 1)
                dve.wait_ge(y_done, i)
                if isinstance(i, int) and i == 1:
                    dve.wait_ge(loaded, 48)
                if not isinstance(i, int) or i >= 3:
                    dve.wait_ge(y_stored[w], by_parity(i - 3, w))
                for s in range(SUB):
                    last = V.scalar_tensor_tensor(ys[:, w, s, :], yb[w][s][:, 0:D], 1.0 / WE, b2[:, e2, :],
                                                  ALU.mult, ALU.add)
                last.then_inc(y_out, 1)

        expert_steps(dve, step)


def combine_block(nc, sems, ctx, t, keep, rows, y, out):
    sb = lambda name, shape, dt: ctx.enter_context(nc.sbuf_tensor(name, shape, dt))
    sem = sems.new
    X, cw = keep["X"], keep["cw"]
    LB = 4
    EDGES = (0, 4, 9, 15, 21, 28, 32)
    NG = len(EDGES) - 1
    BY_POOL = EDGES[2]
    NZ = 8

    y0 = sb("y0", [S, B, D], F32)
    y1 = sb("y1", [S, B, D], F32)
    xn2 = sb("xn2c", [S, B, D], F32)
    stats = sb("stats3", [S, B, 6], F32)
    mv = sb("mv3", [S, B, 2], F32)
    ve = sb("ve3", [S, B], F32)
    minus_half = sb("minus_half3", [S, B], F32)
    rstd = sb("rstd3", [S, B], F32)
    tmp = sb("tmp3", [S, B], F32)
    shift = sb("shift3", [S, B], F32)
    ln_w = sb("ln_w", [S, D], F32)
    ident = sb("ident_c", [S, S], F32)
    banks = [ctx.enter_context(nc.psum_tensor(f"zb{k}", [S, 512], F32)) for k in range(NZ)]
    on_pool = range(1, 8, 2)
    base = [xn2[:, n, :] if n in on_pool else banks[n % NZ][:, 0:D] for n in range(B)]
    pool_sums = lambda n: sum(b in on_pool for b in range(n + 1))

    ident_in, final_pool, based_pool = sem("c_ident_in"), sem("c_final_pool"), sem("c_based_pool")
    loaded, half_set, aggregated, squared, centred = (sem(n) for n in (
        "c_loaded", "half_set", "aggregated", "squared", "centred"))
    y0_in, y1_in, xn_in = ([sem(f"{n}{g}") for g in range(B // LB)] for n in ("y0_in", "y1_in", "xn_in"))
    weighted, based, summed, stated, varied, rooted, refined, normed, scaled, final, stored = (sem("c_" + n) for n in (
        "weighted", "based", "summed", "stated", "varied", "rooted", "refined", "normed", "scaled", "final", "stored"))

    block = ctx.enter_context(nc.Block())
    y_read = [y[1 + k * B * S:1 + (k + 1) * B * S, :].rearrange("(g b s) d -> g s b d", b=LB, s=S) for k in range(2)]
    row_loads = rows[1:1 + B * S, :].rearrange("(g b s) d -> g s b d", b=LB, s=S)
    loads = lambda a: a.rearrange("(g b) s d -> g s b d", b=LB)
    group = lambda g: range(EDGES[g], EDGES[g + 1])
    cols = lambda g: slice(EDGES[g], EDGES[g + 1])
    LAST = NG - 1

    @block.sync
    def _(sp):
        sp.dma_start(ident[:], t["ident"][0:S, 0:S]).then_inc(ident_in, 16)
        for g in range(B // LB):
            here = slice(g * LB, (g + 1) * LB)
            sp.dma_start(y1[:, here, :], y_read[1][g]).then_inc(y1_in[g], 16)
            sp.dma_start(xn2[:, here, :], row_loads[g]).then_inc(xn_in[g], 16)
            sp.dma_start(y0[:, here, :], y_read[0][g]).then_inc(y0_in[g], 16)
            if g == 0:
                sp.dma_start(ln_w[:], t["ln_w"].to_broadcast([S, D])).then_inc(loaded, 16)
        for g in range(B // LB):
            if g * LB < BY_POOL:
                sp.wait_ge(final_pool, min((g + 1) * LB, BY_POOL))
            if (g + 1) * LB > BY_POOL:
                sp.wait_ge(final, (g + 1) * LB - BY_POOL)
            sp.dma_start(loads(out)[g], y0[:, g * LB:(g + 1) * LB, :]).then_inc(stored, 16)
        sp.wait_ge(stored, 16 * (B // LB))

    @block.scalar
    def _(act):
        def weight(g):
            for n in group(g):
                if n % LB == 0:
                    act.wait_ge(y1_in[n // LB], 16)
                nc.scalar.activation(y1[:, n, :], y1[:, n, :], ACT.Copy, scale=cw[:, 1, n:n + 1]).then_inc(weighted, 1)

        def normalise(g):
            act.wait_ge(refined, 4 * (g + 1))
            for n in group(g):
                nc.scalar.activation(y0[:, n, :], y0[:, n, :], ACT.Identity, scale=rstd[:, n:n + 1],
                                     bias=shift[:, n:n + 1]).then_inc(normed, 1)

        weight(0)
        weight(1)
        for g in range(2, NG):
            weight(g)
            normalise(g - 2)
        normalise(LAST - 1)

    @block.tensor
    def _(pe):
        MM = nc.tensor.matmul
        pe.wait_ge(ident_in, 16)
        for n in range(B):
            if n % LB == 0:
                pe.wait_ge(xn_in[n // LB], 16)
            if n in on_pool:
                continue
            if n >= NZ:
                pe.wait_ge(summed, n - NZ + 1)
            MM(base[n], ident[:], xn2[:, n, :], start=True, stop=False)
            pe.wait_ge(weighted, n + 1)
            MM(base[n], ident[:], y1[:, n, :], start=False, stop=True).then_inc(based, 1)

    @block.gpsimd
    def _(pool):
        def root(g):
            pool.wait_ge(varied, g + 1)
            nc.gpsimd.tensor_tensor(rstd[:, cols(g)], ve[:, cols(g)], minus_half[:, cols(g)], ALU.pow).then_inc(rooted, 1)

        def scale(g):
            for n in group(g):
                pool.wait_ge(normed, n + 1)
                nc.gpsimd.tensor_tensor(y0[:, n, :], y0[:, n, :], ln_w[:], ALU.mult).then_inc(scaled, 1)

        def finish(g):
            for n in group(g):
                pool.wait_ge(scaled, n + 1)
                nc.gpsimd.tensor_tensor(y0[:, n, :], y0[:, n, :], X[:, n, :], ALU.add).then_inc(final_pool, 1)

        nc.gpsimd.memset(minus_half[:], -0.5).then_inc(half_set, 1)
        for n in on_pool:
            pool.wait_ge(xn_in[n // LB], 16)
            pool.wait_ge(weighted, n + 1)
            nc.gpsimd.tensor_tensor(xn2[:, n, :], xn2[:, n, :], y1[:, n, :], ALU.add).then_inc(based_pool, 1)
        pool.wait_ge(half_set, 1)
        root(0)
        pool.wait_ge(loaded, 16)
        for g in range(2, NG):
            root(g - 1)
            scale(g - 2)
            if EDGES[g - 1] <= BY_POOL:
                finish(g - 2)
        root(LAST)
        scale(LAST - 1)

    @block.vector
    def _(dve):
        V = nc.vector

        def sum_and_stats(g):
            for n in group(g):
                if n % LB == 0:
                    dve.wait_ge(y0_in[n // LB], 16)
                if n in on_pool:
                    dve.wait_ge(based_pool, pool_sums(n))
                else:
                    dve.wait_ge(based, n + 1 - pool_sums(n))
                V.scalar_tensor_tensor(y0[:, n, :], y0[:, n, :], cw[:, 0, n:n + 1], base[n], ALU.mult,
                                       ALU.add).then_inc(summed, 1)
                if n > EDGES[g]:
                    stats_of(n - 1)
            stats_of(n)
            for n in group(g):
                dve.wait_ge(stated, n + 1)
                last = V.bn_aggr(mv[:, n, :], stats[:, n, :])
            last.then_inc(aggregated, 1)
            dve.wait_ge(aggregated, g + 1)
            V.tensor_scalar(ve[:, cols(g)], mv[:, cols(g), 1], LN3_EPS, None, ALU.add).then_inc(varied, 1)

        def stats_of(n):
            dve.wait_ge(summed, n + 1)
            V.bn_stats(stats[:, n, :], y0[:, n, :]).then_inc(stated, 1)

        def refine(g):
            c = cols(g)
            dve.wait_ge(rooted, g + 1)
            V.tensor_tensor(tmp[:, c], rstd[:, c], rstd[:, c], ALU.mult).then_inc(squared, 1)
            dve.wait_ge(squared, g + 1)
            V.tensor_tensor(tmp[:, c], tmp[:, c], ve[:, c], ALU.mult).then_inc(refined, 1)
            dve.wait_ge(refined, 4 * g + 1)
            V.tensor_scalar(tmp[:, c], tmp[:, c], -0.5, 1.5, ALU.mult, ALU.add).then_inc(refined, 1)
            dve.wait_ge(refined, 4 * g + 2)
            V.tensor_tensor(rstd[:, c], rstd[:, c], tmp[:, c], ALU.mult).then_inc(refined, 1)
            dve.wait_ge(refined, 4 * g + 3)
            V.scalar_tensor_tensor(shift[:, c], mv[:, c, 0], -1.0, rstd[:, c], ALU.mult, ALU.mult).then_inc(refined, 1)

        def finish(g):
            for n in group(g):
                dve.wait_ge(scaled, n + 1)
                V.tensor_tensor(y0[:, n, :], y0[:, n, :], X[:, n, :], ALU.add).then_inc(final, 1)

        sum_and_stats(0)
        sum_and_stats(1)
        refine(0)
        for g in range(2, NG):
            sum_and_stats(g)
            refine(g - 1)
            if EDGES[g - 1] > BY_POOL:
                finish(g - 2)
        refine(LAST)
        dve.wait_ge(refined, 4 * NG)
        dve.wait_ge(loaded, 16)
        for n in group(LAST):
            V.scalar_tensor_tensor(y0[:, n, :], y0[:, n, :], mv[:, n, 0:1], ln_w[:], ALU.subtract,
                                   ALU.mult).then_inc(centred, 1)
        finish(LAST - 1)
        for n in group(LAST):
            dve.wait_ge(centred, n + 1 - EDGES[LAST])
            V.scalar_tensor_tensor(y0[:, n, :], y0[:, n, :], rstd[:, n:n + 1], X[:, n, :], ALU.mult,
                                   ALU.add).then_inc(final, 1)


class Semaphores:
    def __init__(self, nc):
        self.nc, self.stack, self.made = nc, ExitStack(), []

    def new(self, name):
        self.made.append(self.stack.enter_context(self.nc.semaphore(name)))
        return self.made[-1]

    def __enter__(self):
        return self

    def __exit__(self, *error):
        if error[0] is not None:
            return
        with self.nc.Block() as block:
            @block.gpsimd
            def _(pool):
                numbers = sorted(s.num for s in self.made)
                starts = [n for n in numbers if n - 1 not in numbers]
                ends = [n for n in numbers if n + 1 not in numbers]
                for first, last in zip(starts, ends):
                    pool.sem_clear(range(first, last + 1))
        self.stack.close()


def program(nc, t, out):
    rows = nc.dram_tensor("rows", (1 + B * S, D), F32, kind="Internal").ap()
    y = nc.dram_tensor("y", (1 + 2 * B * S + NT * TS, D), F32, kind="Internal").ap()
    w2_halves = nc.dram_tensor("w2_halves", (2, P, B, PIECE), F16, kind="Internal").ap()
    with ExitStack() as hold:
        sb = lambda name, shape, dt, stack=hold: stack.enter_context(nc.sbuf_tensor(name, shape, dt))
        keep = {"cw": sb("cw", [S, 2, B], F32), "tile_expert": sb("tile_expert", [1, NT], I32),
                "take": sb("take", [P, NB], U32), "put": sb("put", [P, NB], U32),
                "logits": sb("logits", [S, B, E], F32), "fixed": sb("fixed", [P, sum(WIDTHS)], F32),
                "X": sb("X", [S, B, D], F32)}
        with ExitStack() as weights:
            for name in ("w1h", "w1l"):
                keep[name] = sb(name, [P, E, HALVES, F], F16, weights)
            with Semaphores(nc) as sems, ExitStack() as ctx:
                attention_block(nc, sems, ctx, t, keep, rows, w2_halves)
            for name in ("w2h", "w2l"):
                keep[name] = sb(name, [P, E, FC, D], F16, weights)
            with Semaphores(nc) as sems, ExitStack() as ctx:
                route_block(nc, sems, ctx, t, keep, rows, w2_halves)
            with Semaphores(nc) as sems, ExitStack() as ctx:
                expert_block(nc, sems, ctx, t, keep, rows, y)
        with Semaphores(nc) as sems, ExitStack() as ctx:
            combine_block(nc, sems, ctx, t, keep, rows, y, out)




def kernel(**inputs):
    import numpy as np
    import concourse.bacc as bacc
    from concourse.bass_utils import run_bass_kernel_spmd

    g = {k: np.asarray(v) for k, v in inputs.items()}
    halves = lambda w: w.T.reshape(HALVES, P, -1).transpose(1, 0, 2)
    column = lambda b: b.reshape(HALVES, P).T
    pieces = lambda w, blocks, n: w.transpose(0, 2, 1).reshape(E, blocks, P, n).transpose(2, 0, 1, 3).reshape(
        P, B, PIECE).transpose(1, 0, 2)
    mask = g["mask_1x1xSxS2_ik0"][0, 0]
    arrays = {
        "x": g["x"],
        "ctxT": g["ctx_1024"].transpose(0, 2, 1).reshape(B, HALVES, P, T).transpose(0, 2, 1, 3).reshape(B, P, HALVES * T),
        "wqkv": np.stack([halves(g["L0_xattn_W" + n]) for n in "qkv"], 1),
        "wo": halves(g["L0_xattn_Wo"]),
        "bqk": np.stack([column(g["L0_xattn_b" + n]) for n in "qk"], 1),
        "bv": column(g["L0_xattn_bv"]),
        "bo": g["L0_xattn_bo"].reshape(1, D),
        "mask_q": mask,
        "router_w": halves(g["L0_ffn_router_w"]).reshape(P, HALVES * E),
        "router_b": g["L0_ffn_router_b"].reshape(1, E),
        "w12": np.stack([pieces(g["L0_ffn_w1"], HALVES, F), pieces(g["L0_ffn_w2"], FC, D)], 2),
        "b1": g["L0_ffn_b1"].reshape(E, FC, P).transpose(2, 0, 1),
        "b2": g["L0_ffn_b2"].reshape(1, E * D),
        "ln_w": g["L0_ffn_ln_w"].reshape(1, D),
        "ln_b": g["L0_ffn_ln_b"].reshape(1, D),
        "mask_k": mask.T.reshape(CH, KC, S).transpose(1, 0, 2),
    }
    arrays.update(constants(np))
    arrays = {k: np.ascontiguousarray(v) for k, v in arrays.items()}
    nc = bacc.Bacc("TRN2", target_bir_lowering=False, num_devices=1)
    t = {k: nc.dram_tensor("in_" + k, a.shape, mybir.dt.from_np(a.dtype), kind="ExternalInput").ap()
         for k, a in arrays.items()}
    out = nc.dram_tensor("out_0", (B, S, D), F32, kind="ExternalOutput").ap()
    program(nc, t, out)
    r = run_bass_kernel_spmd(nc, [{"in_" + k: a for k, a in arrays.items()}], core_ids=[0])
    return r.results[0]["out_0"]


def constants(np):
    f = np.float32
    rows = np.arange(P)
    sel = np.concatenate([np.eye(KC, P), np.ones((1, P))]).astype(f)
    parts = (np.triu(np.ones((P, S)), 1), np.tile(np.arange(E, 0, -1), (P, 1)), np.tile(np.arange(P), (P, 1)),
             P * (np.arange(B) % (B // 2)) + rows[:, None] + 1,
             (1 + 2 * B * S + np.arange(NT * TS)).reshape(NB, P).T,
             np.tile(np.repeat(np.arange(NT) * TS, E), (P, 1)))
    fixed = np.concatenate(parts, 1).astype(f)
    return {
        "ident": np.eye(P, dtype=f),
        "sel": sel,
        "fixed": fixed,
        "parity": np.stack([rows // DH % 2 == 0, rows // DH % 2 == 1], 1).astype(f),
    }
```
